# Optimizing a Trainium2 kernel written in Bass

```python
import numpy as np
import jax
import jax.numpy as jnp

def _softmax(x, axis=-1):
    return jax.nn.softmax(x, axis=axis)

def _gelu(x):
    return jax.nn.gelu(x, approximate=True)

def _silu(x):
    return jax.nn.silu(x)

def _sigmoid(x):
    return jax.nn.sigmoid(x)

def _layernorm(x, axis=-1, eps=1e-05):
    m = jnp.mean(x, axis=axis, keepdims=True)
    v = jnp.var(x, axis=axis, keepdims=True)
    return (x - m) / jnp.sqrt(v + eps)

def _scatter_add(tgt, idx, src, axis=0):
    return tgt.at[idx].add(src)

def _segment_sum(src, seg, n):
    return jax.ops.segment_sum(src, seg, n)
kernel_name = 'mk_xattn_seq_d1_seqx_r4_0c7efa'

def setup_inputs(seed: int=0):
    np.random.seed(seed)
    _w = jnp.asarray

    def _rec_inputs():
        import jax
        import jax.numpy as jnp
        _rk = jax.random.key(seed)
        x = -0.0001233 + 1 * jax.random.normal(jax.random.fold_in(_rk, 1), (32, 100, 320), jnp.float32)
        _lenS = 100 - jax.random.randint(jax.random.fold_in(_rk, 7), (32,), 0, max(1, 100 // 4) + 1, jnp.int32)
        _lenS2 = 361 - jax.random.randint(jax.random.fold_in(_rk, 8), (32,), 0, max(1, 361 // 4) + 1, jnp.int32)
        _ctx_768P = jax.random.normal(jax.random.fold_in(_rk, 11), (32, 16, 192), jnp.float32)
        _ctx_768c = jax.random.dirichlet(jax.random.fold_in(_rk, 511), 0.3 * jnp.ones((16,), jnp.float32), (32, 361))
        _ctx_768t = jnp.einsum('bsk,bkd->bsd', _ctx_768c, _ctx_768P)
        _ctx_768t = _ctx_768t * jax.lax.rsqrt(jnp.mean(jnp.square(_ctx_768t)) + 1e-12) * 0.953939
        ctx_768 = 0.00272024 + 0.999456 * (_ctx_768t + 0.3 * jax.random.normal(jax.random.fold_in(_rk, 611), (32, 361, 192), jnp.float32))
        return (x, ctx_768)
    x, ctx_768 = _rec_inputs()

    def _L0_xattn_setup():
        import jax, jax.numpy as jnp
        import numpy as np
        D = 320
        H = 20
        DH = D // H
        CTX = 192
        FF_IN = 4 * D
        EPS = 1e-05

        def _ln(x, g, b):
            m = jnp.mean(x, axis=-1, keepdims=True)
            v = jnp.mean(jnp.square(x - m), axis=-1, keepdims=True)
            return (x - m) * jax.lax.rsqrt(v + EPS) * g + b

        def _attn(x, ctx, wq, wk, wv, wo, bo, heads):
            b, n, _ = x.shape
            j = ctx.shape[1]
            dh = wq.shape[1] // heads
            scale = dh ** (-0.5)
            q = (x @ wq).reshape(b, n, heads, dh).transpose(0, 2, 1, 3)
            k = (ctx @ wk).reshape(b, j, heads, dh).transpose(0, 2, 1, 3)
            v = (ctx @ wv).reshape(b, j, heads, dh).transpose(0, 2, 1, 3)
            sim = jnp.einsum('bhid,bhjd->bhij', q, k) * scale
            a = jax.nn.softmax(sim, axis=-1)
            out = jnp.einsum('bhij,bhjd->bhid', a, v)
            out = out.transpose(0, 2, 1, 3).reshape(b, n, heads * dh)
            return out @ wo + bo
        key = jax.random.key(seed)
        ks = jax.random.split(key, 24)
        r = lambda k, shp, s: jax.random.normal(k, shp, dtype=jnp.float32) * s
        d = {'x': r(ks[0], (8, 256, D), 1.0), 'context': r(ks[1], (8, 77, CTX), 1.0), 'heads': H, 'n1_g': jnp.ones((D,), jnp.float32), 'n1_b': jnp.zeros((D,), jnp.float32), 'q1': r(ks[2], (D, D), D ** (-0.5)), 'k1': r(ks[3], (D, D), D ** (-0.5)), 'v1': r(ks[4], (D, D), D ** (-0.5)), 'o1_w': r(ks[5], (D, D), D ** (-0.5)), 'o1_b': jnp.zeros((D,), jnp.float32), 'n2_g': jnp.ones((D,), jnp.float32), 'n2_b': jnp.zeros((D,), jnp.float32), 'q2': r(ks[6], (D, D), D ** (-0.5)), 'k2': r(ks[7], (CTX, D), CTX ** (-0.5)), 'v2': r(ks[8], (CTX, D), CTX ** (-0.5)), 'o2_w': r(ks[9], (D, D), D ** (-0.5)), 'o2_b': jnp.zeros((D,), jnp.float32), 'n3_g': jnp.ones((D,), jnp.float32), 'n3_b': jnp.zeros((D,), jnp.float32), 'ff_w1': r(ks[10], (D, 2 * FF_IN), D ** (-0.5)), 'ff_b1': jnp.zeros((2 * FF_IN,), jnp.float32), 'ff_w2': r(ks[11], (FF_IN, D), FF_IN ** (-0.5)), 'ff_b2': jnp.zeros((D,), jnp.float32)}
        return d
    _L0_xattn_all = _L0_xattn_setup()
    _L0_xattn_in = {k: v for k, v in _L0_xattn_all.items() if k in ('n1_g', 'n1_b', 'q1', 'k1', 'v1', 'o1_w', 'o1_b', 'n2_g', 'n2_b', 'q2', 'k2', 'v2', 'o2_w', 'o2_b', 'n3_g', 'n3_b', 'ff_w1', 'ff_b1', 'ff_w2', 'ff_b2')}
    del _L0_xattn_all
    return {'x': x, 'ctx_768': ctx_768, 'L0_xattn_n1_g': _L0_xattn_in['n1_g'], 'L0_xattn_n1_b': _L0_xattn_in['n1_b'], 'L0_xattn_q1': _L0_xattn_in['q1'], 'L0_xattn_k1': _L0_xattn_in['k1'], 'L0_xattn_v1': _L0_xattn_in['v1'], 'L0_xattn_o1_w': _L0_xattn_in['o1_w'], 'L0_xattn_o1_b': _L0_xattn_in['o1_b'], 'L0_xattn_n2_g': _L0_xattn_in['n2_g'], 'L0_xattn_n2_b': _L0_xattn_in['n2_b'], 'L0_xattn_q2': _L0_xattn_in['q2'], 'L0_xattn_k2': _L0_xattn_in['k2'], 'L0_xattn_v2': _L0_xattn_in['v2'], 'L0_xattn_o2_w': _L0_xattn_in['o2_w'], 'L0_xattn_o2_b': _L0_xattn_in['o2_b'], 'L0_xattn_n3_g': _L0_xattn_in['n3_g'], 'L0_xattn_n3_b': _L0_xattn_in['n3_b'], 'L0_xattn_ff_w1': _L0_xattn_in['ff_w1'], 'L0_xattn_ff_b1': _L0_xattn_in['ff_b1'], 'L0_xattn_ff_w2': _L0_xattn_in['ff_w2'], 'L0_xattn_ff_b2': _L0_xattn_in['ff_b2']}

def reference(x, ctx_768, L0_xattn_n1_g, L0_xattn_n1_b, L0_xattn_q1, L0_xattn_k1, L0_xattn_v1, L0_xattn_o1_w, L0_xattn_o1_b, L0_xattn_n2_g, L0_xattn_n2_b, L0_xattn_q2, L0_xattn_k2, L0_xattn_v2, L0_xattn_o2_w, L0_xattn_o2_b, L0_xattn_n3_g, L0_xattn_n3_b, L0_xattn_ff_w1, L0_xattn_ff_b1, L0_xattn_ff_w2, L0_xattn_ff_b2):
    import jax
    import jax.numpy as jnp

    def _L0_xattn_ref(x, context, heads, n1_g, n1_b, q1, k1, v1, o1_w, o1_b, n2_g, n2_b, q2, k2, v2, o2_w, o2_b, n3_g, n3_b, ff_w1, ff_b1, ff_w2, ff_b2):
        import jax, jax.numpy as jnp
        import numpy as np
        D = 320
        H = 20
        DH = D // H
        CTX = 192
        FF_IN = 4 * D
        EPS = 1e-05

        def _ln(x, g, b):
            m = jnp.mean(x, axis=-1, keepdims=True)
            v = jnp.mean(jnp.square(x - m), axis=-1, keepdims=True)
            return (x - m) * jax.lax.rsqrt(v + EPS) * g + b

        def _attn(x, ctx, wq, wk, wv, wo, bo, heads):
            b, n, _ = x.shape
            j = ctx.shape[1]
            dh = wq.shape[1] // heads
            scale = dh ** (-0.5)
            q = (x @ wq).reshape(b, n, heads, dh).transpose(0, 2, 1, 3)
            k = (ctx @ wk).reshape(b, j, heads, dh).transpose(0, 2, 1, 3)
            v = (ctx @ wv).reshape(b, j, heads, dh).transpose(0, 2, 1, 3)
            sim = jnp.einsum('bhid,bhjd->bhij', q, k) * scale
            a = jax.nn.softmax(sim, axis=-1)
            out = jnp.einsum('bhij,bhjd->bhid', a, v)
            out = out.transpose(0, 2, 1, 3).reshape(b, n, heads * dh)
            return out @ wo + bo
        h1 = _ln(x, n1_g, n1_b)
        x = _attn(h1, h1, q1, k1, v1, o1_w, o1_b, heads) + x
        h2 = _ln(x, n2_g, n2_b)
        x = _attn(h2, context, q2, k2, v2, o2_w, o2_b, heads) + x
        h3 = _ln(x, n3_g, n3_b)
        proj = h3 @ ff_w1 + ff_b1
        a, g = jnp.split(proj, 2, axis=-1)
        ff = a * jax.nn.gelu(g, approximate=False) @ ff_w2 + ff_b2
        return ff + x
    x = _L0_xattn_ref(x, ctx_768, 20, L0_xattn_n1_g, L0_xattn_n1_b, L0_xattn_q1, L0_xattn_k1, L0_xattn_v1, L0_xattn_o1_w, L0_xattn_o1_b, L0_xattn_n2_g, L0_xattn_n2_b, L0_xattn_q2, L0_xattn_k2, L0_xattn_v2, L0_xattn_o2_w, L0_xattn_o2_b, L0_xattn_n3_g, L0_xattn_n3_b, L0_xattn_ff_w1, L0_xattn_ff_b1, L0_xattn_ff_w2, L0_xattn_ff_b2)
    return x

_drawn_inputs = setup_inputs


def setup_inputs(seed=0):
    import zlib

    import numpy as np

    out = dict(_drawn_inputs(seed))
    spreads = {'L0_xattn_n1_g': (1.0, 0.2),
     'L0_xattn_n1_b': (0.0, 0.1),
     'L0_xattn_o1_b': (0.0, 0.1),
     'L0_xattn_n2_g': (1.0, 0.2),
     'L0_xattn_n2_b': (0.0, 0.371),
     'L0_xattn_o2_b': (0.0, 0.1),
     'L0_xattn_n3_g': (1.0, 0.2),
     'L0_xattn_n3_b': (0.0, 0.1),
     'L0_xattn_ff_b1': (0.0, 0.1),
     'L0_xattn_ff_b2': (0.0, 0.1)}
    factors = {}
    for name, (base, spread) in spreads.items():
        noise = np.random.default_rng([zlib.crc32(name.encode()), seed]).standard_normal(out[name].shape)
        drawn = base * np.exp(spread * noise) if base else spread * noise
        out[name] = jnp.asarray(drawn.astype(out[name].dtype))
    for name, factor in factors.items():
        out[name] = (out[name] * factor).astype(out[name].dtype)
    return out
```

```python
from contextlib import ExitStack

import concourse.bass as bass
from concourse import mybir

F32 = mybir.dt.float32
F32R = mybir.dt.float32r
BF16 = mybir.dt.bfloat16
ALU = mybir.AluOpType
ACT = mybir.ActivationFunctionType
AX_X = mybir.AxisListType.X

B, N, D = 32, 100, 320
H, DH = 20, 16
J, C = 361, 192
FF = 1280
EPS = 1e-5
SCALE = DH ** -0.5
P = 128
U = 2
NT = B // U
SL = 6
KS = SL * DH
KM = KS + 3
JT = [(0, 120), (120, 120), (240, 121)]
JP = 362
G, HG = 4, 5
DVE_STEPS, POOL_STEPS = 12, 44
HB = 10
D1 = DH + 1



def work_jobs():
    both = range(U)
    jobs = [("h1", u, 0) for u in both]
    jobs += [(w, u, 0) for u in both for w in ("q1", "k1", "v1")]
    jobs += [(w, 0, i) for i in range(3) for w in ("kc", "vc")]
    jobs += [(w, u, i) for u in both for w in ("q1t", "k1t") for i in range(2)]
    jobs += [("kct", 0, i) for i in range(H // 2)]
    jobs += [("m1t", u, i) for u in both for i in range(2)]
    jobs += [("o1t", u, 0) for u in both] + [("o1", u, 0) for u in both]
    jobs += [("kc", 1, 0), ("vc", 1, 0)]
    jobs += [("h2", u, 0) for u in both] + [("q2", u, 0) for u in both]
    jobs += [(w, 1, i) for i in (1, 2) for w in ("kc", "vc")]
    jobs += [("q2t", u, i) for u in both for i in range(2)]
    jobs += [("kct", 1, i) for i in range(H // 2)]
    jobs += [("m2t", u, i) for u in both for i in range(2)]
    jobs += [("o2t", 0, 0), ("o2", 0, 0), ("o2t", 1, 0), ("o2", 1, 0)]
    return jobs


NW = 3
WORK_JOBS = work_jobs()
WORK = {job: (i % NW, i // NW) for i, job in enumerate(WORK_JOBS)}
WORK_PER = [sum(1 for b, _ in WORK.values() if b == k) for k in range(NW)]

SCORE_JOBS = [(1, u, g) for u in range(U) for g in range(G)] + [(2, u, h) for u in range(U) for h in range(H)]
SCORE = {job: (i % 2, i // 2) for i, job in enumerate(SCORE_JOBS)}
SCORE_PER = len(SCORE) // 2
MAX_PER = G + H

EXP_JOBS = [(1, u, g, 0) for u in range(U) for g in range(G)] + \
    [(2, u, g, j) for u in range(U) for g in range(G) for j in range(3)]
EXP = {job: i for i, job in enumerate(EXP_JOBS)}
EXP_PER = len(EXP)
NPT = 6
PV_PER = 2 * U * G


def pv_before(job):
    i = EXP[job]
    if i < NPT:
        return 0
    a, u, g, _ = EXP_JOBS[i - NPT]
    return (a - 1) * U * G + u * G + g + 1


def rows3(w):
    return [(0, P, 0, w[0:P]), (0, P, 1, w[P:2 * P]), (0, 64, 2, w[2 * P:D]), (64, P, 2, w[2 * P:D])]


def rows2(w):
    return [(0, P, 0, w[0:P]), (0, 64, 1, w[P:C]), (64, P, 1, w[P:C])]


def build(nc, x, ctxT, n1_g, n1_b, q1, k1, v1, o1_w, o1_b, n2_g, n2_b, q2, k2, v2, o2_w, o2_b,
          n3_g, n3_b, ff_w1, ff_b1, ff_w2, ff_b2, out):
    x2_dram = nc.dram_tensor("x2_dram", [B * N, D], F32).ap()
    attention_phase(nc, x, ctxT, n1_g, n1_b, (q1, k1, v1), o1_w, o1_b, n2_g, n2_b, q2, k2, v2, o2_w, o2_b,
                    x2_dram.rearrange("(b n) d -> b n d", n=N))
    feed_forward_phase(nc, x2_dram, n3_g, n3_b, ff_w1, ff_b1, ff_w2, ff_b2, out.rearrange("b n d -> (b n) d"))


def attention_phase(nc, x, ctxT, n1_g, n1_b, qkv1, o1_w, o1_b, n2_g, n2_b, q2, k2, v2, o2_w, o2_b, x2_dram):
    with ExitStack() as ctx:
        def sb(name, shape, dt=F32):
            return ctx.enter_context(nc.sbuf_tensor(name, shape, dt))

        names = {"q1": (qkv1[0], 3), "k1": (qkv1[1], 3), "v1": (qkv1[2], 3), "kc": (k2, 2), "vc": (v2, 2),
                 "o1": (o1_w, 3), "q2": (q2, 3), "o2": (o2_w, 3)}
        whi = {k: sb(f"w_{k}_hi", [P, kt, D], F32R) for k, (_, kt) in names.items()}
        wlo = {k: sb(f"w_{k}_lo", [P, kt, D], F32R) for k, (_, kt) in names.items()}
        vectors = {"n1_g": n1_g, "n1_b": n1_b, "n2_g": n2_g, "n2_b": n2_b, "o1_b": o1_b, "o2_b": o2_b}
        vec = {k: sb(f"{k}_rows", [N, D]) for k in vectors}
        identf = sb("identf", [P, P])
        identb = sb("identb", [P, P], BF16)
        neg_half, eps, one = sb("neg_half", [P, 1]), sb("eps", [P, 1]), sb("one", [P, 1])

        with ExitStack() as prep:
            raw = {k: prep.enter_context(nc.sbuf_tensor(f"w_{k}_raw", [P, kt, D], F32))
                   for k, (_, kt) in names.items()}
            weight_landed = {k: prep.enter_context(nc.semaphore(f"w_{k}_landed")) for k in names}
            vectors_landed = prep.enter_context(nc.semaphore("vectors_landed"))
            whi_made = prep.enter_context(nc.semaphore("whi_made"))
            ident_step = prep.enter_context(nc.semaphore("ident_step"))
            block = prep.enter_context(nc.Block())

            @block.sync
            def _(sp):
                for k, (w, kt) in names.items():
                    for p0, p1, tile, src in (rows3(w) if kt == 3 else rows2(w)):
                        sp.dma_start(raw[k][p0:p1, tile, :], src).then_inc(weight_landed[k], 16)
                for k, v in vectors.items():
                    src = v.rearrange("(a d) -> a d", a=1).broadcast_to([N, D])
                    sp.dma_start(vec[k][:], src).then_inc(vectors_landed, 16)
                sp.wait_ge(vectors_landed, 16 * len(vectors))

            @block.scalar
            def _(act):
                for k, (_, kt) in names.items():
                    act.wait_ge(weight_landed[k], 16 * (kt + 1))
                    nc.scalar.copy(whi[k][:], raw[k][:]).then_inc(whi_made, 1)

            @block.vector
            def _(dve):
                nc.vector.memset(neg_half[:], -0.5)
                nc.vector.memset(eps[:], EPS)
                nc.vector.memset(one[:], 1.0)
                for i, k in enumerate(names):
                    dve.wait_ge(whi_made, i + 1)
                    nc.vector.tensor_tensor(wlo[k][:], raw[k][:], whi[k][:].bitcast(F32), ALU.subtract)

            @block.gpsimd
            def _(pool):
                make_identity(nc, pool, identf, ident_step)
                pool.wait_ge(ident_step, 2)
                nc.gpsimd.tensor_copy(identb[:], identf[:])

        def two(name, shape, dt=F32):
            return [sb(f"{name}{u}", shape, dt) for u in range(U)]

        spacer = sb("spacer", [P, 1])
        xin = two("xin", [N, D])
        x1 = two("x1", [N, D])
        x2 = two("x2", [N, D])
        xres = two("xres", [N, D])
        h = two("h", [N, D + 64])
        centred = two("centred", [N, D])
        stats = two("stats", [N, 6])
        mv = two("mv", [N, 2])
        var_eps = two("var_eps", [N, 1])
        rstd = two("rstd", [N, 1])
        t_hi = two("t_hi", [P, 3, N], F32R)
        t_lo = two("t_lo", [P, 2, N], F32R)
        stack_q = two("stack_q", [N, H, SL, DH], BF16)
        stack_k = two("stack_k", [N, H, SL, DH], BF16)
        rest_q = two("rest_q", [N, D])
        rest_k = two("rest_k", [N, D])
        stack_c = [sb(f"stack_c{i}", [n, H, SL, DH], BF16) for i, (_, n) in enumerate(JT)]
        rest_c = [sb(f"rest_c{i}", [n, D]) for i, (_, n) in enumerate(JT)]
        qT = two("qT", [KM, H, N], BF16)
        kT = two("kT", [KM, H, N], BF16)
        kcT = two("kcT", [KM, H, JP], BF16)
        vs = two("vs", [N, H, D1])
        vc = two("vc", [JT[2][1], 3, H, D1])
        ctx_raw = two("ctx_raw", [P, 2, J])
        ctx_hi = sb("ctx_hi", [P, 2, J], F32R)
        ctx_lo = sb("ctx_lo", [P, J], F32R)
        neg_max = two("neg_max", [N, H])
        max_rest = two("max_rest", [N, H])
        max_parts = two("max_parts", [N, H, 4], BF16)
        probs = [sb(f"probs{i}", [JT[2][1], HG * N]) for i in range(NPT)]
        rden = two("rden", [N, H])

        work = [ctx.enter_context(nc.psum_tensor(f"work{i}", [P, 512], F32)) for i in range(NW)]
        score = [ctx.enter_context(nc.psum_tensor(f"score{i}", [P, 512], F32)) for i in range(2)]
        expin = [ctx.enter_context(nc.psum_tensor(f"expin{i}", [P, 512], F32)) for i in range(2)]
        attn = ctx.enter_context(nc.psum_tensor("attn", [P, 512], F32))

        PER, START = {}, {}

        def sem(name, per, first=0):
            s = ctx.enter_context(nc.semaphore(name))
            PER[s], START[s] = per, first
            return s

        def start(eng, *sems):
            for s in sems:
                eng.sem_inc(s, START[s])

        def sem2(name, per, first=0):
            return [sem(f"{name}{u}", per, first) for u in range(U)]

        x_landed, ctx_landed, x2_stored = sem2("x_landed", 16), sem2("ctx_landed", 48), sem2("x2_stored", 16, 16)
        ones_set = sem("ones_set", 0)
        stats_made = sem2("stats_made", 2)
        h_made = sem2("h_made", 2)
        lo_made = sem2("lo_made", 4, 1)
        rest_q_made, rest_k_made, rest_c_made = sem2("rest_q_made", 2), sem2("rest_k_made", 1), sem("rest_c_made", 6)
        qT_made = sem2("qT_made", 4)
        max_made = sem2("max_made", MAX_PER, 1)
        mT_made = sem2("mT_made", 4)
        o_normed = sem2("o_normed", 2, 1)
        x1_made, x2_made = sem2("x1_made", 1), sem2("x2_made", 1, 1)
        rstd_made = sem2("rstd_made", 2)
        xres_made = sem2("xres_made", 2)
        ctx_split = sem("ctx_split", 2)
        stack_q_made, stack_k_made, stack_c_made = sem2("stack_q_made", 2), sem2("stack_k_made", 1), sem("stack_c_made", 6)
        parts_made = sem2("parts_made", 4)
        hi_made = sem2("hi_made", 4)
        p0_q_made, p0_k_made, p0_c_made = sem2("p0_q_made", 2), sem2("p0_k_made", 1), sem("p0_c_made", 6)
        v_made, vc_made = sem2("v_made", 1), sem2("vc_made", 3)
        kT_made = sem2("kT_made", 2)
        kcT_made = sem2("kcT_made", H // 2)
        probs_made = sem("probs_made", EXP_PER, 1)
        work_ready = [sem(f"work_ready{i}", WORK_PER[i], 1) for i in range(NW)]
        score_ready = [sem(f"score_ready{i}", SCORE_PER) for i in range(2)]
        exp_ready = [sem(f"exp_ready{i}", EXP_PER // 2) for i in range(2)]
        pv_made = sem("pv_made", PV_PER, 1)
        dve_step = sem("dve_step", DVE_STEPS)
        pool_step = sem("pool_step", POOL_STEPS)

        def at(t, s, n):
            assert n > 0 or START[s] > 0, s
            return t * PER[s] + (START[s] + n)

        def emptied(job):
            kind, u, i = job
            return {
                "h1": (lo_made[u], 1), "o1t": (lo_made[u], 2), "h2": (lo_made[u], 3), "o2t": (lo_made[u], 4),
                "q1": (rest_q_made[u], 1), "q2": (rest_q_made[u], 2), "k1": (rest_k_made[u], 1),
                "v1": (v_made[u], 1), "kc": (rest_c_made, 3 * u + i + 1), "vc": (vc_made[u], i + 1),
                "q1t": (qT_made[u], i + 1), "q2t": (qT_made[u], i + 3), "k1t": (kT_made[u], i + 1),
                "kct": (kcT_made[u], i + 1), "m1t": (mT_made[u], i + 1), "m2t": (mT_made[u], i + 3),
                "o1": (x1_made[u], 1), "o2": (x2_made[u], 1),
            }[kind]

        def wbank(job):
            return work[WORK[job][0]]

        def wbank16(job):
            return work[WORK[job][0]][:, :].bitcast(BF16)

        def filled(t, job):
            k, n = WORK[job]
            return work_ready[k], at(t, work_ready[k], n + 1)

        def q_slots(stack, part):
            return {0: stack[:, :, 0:4:3, :], 1: stack[:, :, 1:5:3, :], 2: stack[:, :, 2, :],
                    "last": stack[:, :, 5, :]}[part]

        def k_slots(stack, part):
            return {0: stack[:, :, 0:3, :], 1: stack[:, :, 3:5, :], 2: stack[:, :, 5, :]}[part]

        def heads(ap):
            return ap.rearrange("p (h d) -> p h d", d=DH)

        def repeated(ap, n, k):
            return heads(ap).unsqueeze(2).broadcast_to([n, H, k, DH])

        block = ctx.enter_context(nc.Block())

        @block.sync
        def _(sp):
            def load(b, u):
                sp.dma_start(xin[u][:], x[b]).then_inc(x_landed[u], 16)

            def load_context(b, u):
                c = ctxT[b]
                sp.dma_start(ctx_raw[u][0:P, 0, :], c[0:P]).then_inc(ctx_landed[u], 16)
                sp.dma_start(ctx_raw[u][0:64, 1, :], c[P:C]).then_inc(ctx_landed[u], 16)
                sp.dma_start(ctx_raw[u][64:P, 1, :], c[P:C]).then_inc(ctx_landed[u], 16)

            start(sp, *x2_stored)
            for u in range(U):
                load(u, u)
                load_context(u, u)
            with sp.Fori(0, NT - 1) as t:
                for u in range(U):
                    sp.wait_ge(ctx_split, at(t, ctx_split, u + 1))
                    load_context(t * U + (U + u), u)
                for u in range(U):
                    sp.wait_ge(xres_made[u], at(t, xres_made[u], 1))
                    sp.wait_ge(h_made[u], at(t, h_made[u], 1))
                    load(t * U + (U + u), u)
                for u in range(U):
                    sp.wait_ge(x2_made[u], at(t, x2_made[u], 1))
                    sp.dma_start(x2_dram[t * U + u], x2[u][:]).then_inc(x2_stored[u], 16)
            for u in range(U):
                sp.wait_ge(x2_made[u], at(NT - 1, x2_made[u], 1))
                sp.dma_start(x2_dram[B - U + u], x2[u][:]).then_inc(x2_stored[u], 16)
            for u in range(U):
                sp.wait_ge(x2_stored[u], at(NT - 1, x2_stored[u], 16))

        @block.tensor
        def _(pe):
            def fill(t, job):
                k, n = WORK[job]
                if n:
                    s, rise = emptied(WORK_JOBS[(n - 1) * NW + k])
                    pe.wait_ge(s, at(t, s, rise))
                else:
                    s, _ = emptied(WORK_JOBS[(WORK_PER[k] - 1) * NW + k])
                    pe.wait_ge(s, at(t, s, 0))

            def done(ins, job):
                ins.then_inc(work_ready[WORK[job][0]], 1)

            def transpose_features(t, job, u):
                fill(t, job)
                for k in range(3):
                    mm = pe.transpose(wbank(job)[:, k * N:(k + 1) * N], h[u][:, k * P:(k + 1) * P], identf[0:N, 0:N])
                done(mm, job)

            def project(t, job, u, w, n):
                fill(t, job)
                dst, a, b = wbank(job)[0:N, 0:D], t_hi[u], t_lo[u]
                pe.wait_ge(hi_made[u], at(t, hi_made[u], n))
                pe.matmul(dst, a[:, 0, :], whi[w][:, 0, :], start=True, stop=False)
                pe.matmul(dst, a[:, 0, :], wlo[w][:, 0, :], start=False, stop=False)
                pe.matmul(dst, a[:, 1, :], whi[w][:, 1, :], start=False, stop=False)
                pe.matmul(dst, a[:, 1, :], wlo[w][:, 1, :], start=False, stop=False)
                pe.wait_ge(lo_made[u], at(t, lo_made[u], n))
                pe.matmul(dst, b[:, 0, :], whi[w][:, 0, :], start=False, stop=False)
                pe.matmul(dst, b[:, 1, :], whi[w][:, 1, :], start=False, stop=False)
                pe.matmul(dst, a[:, 2, :], whi[w][:, 2, :], start=False, stop=False)
                done(pe.matmul(dst, a[:, 2, :], wlo[w][:, 2, :], start=False, stop=True), job)

            def project_context(t, u, i):
                pe.wait_ge(ctx_split, at(t, ctx_split, u + 1))
                j0, n = JT[i]
                hi0, lo0, last = ctx_hi[:, 0, j0:j0 + n], ctx_lo[:, j0:j0 + n], ctx_hi[:, 1, j0:j0 + n]
                for w in ("kc", "vc"):
                    job = (w, u, i)
                    fill(t, job)
                    dst = wbank(job)[0:n, 0:D]
                    pe.matmul(dst, hi0, whi[w][:, 0, :], start=True, stop=False)
                    pe.matmul(dst, hi0, wlo[w][:, 0, :], start=False, stop=False)
                    pe.matmul(dst, lo0, whi[w][:, 0, :], start=False, stop=False)
                    pe.matmul(dst, last, whi[w][:, 1, :], start=False, stop=False)
                    done(pe.matmul(dst, last, wlo[w][:, 1, :], start=False, stop=True), job)

            def transpose_stack(t, kind, u, stack):
                for i in range(2):
                    job = (kind, u, i)
                    fill(t, job)
                    for k in range(HB):
                        src = stack[:, i * HB + k].rearrange("p s d -> p (s d)")
                        mm = pe.transpose(wbank16(job)[0:KS, k * N:(k + 1) * N], src, identb[0:N, 0:N])
                    done(mm, job)

            def transpose_context_stack(t, u, i):
                job = ("kct", u, i)
                fill(t, job)
                for k in range(2):
                    for jt, (j0, n) in enumerate(JT):
                        src = stack_c[jt][:, 2 * i + k].rearrange("p s d -> p (s d)")
                        mm = pe.transpose(wbank16(job)[0:KS, k * JP + j0:k * JP + j0 + n], src, identb[0:n, 0:n])
                done(mm, job)

            def score_bank(t, a, u, i):
                n = SCORE_JOBS.index((a, u, i)) - 2
                if n >= 0:
                    a0, u0, i0 = SCORE_JOBS[n]
                    pe.wait_ge(max_made[u0], at(t, max_made[u0], (a0 - 1) * G + i0 + 1))
                else:
                    pe.wait_ge(max_made[1], at(t, max_made[1], 0))

            def self_scores(t, u, g):
                k = SCORE[1, u, g][0]
                score_bank(t, 1, u, g)
                for i in range(HG):
                    hd = g * HG + i
                    mm = pe.matmul(score[k][0:N, i * N:(i + 1) * N], qT[u][0:KS, hd, :], kT[u][0:KS, hd, :],
                                   start=True, stop=True)
                mm.then_inc(score_ready[k], 1)

            def cross_scores(t, u, hd):
                k = SCORE[2, u, hd][0]
                score_bank(t, 2, u, hd)
                pe.matmul(score[k][0:N, 0:J], qT[u][0:KS, hd, :], kcT[u][0:KS, hd, 0:J],
                          start=True, stop=True).then_inc(score_ready[k], 1)

            def transpose_max(t, a, u):
                for i in range(2):
                    job = (f"m{a}t", u, i)
                    fill(t, job)
                    pe.wait_ge(parts_made[u], at(t, parts_made[u], (a - 1) * 2 + i + 1))
                    for k in range(HB):
                        mm = pe.transpose(wbank16(job)[KS:KM, k * N:(k + 1) * N], max_parts[u][:, i * HB + k, 0:3],
                                          identb[0:N, 0:N])
                    done(mm, job)

            def scores_for_exp(t, a, u, g, jt):
                e = EXP[a, u, g, jt]
                pe.wait_ge(probs_made, at(t, probs_made, max(e - 1, 0)))
                pe.wait_ge(mT_made[u], at(t, mT_made[u], (a - 1) * 2 + (g * HG + HG - 1) // HB + 1))
                j0, n = JT[jt] if a == 2 else (0, N)
                keys = kcT if a == 2 else kT
                for i in range(HG):
                    hd = g * HG + i
                    mm = pe.matmul(expin[e % 2][0:n, i * N:(i + 1) * N], keys[u][:, hd, j0:j0 + n],
                                   qT[u][:, hd, :], start=True, stop=True)
                mm.then_inc(exp_ready[e % 2], 1)

            def times_v(t, a, u, g):
                if g == 0:
                    pe.wait_ge(o_normed[1 - u], at(t, o_normed[1 - u], a - 1 if u == 0 else a))
                    if a == 1:
                        pe.wait_ge(v_made[u], at(t, v_made[u], 1))
                    else:
                        pe.wait_ge(vc_made[u], at(t, vc_made[u], 3))
                tiles = range(3) if a == 2 else range(1)
                pe.wait_ge(probs_made, at(t, probs_made, EXP[a, u, g, tiles[-1]] + 1))
                for i in range(HG):
                    hd = g * HG + i
                    for jt in tiles:
                        n = JT[jt][1] if a == 2 else N
                        v = vc[u][0:n, jt, hd, :] if a == 2 else vs[u][:, hd, :]
                        mm = pe.matmul(attn[0:N, hd * D1:(hd + 1) * D1],
                                       probs[EXP[a, u, g, jt] % NPT][0:n, i * N:(i + 1) * N], v,
                                       start=(jt == 0), stop=(jt == tiles[-1]))
                mm.then_inc(pv_made, 1)

            start(pe, *work_ready, pv_made)
            pe.wait_ge(ones_set, 3 * U)
            with pe.Fori(0, NT) as t:
                for u in range(U):
                    pe.wait_ge(h_made[u], at(t, h_made[u], 1))
                    transpose_features(t, ("h1", u, 0), u)
                for u in range(U):
                    for w in ("q1", "k1", "v1"):
                        project(t, (w, u, 0), u, w, 1)
                for i in range(3):
                    project_context(t, 0, i)
                for u in range(U):
                    pe.wait_ge(stack_q_made[u], at(t, stack_q_made[u], 1))
                    transpose_stack(t, "q1t", u, stack_q[u])
                    pe.wait_ge(stack_k_made[u], at(t, stack_k_made[u], 1))
                    transpose_stack(t, "k1t", u, stack_k[u])
                for u in range(U):
                    pe.wait_ge(qT_made[u], at(t, qT_made[u], 2))
                    pe.wait_ge(kT_made[u], at(t, kT_made[u], 2))
                    for g in range(G):
                        self_scores(t, u, g)
                pe.wait_ge(stack_c_made, at(t, stack_c_made, 3))
                for i in range(H // 2):
                    transpose_context_stack(t, 0, i)
                for u in range(U):
                    transpose_max(t, 1, u)
                for u in range(U):
                    for g in range(G):
                        scores_for_exp(t, 1, u, g, 0)
                        if g:
                            times_v(t, 1, u, g - 1)
                    times_v(t, 1, u, G - 1)
                for u in range(U):
                    pe.wait_ge(o_normed[u], at(t, o_normed[u], 1))
                    transpose_features(t, ("o1t", u, 0), u)
                for u in range(U):
                    project(t, ("o1", u, 0), u, "o1", 2)
                project_context(t, 1, 0)
                for u in range(U):
                    pe.wait_ge(h_made[u], at(t, h_made[u], 2))
                    transpose_features(t, ("h2", u, 0), u)
                for u in range(U):
                    project(t, ("q2", u, 0), u, "q2", 3)
                for i in (1, 2):
                    project_context(t, 1, i)
                for u in range(U):
                    pe.wait_ge(stack_q_made[u], at(t, stack_q_made[u], 2))
                    transpose_stack(t, "q2t", u, stack_q[u])
                pe.wait_ge(qT_made[0], at(t, qT_made[0], 4))
                pe.wait_ge(kcT_made[0], at(t, kcT_made[0], H // 2))
                pe.wait_ge(stack_c_made, at(t, stack_c_made, 6))
                for hd in range(H):
                    cross_scores(t, 0, hd)
                    if hd % 2:
                        transpose_context_stack(t, 1, hd // 2)
                transpose_max(t, 2, 0)
                pe.wait_ge(qT_made[1], at(t, qT_made[1], 4))
                pe.wait_ge(kcT_made[1], at(t, kcT_made[1], H // 2))
                for g in range(G):
                    for jt in range(3):
                        scores_for_exp(t, 2, 0, g, jt)
                        cross_scores(t, 1, g * HG + jt)
                    for k in range(3, HG):
                        cross_scores(t, 1, g * HG + k)
                    if g:
                        times_v(t, 2, 0, g - 1)
                times_v(t, 2, 0, G - 1)
                transpose_max(t, 2, 1)
                for g in range(G):
                    for jt in range(3):
                        scores_for_exp(t, 2, 1, g, jt)
                    if g == 0:
                        pe.wait_ge(o_normed[0], at(t, o_normed[0], 2))
                        transpose_features(t, ("o2t", 0, 0), 0)
                    else:
                        times_v(t, 2, 1, g - 1)
                    if g == 1:
                        project(t, ("o2", 0, 0), 0, "o2", 4)
                times_v(t, 2, 1, G - 1)
                pe.wait_ge(o_normed[1], at(t, o_normed[1], 2))
                transpose_features(t, ("o2t", 1, 0), 1)
                project(t, ("o2", 1, 0), 1, "o2", 4)

        @block.vector
        def _(dve):
            step = [0]

            def link(t, ins):
                step[0] += 1
                ins.then_inc(dve_step, 1)
                dve.wait_ge(dve_step, at(t, dve_step, step[0]))

            def layer_norm(t, u, a, src):
                g, b = ("n1_g", "n1_b") if a == 1 else ("n2_g", "n2_b")
                link(t, nc.vector.bn_stats(stats[u][:], src[:]))
                nc.vector.memset(spacer[0:1, :], 0.0)
                nc.vector.bn_aggr(mv[u][:], stats[u][:]).then_inc(stats_made[u], 1)
                dve.wait_ge(stats_made[u], at(t, stats_made[u], a))
                link(t, nc.vector.scalar_tensor_tensor(out=centred[u][:], in0=src[:], scalar=mv[u][:, 0:1],
                                                       in1=vec[g][:], op0=ALU.subtract, op1=ALU.mult))
                dve.wait_ge(rstd_made[u], at(t, rstd_made[u], a))
                nc.vector.scalar_tensor_tensor(out=h[u][:, D:D + 64], in0=centred[u][:, 2 * P:D], scalar=rstd[u][:],
                                               in1=vec[b][:, 2 * P:D], op0=ALU.mult, op1=ALU.add)
                nc.vector.scalar_tensor_tensor(out=h[u][:, 0:D], in0=centred[u][:], scalar=rstd[u][:],
                                               in1=vec[b][:], op0=ALU.mult, op1=ALU.add).then_inc(h_made[u], 1)

            def lows(t, job, u, n):
                dve.wait_ge(hi_made[u], at(t, hi_made[u], n))
                v = wbank(job)[:, 0:3 * N].rearrange("p (k n) -> p k n", k=3)
                nc.vector.tensor_tensor(t_hi[u][64:P, 2, :], v[64:P, 2, :], t_hi[u][64:P, 2, :].bitcast(F32),
                                        ALU.subtract)
                nc.vector.tensor_tensor(t_lo[u][:], v[:, 0:2, :], t_hi[u][:, 0:2, :].bitcast(F32),
                                        ALU.subtract).then_inc(lo_made[u], 1)

            def rest(job, n, first, dst, made):
                nc.vector.tensor_tensor(heads(dst[:]), heads(wbank(job)[0:n, 0:D]), first,
                                        ALU.subtract).then_inc(made, 1)

            def rest_q_of(t, kind, u, n):
                dve.wait_ge(p0_q_made[u], at(t, p0_q_made[u], n))
                rest((kind, u, 0), N, stack_q[u][:, :, 0, :], rest_q[u], rest_q_made[u])

            def rest_c_of(t, u, i):
                dve.wait_ge(p0_c_made, at(t, p0_c_made, 3 * u + i + 1))
                rest(("kc", u, i), JT[i][1], stack_c[i][:, :, 0, :], rest_c[i], rest_c_made)

            def copy_q(t, kind, u):
                for i in range(2):
                    job = (kind, u, i)
                    dve.wait_ge(*filled(t, job))
                    nc.vector.tensor_copy(qT[u][0:KS, i * HB:(i + 1) * HB, :],
                                          wbank16(job)[0:KS, 0:HB * N].rearrange("p (h n) -> p h n", h=HB))\
                        .then_inc(qT_made[u], 1)

            def copy_max(t, a, u):
                for i in range(2):
                    job = (f"m{a}t", u, i)
                    dve.wait_ge(*filled(t, job))
                    nc.vector.tensor_copy(qT[u][KS:KM, i * HB:(i + 1) * HB, :],
                                          wbank16(job)[KS:KM, 0:HB * N].rearrange("p (h n) -> p h n", h=HB))\
                        .then_inc(mT_made[u], 1)

            def maxima(t, a, u, i):
                k, n = SCORE[a, u, i]
                dve.wait_ge(score_ready[k], at(t, score_ready[k], n + 1))
                if a == 1:
                    dst, src = neg_max[u][:, i * HG:(i + 1) * HG], \
                        score[k][0:N, 0:HG * N].rearrange("p (h j) -> p h j", h=HG)
                else:
                    dst, src = neg_max[u][:, i:i + 1], score[k][0:N, 0:J]
                nc.vector.tensor_reduce(dst, src, AX_X, ALU.max, negate=True).then_inc(max_made[u], 1)

            def divide(t, a, u):
                dve.wait_ge(pv_made, at(t, pv_made, (a - 1) * U * G + (u + 1) * G))
                o = attn[0:N, 0:H * D1].rearrange("p (h d) -> p h d", h=H)
                link(t, nc.vector.reciprocal(rden[u][:].unsqueeze(2), o[:, :, DH:D1]))
                r = rden[u][:].unsqueeze(2).broadcast_to([N, H, DH])
                nc.vector.tensor_tensor(heads(h[u][:, D:D + 64]), o[:, 16:H, 0:DH], r[:, 16:H, :], ALU.mult)
                nc.vector.tensor_tensor(heads(h[u][:, 0:D]), o[:, :, 0:DH], r, ALU.mult).then_inc(o_normed[u], 1)

            def add_residual(t, a, u, dst, made):
                job = (f"o{a}", u, 0)
                dve.wait_ge(*filled(t, job))
                dve.wait_ge(xres_made[u], at(t, xres_made[u], a))
                nc.vector.tensor_tensor(dst[:], wbank(job)[0:N, 0:D], xres[u][:], ALU.add).then_inc(made, 1)

            start(dve, *lo_made, *max_made, *o_normed, *x2_made)
            for u in range(U):
                nc.vector.memset(kT[u][KS:KM, :, :], 1.0).then_inc(ones_set, 1)
                nc.vector.memset(kcT[u][KS:KM, :, :], 1.0).then_inc(ones_set, 1)
                nc.vector.memset(vs[u][:, :, DH:D1], 1.0)
                nc.vector.memset(vc[u][:, :, :, DH:D1], 1.0).then_inc(ones_set, 1)
            with dve.Fori(0, NT) as t:
                for u in range(U):
                    dve.wait_ge(x_landed[u], at(t, x_landed[u], 16))
                    layer_norm(t, u, 1, xin[u])
                for u in range(U):
                    lows(t, ("h1", u, 0), u, 1)
                for u in range(U):
                    rest_q_of(t, "q1", u, 1)
                    dve.wait_ge(p0_k_made[u], at(t, p0_k_made[u], 1))
                    rest(("k1", u, 0), N, stack_k[u][:, :, 0, :], rest_k[u], rest_k_made[u])
                for i in range(3):
                    rest_c_of(t, 0, i)
                for u in range(U):
                    copy_q(t, "q1t", u)
                for u in range(U):
                    for g in range(G):
                        maxima(t, 1, u, g)
                for i in range(H // 2):
                    job = ("kct", 0, i)
                    dve.wait_ge(*filled(t, job))
                    nc.vector.tensor_copy(kcT[0][0:KS, 2 * i:2 * i + 2, 0:J],
                                          wbank16(job)[0:KS, 0:2 * JP].rearrange("p (h j) -> p h j", h=2)[:, :, 0:J])\
                        .then_inc(kcT_made[0], 1)
                for u in range(U):
                    copy_max(t, 1, u)
                for u in range(U):
                    divide(t, 1, u)
                for u in range(U):
                    lows(t, ("o1t", u, 0), u, 2)
                for u in range(U):
                    add_residual(t, 1, u, x1[u], x1_made[u])
                    dve.wait_ge(x1_made[u], at(t, x1_made[u], 1))
                    layer_norm(t, u, 2, x1[u])
                rest_c_of(t, 1, 0)
                for u in range(U):
                    lows(t, ("h2", u, 0), u, 3)
                for u in range(U):
                    rest_q_of(t, "q2", u, 2)
                for i in (1, 2):
                    rest_c_of(t, 1, i)
                for u in range(U):
                    copy_q(t, "q2t", u)
                for hd in range(H):
                    maxima(t, 2, 0, hd)
                copy_max(t, 2, 0)
                for hd in range(H):
                    maxima(t, 2, 1, hd)
                copy_max(t, 2, 1)
                divide(t, 2, 0)
                lows(t, ("o2t", 0, 0), 0, 4)
                dve.wait_ge(x2_stored[0], at(t, x2_stored[0], 0))
                add_residual(t, 2, 0, x2[0], x2_made[0])
                divide(t, 2, 1)
                lows(t, ("o2t", 1, 0), 1, 4)
                dve.wait_ge(x2_stored[1], at(t, x2_stored[1], 0))
                add_residual(t, 2, 1, x2[1], x2_made[1])
            assert step[0] == DVE_STEPS, step[0]

        @block.scalar
        def _(act):
            def high(t, job, u):
                act.wait_ge(*filled(t, job))
                nc.scalar.copy(t_hi[u][:], wbank(job)[:, 0:3 * N].rearrange("p (k n) -> p k n", k=3))\
                    .then_inc(hi_made[u], 1)

            def first_q(t, kind, u):
                job = (kind, u, 0)
                act.wait_ge(*filled(t, job))
                src = wbank(job)[0:N, 0:D]
                nc.scalar.copy(q_slots(stack_q[u], "last"), heads(src))
                nc.scalar.copy(q_slots(stack_q[u], 0), repeated(src, N, 2)).then_inc(p0_q_made[u], 1)

            def first_k(t, job, n, stack, made):
                act.wait_ge(*filled(t, job))
                nc.scalar.copy(k_slots(stack, 0), repeated(wbank(job)[0:n, 0:D], n, 3)).then_inc(made, 1)

            def copy_v(t, job, n, dst, made):
                act.wait_ge(*filled(t, job))
                nc.scalar.copy(dst[:, :, 0:DH], heads(wbank(job)[0:n, 0:D])).then_inc(made, 1)

            def context_parts(t, u, i):
                n = JT[i][1]
                first_k(t, ("kc", u, i), n, stack_c[i], p0_c_made)
                copy_v(t, ("vc", u, i), n, vc[u][0:n, i], vc_made[u])

            def exponentials(t, a, u, g, jt):
                e = EXP[a, u, g, jt]
                n = JT[jt][1] if a == 2 else N
                act.wait_ge(exp_ready[e % 2], at(t, exp_ready[e % 2], e // 2 + 1))
                act.wait_ge(pv_made, at(t, pv_made, pv_before((a, u, g, jt))))
                nc.scalar.activation(probs[e % NPT][0:n, :], expin[e % 2][0:n, 0:HG * N], ACT.Exp,
                                     scale=SCALE).then_inc(probs_made, 1)

            start(act, probs_made)
            with act.Fori(0, NT) as t:
                for u in range(U):
                    high(t, ("h1", u, 0), u)
                for u in range(U):
                    first_q(t, "q1", u)
                    first_k(t, ("k1", u, 0), N, stack_k[u], p0_k_made[u])
                    copy_v(t, ("v1", u, 0), N, vs[u], v_made[u])
                for i in range(3):
                    context_parts(t, 0, i)
                for u in range(U):
                    for i in range(2):
                        job = ("k1t", u, i)
                        act.wait_ge(*filled(t, job))
                        nc.scalar.copy(kT[u][0:KS, i * HB:(i + 1) * HB, :],
                                       wbank16(job)[0:KS, 0:HB * N].rearrange("p (h n) -> p h n", h=HB))\
                            .then_inc(kT_made[u], 1)
                for u in range(U):
                    for g in range(G):
                        exponentials(t, 1, u, g, 0)
                for u in range(U):
                    high(t, ("o1t", u, 0), u)
                context_parts(t, 1, 0)
                for u in range(U):
                    high(t, ("h2", u, 0), u)
                for u in range(U):
                    first_q(t, "q2", u)
                for i in (1, 2):
                    context_parts(t, 1, i)
                for i in range(H // 2):
                    job = ("kct", 1, i)
                    act.wait_ge(*filled(t, job))
                    nc.scalar.copy(kcT[1][0:KS, 2 * i:2 * i + 2, 0:J],
                                   wbank16(job)[0:KS, 0:2 * JP].rearrange("p (h j) -> p h j", h=2)[:, :, 0:J])\
                        .then_inc(kcT_made[1], 1)
                for g in range(G):
                    for jt in range(3):
                        exponentials(t, 2, 0, g, jt)
                for g in range(G):
                    for jt in range(3):
                        exponentials(t, 2, 1, g, jt)
                    if g == 0:
                        high(t, ("o2t", 0, 0), 0)
                high(t, ("o2t", 1, 0), 1)

        @block.gpsimd
        def _(pool):
            step = [0]

            def link(t, ins):
                step[0] += 1
                ins.then_inc(pool_step, 1)
                pool.wait_ge(pool_step, at(t, pool_step, step[0]))

            def inverse_deviation(t, u, a):
                pool.wait_ge(stats_made[u], at(t, stats_made[u], a))
                link(t, nc.gpsimd.tensor_tensor(var_eps[u][:], mv[u][:, 1:2], eps[0:N, :], ALU.add))
                nc.gpsimd.tensor_tensor(rstd[u][:], var_eps[u][:], neg_half[0:N, :], ALU.pow)\
                    .then_inc(rstd_made[u], 1)

            def residual(t, u, a, src):
                nc.gpsimd.tensor_tensor(xres[u][:], src[:], vec[f"o{a}_b"][:], ALU.add).then_inc(xres_made[u], 1)

            def split_context(t, u):
                pool.wait_ge(ctx_landed[u], at(t, ctx_landed[u], 48))
                link(t, nc.gpsimd.tensor_tensor(ctx_hi[:], ctx_raw[u][:], one[:].unsqueeze(2).broadcast_to([P, 2, J]),
                                                ALU.mult))
                link(t, nc.gpsimd.tensor_tensor(ctx_hi[64:P, 1, :], ctx_raw[u][64:P, 1, :],
                                                ctx_hi[64:P, 1, :].bitcast(F32), ALU.subtract))
                nc.gpsimd.tensor_tensor(ctx_lo[:], ctx_raw[u][:, 0, :], ctx_hi[:, 0, :].bitcast(F32),
                                        ALU.subtract).then_inc(ctx_split, 1)

            def more_parts(t, slots, stack, rest, n, made):
                link(t, nc.gpsimd.tensor_tensor(slots(stack, 1), repeated(rest[:], n, 2),
                                                one[0:n, :].unsqueeze(2).unsqueeze(3).broadcast_to([n, H, 2, DH]), ALU.mult))
                second = 1 if slots is q_slots else 3
                nc.gpsimd.tensor_tensor(slots(stack, 2), heads(rest[:]), stack[:, :, second, :], ALU.subtract)\
                    .then_inc(made, 1)

            def more_parts_q(t, u, n):
                pool.wait_ge(rest_q_made[u], at(t, rest_q_made[u], n))
                more_parts(t, q_slots, stack_q[u], rest_q[u], N, stack_q_made[u])

            def more_parts_c(t, u, i):
                pool.wait_ge(rest_c_made, at(t, rest_c_made, 3 * u + i + 1))
                more_parts(t, k_slots, stack_c[i], rest_c[i], JT[i][1], stack_c_made)

            def split_maxima(t, a, u, i):
                pool.wait_ge(max_made[u], at(t, max_made[u], (i + 1) * 2 if a == 1 else G + (i + 1) * HB))
                c = slice(i * HB, (i + 1) * HB)
                ones = one[0:N, :].broadcast_to([N, HB])
                m, r, parts = neg_max[u][:, c], max_rest[u][:, c], max_parts[u][:, c, :]
                link(t, nc.gpsimd.tensor_tensor(parts[:, :, 0], m, ones, ALU.mult))
                link(t, nc.gpsimd.tensor_tensor(r, m, parts[:, :, 0], ALU.subtract))
                link(t, nc.gpsimd.tensor_tensor(parts[:, :, 1], r, ones, ALU.mult))
                nc.gpsimd.tensor_tensor(parts[:, :, 2], r, parts[:, :, 1], ALU.subtract).then_inc(parts_made[u], 1)

            with pool.Fori(0, NT) as t:
                for u in range(U):
                    inverse_deviation(t, u, 1)
                k, n = WORK["vc", 1, 2]
                pool.wait_ge(work_ready[k], at(t, work_ready[k], 0))
                split_context(t, 0)
                for u in range(U):
                    pool.wait_ge(x_landed[u], at(t, x_landed[u], 16))
                    residual(t, u, 1, xin[u])
                for u in range(U):
                    more_parts_q(t, u, 1)
                    pool.wait_ge(rest_k_made[u], at(t, rest_k_made[u], 1))
                    more_parts(t, k_slots, stack_k[u], rest_k[u], N, stack_k_made[u])
                for i in range(3):
                    more_parts_c(t, 0, i)
                pool.wait_ge(*filled(t, ("vc", 0, 2)))
                split_context(t, 1)
                for u in range(U):
                    for i in range(2):
                        split_maxima(t, 1, u, i)
                for u in range(U):
                    inverse_deviation(t, u, 2)
                for u in range(U):
                    residual(t, u, 2, x1[u])
                more_parts_c(t, 1, 0)
                for u in range(U):
                    more_parts_q(t, u, 2)
                for i in (1, 2):
                    more_parts_c(t, 1, i)
                for u in range(U):
                    for i in range(2):
                        split_maxima(t, 2, u, i)
            assert step[0] == POOL_STEPS, step[0]


def make_identity(nc, pool, ident, step):
    nc.gpsimd.memset(ident[:], 0.0).then_inc(step, 1)
    pool.wait_ge(step, 1)
    nc.gpsimd.affine_select(out=ident[:], in_=ident[:], compare_op=ALU.not_equal, fill=1.0, base=0,
                            pattern=[[-1, P]], channel_multiplier=1).then_inc(step, 1)


TT = 5
NF = B * N // (P * TT)
FT = FF // P
W = TT * P // 2
FV_STEPS, FP_STEPS = 2 * TT, TT


def feed_forward_phase(nc, x2, n3_g, n3_b, ff_w1, ff_b1, ff_w2, ff_b2, out):
    with ExitStack() as ctx:
        def sb(name, shape, dt=F32):
            return ctx.enter_context(nc.sbuf_tensor(name, shape, dt))

        w1_hi, w1_lo = sb("w1_hi", [P, 3, 2 * FF], F32R), sb("w1_lo", [P, 3, 2 * FF], F32R)
        w2_hi, w2_lo = sb("w2_hi", [P, FT, D], F32R), sb("w2_lo", [P, FT, D], F32R)
        vectors = {"g": n3_g, "b": n3_b, "ff_b2": ff_b2}
        vec = {k: sb(f"{k}3_rows", [P, D]) for k in vectors}
        b1 = sb("b1_cols", [P, 2 * FT])
        identf = sb("identf3", [P, P])
        neg_half, eps = sb("neg_half3", [P, 1]), sb("eps3", [P, 1])

        CB = 640
        with ExitStack() as prep:
            NB1 = 2 * FF // CB
            raw = [prep.enter_context(nc.sbuf_tensor(f"w1_raw{i}", [P, 3, CB], F32)) for i in range(2)]
            w2_raw = [prep.enter_context(nc.sbuf_tensor(f"w2_raw{i}", [P, FT // 2, D], F32)) for i in range(2)]
            w1_landed = [prep.enter_context(nc.semaphore(f"w1_landed{i}")) for i in range(2)]
            w2_landed = [prep.enter_context(nc.semaphore(f"w2_landed{i}")) for i in range(2)]
            vectors_landed = prep.enter_context(nc.semaphore("vectors3_landed"))
            w_hi_made = prep.enter_context(nc.semaphore("w_hi_made"))
            w_lo_made = prep.enter_context(nc.semaphore("w_lo_made"))
            ident_step = prep.enter_context(nc.semaphore("ident3_step"))
            block = prep.enter_context(nc.Block())

            @block.sync
            def _(sp):
                for i in range(NB1):
                    if i >= 2:
                        sp.wait_ge(w_lo_made, i - 1)
                    w = ff_w1[:, i * CB:(i + 1) * CB]
                    for p0, p1, tile, src in rows3(w):
                        sp.dma_start(raw[i % 2][p0:p1, tile, :], src).then_inc(w1_landed[i % 2], 16)
                    if i < 2:
                        sp.dma_start(w2_raw[i][:], ff_w2.rearrange("(h k p) n -> h p k n", h=2, p=P)[i])\
                            .then_inc(w2_landed[i], 16)
                for k, v in vectors.items():
                    sp.dma_start(vec[k][:], v.rearrange("(a d) -> a d", a=1).broadcast_to([P, D]))\
                        .then_inc(vectors_landed, 16)
                with nc.allow_non_contiguous_dma("a bias, once"):
                    sp.dma_start(b1[:], ff_b1.rearrange("(k p) -> p k", p=P)).then_inc(vectors_landed, 16)
                sp.wait_ge(vectors_landed, 16 * (len(vectors) + 1))

            @block.scalar
            def _(act):
                for i in range(NB1):
                    act.wait_ge(w1_landed[i % 2], 64 * (i // 2 + 1))
                    nc.scalar.copy(w1_hi[:, :, i * CB:(i + 1) * CB], raw[i % 2][:]).then_inc(w_hi_made, 1)
                for i in range(2):
                    act.wait_ge(w2_landed[i], 16)
                    c = slice(i * (FT // 2), (i + 1) * (FT // 2))
                    nc.scalar.copy(w2_hi[:, c, :], w2_raw[i][:]).then_inc(w_hi_made, 1)

            @block.vector
            def _(dve):
                nc.vector.memset(neg_half[:], -0.5)
                nc.vector.memset(eps[:], EPS)
                for i in range(NB1):
                    dve.wait_ge(w_hi_made, i + 1)
                    c = slice(i * CB, (i + 1) * CB)
                    nc.vector.tensor_tensor(w1_lo[:, :, c], raw[i % 2][:], w1_hi[:, :, c].bitcast(F32),
                                            ALU.subtract).then_inc(w_lo_made, 1)
                for i in range(2):
                    dve.wait_ge(w_hi_made, NB1 + i + 1)
                    c = slice(i * (FT // 2), (i + 1) * (FT // 2))
                    nc.vector.tensor_tensor(w2_lo[:, c, :], w2_raw[i][:], w2_hi[:, c, :].bitcast(F32), ALU.subtract)

            @block.gpsimd
            def _(pool):
                make_identity(nc, pool, identf, ident_step)

        spacer = sb("spacer3", [P, 1])
        xt = [sb(f"xt{i}", [P, D]) for i in range(TT)]
        xb = [sb(f"xb{i}", [P, D]) for i in range(TT)]
        yt = [sb(f"yt{i}", [P, D]) for i in range(2)]
        h = [sb(f"h3_{i}", [P, D + 64]) for i in range(2)]
        centred = [sb(f"centred3_{i}", [P, D]) for i in range(2)]
        stats = [sb(f"stats3_{i}", [P, 6]) for i in range(TT)]
        mv = [sb(f"mv3_{i}", [P, 2]) for i in range(TT)]
        var_eps = [sb(f"var_eps3_{i}", [P, 1]) for i in range(TT)]
        rstd = [sb(f"rstd3_{i}", [P, 1]) for i in range(TT)]
        t_hi = sb("t3_hi", [P, 3, TT * P], F32R)
        t_lo = sb("t3_lo", [P, 2, TT * P], F32R)
        gelu = [sb(f"gelu{i}", [P, W]) for i in range(2)]
        hidden = [sb(f"hidden{i}", [P, W]) for i in range(2)]
        hid_hi, hid_lo = sb("hid_hi", [P, FT, TT * P], F32R), sb("hid_lo", [P, FT, TT * P], F32R)

        turn = [ctx.enter_context(nc.psum_tensor(f"turn{i}", [P, 512], F32)) for i in range(2)]
        ps_a = [ctx.enter_context(nc.psum_tensor(f"ps_a{i}", [P, 512], F32)) for i in range(2)]
        ps_g = [ctx.enter_context(nc.psum_tensor(f"ps_g{i}", [P, 512], F32)) for i in range(2)]
        ps_y = [ctx.enter_context(nc.psum_tensor(f"ps_y{i}", [P, 512], F32)) for i in range(2)]

        PER, START = {}, {}

        def sem(name, per, first=0):
            s = ctx.enter_context(nc.semaphore(name))
            PER[s], START[s] = per, first
            return s

        def start(eng, *sems):
            for s in sems:
                eng.sem_inc(s, START[s])

        def at(t, s, n):
            assert n > 0 or START[s] > 0, s
            return t * PER[s] + (START[s] + n)

        NU = 2 * FT
        xt_landed = [sem(f"xt_landed{i}", 16) for i in range(TT)]
        y_stored = [sem(f"y_stored{i}", 16 * [3, 2][i], 16) for i in range(2)]
        stats_made, h_made, lo_made, hidden_made, y_made = (
            sem("stats3_made", TT), sem("h3_made", TT), sem("lo3_made", TT, 1), sem("hidden_made", NU, 1), sem("y_made", TT, 1))
        rstd_made, xb_made, hid_lo_made = sem("rstd3_made", TT), sem("xb_made", TT), sem("hid_lo_made", NU, 1)
        hi_made, gelu_made, hid_hi_made = sem("hi3_made", TT), sem("gelu_made", NU), sem("hid_hi_made", NU)
        turned, g_ready, a_ready, y_ready = sem("turned", TT, 1), sem("g_ready", NU), sem("a_ready", NU), sem("y_ready", TT)
        dve_step, pool_step = sem("dve3_step", FV_STEPS), sem("pool3_step", FP_STEPS)

        x2_tiles = x2.rearrange("(t i p) d -> t i p d", i=TT, p=P)
        out_tiles = out.rearrange("(t i p) d -> t i p d", i=TT, p=P)
        block = ctx.enter_context(nc.Block())

        @block.sync
        def _(sp):
            def load(t, i):
                sp.dma_start(xt[i][:], x2_tiles[t, i]).then_inc(xt_landed[i], 16)

            def store(t, i):
                sp.wait_ge(y_made, at(t, y_made, i + 1))
                sp.dma_start(out_tiles[t, i], yt[i % 2][:]).then_inc(y_stored[i % 2], 16)

            start(sp, *y_stored)
            for i in range(TT):
                load(0, i)
            with sp.Fori(0, NF - 1) as t:
                for i in range(TT):
                    sp.wait_ge(h_made, at(t, h_made, i + 1))
                    sp.wait_ge(xb_made, at(t, xb_made, i + 1))
                    load(t + 1, i)
                for i in range(TT):
                    store(t, i)
            for i in range(TT):
                store(NF - 1, i)
            for i in range(2):
                sp.wait_ge(y_stored[i], at(NF - 1, y_stored[i], PER[y_stored[i]]))

        @block.tensor
        def _(pe):
            start(pe, turned)
            with pe.Fori(0, NF) as t:
                for i in range(TT):
                    pe.wait_ge(lo_made, at(t, lo_made, max(i - 1, 0)))
                    pe.wait_ge(h_made, at(t, h_made, i + 1))
                    for k in range(3):
                        mm = pe.transpose(turn[i % 2][:, k * P:(k + 1) * P], h[i % 2][:, k * P:(k + 1) * P], identf[:])
                    mm.then_inc(turned, 1)
                for half in range(2):
                    for f in range(FT):
                        n = half * FT + f
                        c = slice(half * W, (half + 1) * W)
                        pe.wait_ge(lo_made, at(t, lo_made, [3, TT][half]))
                        for bank, f0, ready in ((ps_g[n % 2], FT + f, g_ready), (ps_a[n % 2], f, a_ready)):
                            pe.wait_ge(hidden_made, at(t, hidden_made, max(n - 1, 0)))
                            w = slice(f0 * P, (f0 + 1) * P)
                            passes = [(w1_hi[:, 0, w], t_hi[:, 0, c]), (w1_lo[:, 0, w], t_hi[:, 0, c]),
                                      (w1_hi[:, 1, w], t_hi[:, 1, c]), (w1_lo[:, 1, w], t_hi[:, 1, c]),
                                      (w1_hi[:, 0, w], t_lo[:, 0, c]), (w1_hi[:, 1, w], t_lo[:, 1, c]),
                                      (w1_hi[:, 2, w], t_hi[:, 2, c]), (w1_lo[:, 2, w], t_hi[:, 2, c])]
                            for k, (a, b) in enumerate(passes):
                                mm = pe.matmul(bank[:, 0:W], a, b, start=(k == 0), stop=(k == len(passes) - 1))
                            mm.then_inc(ready, 1)
                for i in range(TT):
                    pe.wait_ge(y_made, at(t, y_made, max(i - 1, 0)))
                    pe.wait_ge(hid_hi_made, at(t, hid_hi_made, FT if i < 2 else NU))
                    pe.wait_ge(hid_lo_made, at(t, hid_lo_made, FT if i < 2 else NU))
                    y, c = ps_y[i % 2][:, 0:D], slice(i * P, (i + 1) * P)
                    for f in range(FT):
                        pe.matmul(y, hid_hi[:, f, c], w2_hi[:, f, :], start=(f == 0), stop=False)
                        pe.matmul(y, hid_hi[:, f, c], w2_lo[:, f, :], start=False, stop=False)
                        mm = pe.matmul(y, hid_lo[:, f, c], w2_hi[:, f, :], start=False, stop=(f == FT - 1))
                    mm.then_inc(y_ready, 1)

        @block.vector
        def _(dve):
            step = [0]

            def link(t, ins):
                step[0] += 1
                ins.then_inc(dve_step, 1)
                dve.wait_ge(dve_step, at(t, dve_step, step[0]))

            def split_low(t, i):
                dve.wait_ge(hi_made, at(t, hi_made, i + 1))
                c = slice(i * P, (i + 1) * P)
                v = turn[i % 2][:, 0:3 * P].rearrange("p (k n) -> p k n", k=3)
                nc.vector.tensor_tensor(t_hi[64:P, 2, c], v[64:P, 2, :], t_hi[64:P, 2, c].bitcast(F32), ALU.subtract)
                nc.vector.tensor_tensor(t_lo[:, :, c], v[:, 0:2, :], t_hi[:, 0:2, c].bitcast(F32),
                                        ALU.subtract).then_inc(lo_made, 1)

            start(dve, lo_made, hidden_made, y_made)
            with dve.Fori(0, NF) as t:
                for i in range(TT):
                    dve.wait_ge(xt_landed[i], at(t, xt_landed[i], 16))
                    link(t, nc.vector.bn_stats(stats[i][:], xt[i][:]))
                    nc.vector.memset(spacer[0:1, :], 0.0)
                    nc.vector.bn_aggr(mv[i][:], stats[i][:]).then_inc(stats_made, 1)
                for i in range(TT):
                    hb = h[i % 2]
                    dve.wait_ge(turned, at(t, turned, max(i - 1, 0)))
                    dve.wait_ge(stats_made, at(t, stats_made, i + 1))
                    link(t, nc.vector.scalar_tensor_tensor(out=centred[i % 2][:], in0=xt[i][:], scalar=mv[i][:, 0:1],
                                                           in1=vec["g"][:], op0=ALU.subtract, op1=ALU.mult))
                    dve.wait_ge(rstd_made, at(t, rstd_made, i + 1))
                    nc.vector.scalar_tensor_tensor(out=hb[:, D:D + 64], in0=centred[i % 2][:, 2 * P:D], scalar=rstd[i][:],
                                                   in1=vec["b"][:, 2 * P:D], op0=ALU.mult, op1=ALU.add)
                    nc.vector.scalar_tensor_tensor(out=hb[:, 0:D], in0=centred[i % 2][:], scalar=rstd[i][:],
                                                   in1=vec["b"][:], op0=ALU.mult, op1=ALU.add).then_inc(h_made, 1)
                    if i:
                        split_low(t, i - 1)
                split_low(t, TT - 1)
                for n in range(NU):
                    dve.wait_ge(a_ready, at(t, a_ready, n + 1))
                    dve.wait_ge(gelu_made, at(t, gelu_made, n + 1))
                    dve.wait_ge(hid_lo_made, at(t, hid_lo_made, max(n - 1, 0)))
                    nc.vector.scalar_tensor_tensor(out=hidden[n % 2][:], in0=ps_a[n % 2][:, 0:W],
                                                   scalar=b1[:, n % FT:n % FT + 1], in1=gelu[n % 2][:],
                                                   op0=ALU.add, op1=ALU.mult).then_inc(hidden_made, 1)
                for i in range(TT):
                    dve.wait_ge(y_ready, at(t, y_ready, i + 1))
                    dve.wait_ge(xb_made, at(t, xb_made, i + 1))
                    dve.wait_ge(y_stored[i % 2], at(t, y_stored[i % 2], 16 * (i // 2)))
                    nc.vector.tensor_tensor(yt[i % 2][:], ps_y[i % 2][:, 0:D], xb[i][:], ALU.add)\
                        .then_inc(y_made, 1)
            assert step[0] == FV_STEPS, step[0]

        @block.scalar
        def _(act):
            def features(n):
                half, f = n // FT, n % FT
                return f, slice(half * W, (half + 1) * W)

            def split_high(t, n):
                f, c = features(n)
                act.wait_ge(hidden_made, at(t, hidden_made, n + 1))
                nc.scalar.copy(hid_hi[:, f, c], hidden[n % 2][:]).then_inc(hid_hi_made, 1)

            with act.Fori(0, NF) as t:
                for i in range(TT):
                    act.wait_ge(turned, at(t, turned, i + 1))
                    nc.scalar.copy(t_hi[:, :, i * P:(i + 1) * P],
                                   turn[i % 2][:, 0:3 * P].rearrange("p (k n) -> p k n", k=3)).then_inc(hi_made, 1)
                for n in range(NU):
                    act.wait_ge(g_ready, at(t, g_ready, n + 1))
                    act.wait_ge(hidden_made, at(t, hidden_made, max(n - 1, 0)))
                    f = n % FT
                    nc.scalar.activation(gelu[n % 2][:], ps_g[n % 2][:, 0:W], ACT.Gelu,
                                         bias=b1[:, FT + f:FT + f + 1]).then_inc(gelu_made, 1)
                    if n:
                        split_high(t, n - 1)
                split_high(t, NU - 1)

        @block.gpsimd
        def _(pool):
            step = [0]

            def link(t, ins):
                step[0] += 1
                ins.then_inc(pool_step, 1)
                pool.wait_ge(pool_step, at(t, pool_step, step[0]))

            start(pool, hid_lo_made)
            with pool.Fori(0, NF) as t:
                for i in range(TT):
                    pool.wait_ge(stats_made, at(t, stats_made, i + 1))
                    link(t, nc.gpsimd.tensor_tensor(var_eps[i][:], mv[i][:, 1:2], eps[:], ALU.add))
                    nc.gpsimd.tensor_tensor(rstd[i][:], var_eps[i][:], neg_half[:], ALU.pow).then_inc(rstd_made, 1)
                pool.wait_ge(y_made, at(t, y_made, 0))
                for i in range(TT):
                    pool.wait_ge(xt_landed[i], at(t, xt_landed[i], 16))
                    nc.gpsimd.tensor_tensor(xb[i][:], xt[i][:], vec["ff_b2"][:], ALU.add).then_inc(xb_made, 1)
                for n in range(NU):
                    half, f = n // FT, n % FT
                    c = slice(half * W, (half + 1) * W)
                    pool.wait_ge(hid_hi_made, at(t, hid_hi_made, n + 1))
                    nc.gpsimd.tensor_tensor(hid_lo[:, f, c], hidden[n % 2][:], hid_hi[:, f, c].bitcast(F32),
                                            ALU.subtract).then_inc(hid_lo_made, 1)
            assert step[0] == FP_STEPS, step[0]


_P = "L0_xattn_"
_WEIGHTS = ["n1_g", "n1_b", "q1", "k1", "v1", "o1_w", "o1_b", "n2_g", "n2_b", "q2", "k2", "v2", "o2_w", "o2_b",
            "n3_g", "n3_b", "ff_w1", "ff_b1", "ff_w2", "ff_b2"]


def kernel(**inputs):
    import numpy as np
    import concourse.bacc as bacc
    from concourse.bass_utils import run_bass_kernel_spmd

    arrays = {"x": np.ascontiguousarray(inputs["x"]),
              "ctxT": np.ascontiguousarray(np.transpose(inputs["ctx_768"], (0, 2, 1)))}
    for name in _WEIGHTS:
        arrays[name] = np.ascontiguousarray(inputs[_P + name])
    nc = bacc.Bacc("TRN2", target_bir_lowering=False, num_devices=1)
    args = [nc.dram_tensor(f"in_{name}", a.shape, mybir.dt.from_np(a.dtype), kind="ExternalInput").ap()
            for name, a in arrays.items()]
    out = nc.dram_tensor("out_0", (B, N, D), F32, kind="ExternalOutput").ap()
    build(nc, *args, out)
    r = run_bass_kernel_spmd(nc, [{f"in_{name}": a for name, a in arrays.items()}], core_ids=[0])
    return r.results[0]["out_0"]
```

```python
from contextlib import ExitStack

import concourse.bass as bass
from concourse import mybir

F32 = mybir.dt.float32
F32R = mybir.dt.float32r
BF16 = mybir.dt.bfloat16
ALU = mybir.AluOpType
ACT = mybir.ActivationFunctionType
AX_X = mybir.AxisListType.X

B, N, D = 32, 100, 320
H, DH = 20, 16
J, C = 361, 192
FF = 1280
EPS = 1e-5
SCALE = DH ** -0.5
P = 128
U = 2
NT = B // U
SL = 6
KS = SL * DH
KM = KS + 3
JT = [(0, 120), (120, 120), (240, 121)]
JP = 362
G, HG = 4, 5
DVE_STEPS = {"first": 6, "body": 16, "last": 10}
POOL_STEPS = {"first": 18, "body": 44, "last": 26}
HB = 10
D1 = DH + 1
QH = 4
HC = H // QH
XB = [(0, 3), (3, HC)]



STEPS = {"first": [(None, 0)], "body": [(0, 1), (1, 0)], "last": [(0, 1), (1, None)]}
NW = 3
NPT = 6
OF_CROSS = ("m2t", "o2x", "o2t", "o2")


def work_jobs(x, s):
    order = [("kc", 0), ("vc", 0), ("h1", 0), ("kc", 1), ("vc", 1), ("q1", 0), ("k1", 0), ("v1", 0),
             ("kc", 2), ("vc", 2), ("q1t", 0), ("q1t", 1), ("k1t", 0), ("k1t", 1), ("kct", 0), ("kct", 1),
             ("m1t", 0), ("m1t", 1), ("m2t", 0), ("m2t", 1), ("kct", 2), ("kct", 3), ("o1x", 0), ("o1x", 1),
             ("kct", 4), ("o1t", 0), ("kct", 5), ("o1", 0), ("kct", 6), ("h2", 0), ("kct", 7), ("q2", 0),
             ("kct", 8), ("o2x", 0), ("o2x", 1), ("kct", 9), ("o2t", 0), ("q2t", 0), ("q2t", 1), ("o2", 0)]
    whose = {kind: x if kind in OF_CROSS else s for kind, _ in order}
    return [(kind, whose[kind], i) for kind, i in order if whose[kind] is not None]


def score_jobs(x, s):
    cross = [] if x is None else [(2, x, hd) for hd in range(H)]
    own = [] if s is None else [(1, s, g) for g in range(G)]
    return cross[:16] + own[:2] + cross[16:17] + own[2:] + cross[17:]


def exp_jobs(x, s):
    return ([] if s is None else [(1, s, g, 0) for g in range(G)]) + \
        ([] if x is None else [(2, x, g, j) for g in range(G) for j in range(3)])


def pv_jobs(x, s):
    return ([] if s is None else [(1, s, g) for g in range(G)]) + ([] if x is None else [(2, x, g) for g in range(G)])


class Plan:

    def __init__(self, name):
        def over(jobs):
            return [job for x, s in STEPS[name] for job in jobs(x, s)]

        self.name = name
        self.work, self.score, self.exp, self.pv = over(work_jobs), over(score_jobs), over(exp_jobs), over(pv_jobs)
        self.work_at = {job: (i % NW, i // NW) for i, job in enumerate(self.work)}
        self.score_at = {job: (i % 2, i // 2) for i, job in enumerate(self.score)}
        self.exp_at = {job: i for i, job in enumerate(self.exp)}

    def on_work(self, k):
        return sum(1 for b, _ in self.work_at.values() if b == k)

    def ahead(self, of_self, u):
        return int(self.name == "body" and of_self and u == 0)

    def pv_before(self, job):
        i = self.exp_at[job] - NPT
        return self.pv.index(self.exp[i][:3]) + 1 if i >= 0 else 0


FIRST, BODY, LAST = Plan("first"), Plan("body"), Plan("last")


class When:

    def __init__(self, plan, t, ahead=0):
        self.plan, self.t, self.ahead = plan, t, ahead


def moments(plan, t):
    return [(When(plan, t), x, When(plan, t, plan.ahead(True, s)), s) for x, s in STEPS[plan.name]]


def rows3(w):
    return [(0, P, 0, w[0:P]), (0, P, 1, w[P:2 * P]), (0, 64, 2, w[2 * P:D]), (64, P, 2, w[2 * P:D])]


def rows2(w):
    return [(0, P, 0, w[0:P]), (0, 64, 1, w[P:C]), (64, P, 1, w[P:C])]


def build(nc, x, ctxT, n1_g, n1_b, q1, k1, v1, o1_w, o1_b, n2_g, n2_b, q2, k2, v2, o2_w, o2_b,
          n3_g, n3_b, ff_w1, ff_b1, ff_w2, ff_b2, out):
    x2_dram = nc.dram_tensor("x2_dram", [B * N, D], F32).ap()
    attention_phase(nc, x, ctxT, n1_g, n1_b, (q1, k1, v1), o1_w, o1_b, n2_g, n2_b, q2, k2, v2, o2_w, o2_b,
                    x2_dram.rearrange("(b n) d -> b n d", n=N))
    feed_forward_phase(nc, x2_dram, n3_g, n3_b, ff_w1, ff_b1, ff_w2, ff_b2, out.rearrange("b n d -> (b n) d"))


def attention_phase(nc, x, ctxT, n1_g, n1_b, qkv1, o1_w, o1_b, n2_g, n2_b, q2, k2, v2, o2_w, o2_b, x2_dram):
    with ExitStack() as ctx:
        def sb(name, shape, dt=F32):
            return ctx.enter_context(nc.sbuf_tensor(name, shape, dt))

        names = {"q1": (qkv1[0], 3), "k1": (qkv1[1], 3), "v1": (qkv1[2], 3), "kc": (k2, 2), "vc": (v2, 2),
                 "o1": (o1_w, 3), "q2": (q2, 3), "o2": (o2_w, 3)}
        whi = {k: sb(f"w_{k}_hi", [P, kt, D], F32R) for k, (_, kt) in names.items()}
        wlo = {k: sb(f"w_{k}_lo", [P, kt, D], F32R) for k, (_, kt) in names.items()}
        vectors = {"n1_g": n1_g, "n1_b": n1_b, "n2_g": n2_g, "n2_b": n2_b, "o1_b": o1_b, "o2_b": o2_b}
        vec = {k: sb(f"{k}_rows", [N, D]) for k in vectors}
        identf = sb("identf", [P, P])
        identb = sb("identb", [P, P], BF16)
        neg_half, eps, one = sb("neg_half", [P, 1]), sb("eps", [P, 1]), sb("one", [P, 1])

        with ExitStack() as prep:
            raw = {k: prep.enter_context(nc.sbuf_tensor(f"w_{k}_raw", [P, kt, D], F32))
                   for k, (_, kt) in names.items()}
            weight_landed = {k: prep.enter_context(nc.semaphore(f"w_{k}_landed")) for k in names}
            vectors_landed = prep.enter_context(nc.semaphore("vectors_landed"))
            whi_made = prep.enter_context(nc.semaphore("whi_made"))
            ident_step = prep.enter_context(nc.semaphore("ident_step"))
            block = prep.enter_context(nc.Block())

            @block.sync
            def _(sp):
                for k, (w, kt) in names.items():
                    for p0, p1, tile, src in (rows3(w) if kt == 3 else rows2(w)):
                        sp.dma_start(raw[k][p0:p1, tile, :], src).then_inc(weight_landed[k], 16)
                for k, v in vectors.items():
                    src = v.rearrange("(a d) -> a d", a=1).broadcast_to([N, D])
                    sp.dma_start(vec[k][:], src).then_inc(vectors_landed, 16)
                sp.wait_ge(vectors_landed, 16 * len(vectors))

            @block.scalar
            def _(act):
                for k, (_, kt) in names.items():
                    act.wait_ge(weight_landed[k], 16 * (kt + 1))
                    nc.scalar.copy(whi[k][:], raw[k][:]).then_inc(whi_made, 1)

            @block.vector
            def _(dve):
                nc.vector.memset(neg_half[:], -0.5)
                nc.vector.memset(eps[:], EPS)
                nc.vector.memset(one[:], 1.0)
                for i, k in enumerate(names):
                    dve.wait_ge(whi_made, i + 1)
                    nc.vector.tensor_tensor(wlo[k][:], raw[k][:], whi[k][:].bitcast(F32), ALU.subtract)

            @block.gpsimd
            def _(pool):
                make_identity(nc, pool, identf, ident_step)
                pool.wait_ge(ident_step, 2)
                nc.gpsimd.tensor_copy(identb[:], identf[:])

        def two(name, shape, dt=F32):
            return [sb(f"{name}{u}", shape, dt) for u in range(U)]

        spacer = sb("spacer", [P, 1])
        xin = two("xin", [N, D])
        x1 = two("x1", [N, D])
        x2 = two("x2", [N, D])
        xres = two("xres", [N, D])
        h = two("h", [N, D + 64])
        centred = two("centred", [N, D])
        stats = two("stats", [N, 6])
        mv = two("mv", [N, 2])
        var_eps = two("var_eps", [N, 1])
        rstd = two("rstd", [N, 1])
        t_hi = two("t_hi", [P, 3, N], F32R)
        t_lo = two("t_lo", [P, 2, N], F32R)
        stack_q = two("stack_q", [N, H, SL, DH], BF16)
        stack_k = two("stack_k", [N, H, SL, DH], BF16)
        rest_q = two("rest_q", [N, D])
        rest_k = two("rest_k", [N, D])
        stack_c = [sb(f"stack_c{i}", [n, H, SL, DH], BF16) for i, (_, n) in enumerate(JT)]
        rest_c = [sb(f"rest_c{i}", [n, D]) for i, (_, n) in enumerate(JT)]
        qT = two("qT", [KM, H, N], BF16)
        kT = two("kT", [KM, H, N], BF16)
        kcT = two("kcT", [KM, H, JP], BF16)
        vs = two("vs", [N, H, D1])
        vc = two("vc", [JT[2][1], 3, H, D1])
        ctx_raw = two("ctx_raw", [P, 2, J])
        ctx_hi = sb("ctx_hi", [P, 2, J], F32R)
        ctx_lo = sb("ctx_lo", [P, J], F32R)
        neg_max = two("neg_max", [N, H])
        max_rest = two("max_rest", [N, H])
        max_parts = two("max_parts", [N, H, 4], BF16)
        probs = [sb(f"probs{i}", [JT[2][1], HG * N]) for i in range(NPT)]
        rden = two("rden", [N, H])
        pv = two("pv", [P, HC * N])

        work = [ctx.enter_context(nc.psum_tensor(f"work{i}", [P, 512], F32)) for i in range(NW)]
        score = [ctx.enter_context(nc.psum_tensor(f"score{i}", [P, 512], F32)) for i in range(2)]
        expin = [ctx.enter_context(nc.psum_tensor(f"expin{i}", [P, 512], F32)) for i in range(2)]
        attn = ctx.enter_context(nc.psum_tensor("attn", [P, 512], F32))

        PER, START, BEFORE = {}, {}, {}

        def sem(name, per, first=0):
            s = ctx.enter_context(nc.semaphore(name))
            PER[s], START[s] = per, first
            return s

        def shared(name, count):
            s = sem(name, count(BODY), 1)
            BEFORE[s] = count(FIRST)
            return s

        def start(eng, *sems):
            for s in sems:
                eng.sem_inc(s, START[s])

        def sem2(name, per, first=0):
            return [sem(f"{name}{u}", per, first) for u in range(U)]

        x_landed, ctx_landed, x2_stored = sem2("x_landed", 16), sem2("ctx_landed", 48), sem2("x2_stored", 16, 16)
        ones_set = sem("ones_set", 0)
        stats_made = sem2("stats_made", 2)
        h_made = sem2("h_made", 2)
        lo_made = sem2("lo_made", 4, 4)
        rest_q_made, rest_k_made, rest_c_made = sem2("rest_q_made", 2, 2), sem2("rest_k_made", 1, 1), sem2("rest_c_made", 3, 3)
        qT_made = sem2("qT_made", 4, 4)
        max_made = sem2("max_made", G + H, G + H)
        mT_made = sem2("mT_made", 4, 4)
        o_normed = sem2("o_normed", 4, 4)
        x1_made, x2_made = sem2("x1_made", 1, 1), sem2("x2_made", 1, 1)
        rstd_made = sem2("rstd_made", 2)
        xres_made = sem2("xres_made", 2)
        ctx_split = sem2("ctx_split", 1)
        stack_q_made, stack_k_made, stack_c_made = sem2("stack_q_made", 2), sem2("stack_k_made", 1), sem2("stack_c_made", 3)
        parts_made = sem2("parts_made", 4)
        hi_made = sem2("hi_made", 4)
        p0_q_made, p0_k_made, p0_c_made = sem2("p0_q_made", 2), sem2("p0_k_made", 1), sem2("p0_c_made", 3)
        pv_copied = sem2("pv_copied", 2, 2)
        v_made, vc_made = sem2("v_made", 1, 1), sem2("vc_made", 3, 3)
        kT_made = sem2("kT_made", 2, 2)
        kcT_made = sem2("kcT_made", H // 2, H // 2)
        probs_made = shared("probs_made", lambda plan: len(plan.exp))
        work_ready = [shared(f"work_ready{k}", lambda plan: plan.on_work(k)) for k in range(NW)]
        score_ready = [shared(f"score_ready{k}", lambda plan: len(plan.score) // 2) for k in range(2)]
        exp_ready = [shared(f"exp_ready{k}", lambda plan: len(plan.exp) // 2) for k in range(2)]
        pv_made = shared("pv_made", lambda plan: len(plan.pv))
        dve_step = shared("dve_step", lambda plan: DVE_STEPS[plan.name])
        pool_step = shared("pool_step", lambda plan: POOL_STEPS[plan.name])

        def at(w, s, n):
            if s not in BEFORE:
                return w.t * PER[s] + (w.ahead * PER[s] + START[s] + n)
            if w.plan is FIRST:
                return START[s] + n
            return w.t * PER[s] + (START[s] + BEFORE[s] + n)

        def emptied(w, job, back=0):
            kind, u, i = job
            s, n = {
                "h1": (lo_made[u], 1), "o1t": (lo_made[u], 2), "h2": (lo_made[u], 3), "o2t": (lo_made[u], 4),
                "q1": (rest_q_made[u], 1), "q2": (rest_q_made[u], 2), "k1": (rest_k_made[u], 1),
                "v1": (v_made[u], 1), "kc": (rest_c_made[u], i + 1), "vc": (vc_made[u], i + 1),
                "q1t": (qT_made[u], i + 1), "q2t": (qT_made[u], i + 3), "k1t": (kT_made[u], i + 1),
                "kct": (kcT_made[u], i + 1), "m1t": (mT_made[u], i + 1), "m2t": (mT_made[u], i + 3),
                "o1x": (o_normed[u], i + 1), "o2x": (o_normed[u], i + 3),
                "o1": (x1_made[u], 1), "o2": (x2_made[u], 1),
            }[kind]
            plan = BODY if back else w.plan
            return s, at(When(w.plan, w.t, plan.ahead(kind not in OF_CROSS, u) - back), s, n)

        def wbank(w, job):
            return work[w.plan.work_at[job][0]]

        def wbank16(w, job):
            return wbank(w, job)[:, :].bitcast(BF16)

        def filled(w, job):
            k, n = w.plan.work_at[job]
            return work_ready[k], at(w, work_ready[k], n + 1)

        def q_slots(stack, part):
            return {0: stack[:, :, 0:4:3, :], 1: stack[:, :, 1:5:3, :], 2: stack[:, :, 2, :],
                    "last": stack[:, :, 5, :]}[part]

        def k_slots(stack, part):
            return {0: stack[:, :, 0:3, :], 1: stack[:, :, 3:5, :], 2: stack[:, :, 5, :]}[part]

        def heads(ap):
            return ap.rearrange("p (h d) -> p h d", d=DH)

        def repeated(ap, n, k):
            return heads(ap).unsqueeze(2).broadcast_to([n, H, k, DH])

        block = ctx.enter_context(nc.Block())

        @block.sync
        def _(sp):
            def load(b, u):
                sp.dma_start(xin[u][:], x[b]).then_inc(x_landed[u], 16)

            def load_context(b, u):
                c = ctxT[b]
                sp.dma_start(ctx_raw[u][0:P, 0, :], c[0:P]).then_inc(ctx_landed[u], 16)
                sp.dma_start(ctx_raw[u][0:64, 1, :], c[P:C]).then_inc(ctx_landed[u], 16)
                sp.dma_start(ctx_raw[u][64:P, 1, :], c[P:C]).then_inc(ctx_landed[u], 16)

            start(sp, *x2_stored)
            for u in range(U):
                load_context(u, u)
                load(u, u)
            with sp.Fori(0, NT - 1) as t:
                now = When(BODY, t)
                for u in range(U):
                    sp.wait_ge(ctx_split[u], at(now, ctx_split[u], 1))
                    load_context(t * U + (U + u), u)
                    sp.wait_ge(xres_made[u], at(now, xres_made[u], 1))
                    sp.wait_ge(h_made[u], at(now, h_made[u], 1))
                    load(t * U + (U + u), u)
                for u in range(U):
                    sp.wait_ge(x2_made[u], at(now, x2_made[u], 1))
                    sp.dma_start(x2_dram[t * U + u], x2[u][:]).then_inc(x2_stored[u], 16)
            now = When(LAST, NT - 1)
            for u in range(U):
                sp.wait_ge(x2_made[u], at(now, x2_made[u], 1))
                sp.dma_start(x2_dram[B - U + u], x2[u][:]).then_inc(x2_stored[u], 16)
            for u in range(U):
                sp.wait_ge(x2_stored[u], at(now, x2_stored[u], 16))

        @block.tensor
        def _(pe):
            filling = [0]

            def fill(w, job):
                assert w.plan.work[filling[0]] == job, (w.plan.work[filling[0]], job)
                filling[0] = (filling[0] + 1) % len(w.plan.work)
                k, n = w.plan.work_at[job]
                if n:
                    pe.wait_ge(*emptied(w, w.plan.work[(n - 1) * NW + k]))
                elif w.plan is not FIRST:
                    pe.wait_ge(*emptied(w, BODY.work[(BODY.on_work(k) - 1) * NW + k], back=1))

            def done(w, ins, job):
                ins.then_inc(work_ready[w.plan.work_at[job][0]], 1)

            def transpose_features(w, job, u):
                fill(w, job)
                for k in range(3):
                    mm = pe.transpose(wbank(w, job)[:, k * N:(k + 1) * N], h[u][:, k * P:(k + 1) * P], identf[0:N, 0:N])
                done(w, mm, job)

            def project(w, job, u, weight, n):
                fill(w, job)
                dst, a, b = wbank(w, job)[0:N, 0:D], t_hi[u], t_lo[u]
                pe.wait_ge(hi_made[u], at(w, hi_made[u], n))
                pe.matmul(dst, a[:, 0, :], whi[weight][:, 0, :], start=True, stop=False)
                pe.matmul(dst, a[:, 0, :], wlo[weight][:, 0, :], start=False, stop=False)
                pe.matmul(dst, a[:, 1, :], whi[weight][:, 1, :], start=False, stop=False)
                pe.matmul(dst, a[:, 1, :], wlo[weight][:, 1, :], start=False, stop=False)
                pe.wait_ge(lo_made[u], at(w, lo_made[u], n))
                pe.matmul(dst, b[:, 0, :], whi[weight][:, 0, :], start=False, stop=False)
                pe.matmul(dst, b[:, 1, :], whi[weight][:, 1, :], start=False, stop=False)
                pe.matmul(dst, a[:, 2, :], whi[weight][:, 2, :], start=False, stop=False)
                done(w, pe.matmul(dst, a[:, 2, :], wlo[weight][:, 2, :], start=False, stop=True), job)

            def project_context(w, u, i):
                pe.wait_ge(ctx_split[u], at(w, ctx_split[u], 1))
                j0, n = JT[i]
                hi0, lo0, last = ctx_hi[:, 0, j0:j0 + n], ctx_lo[:, j0:j0 + n], ctx_hi[:, 1, j0:j0 + n]
                for weight in ("kc", "vc"):
                    job = (weight, u, i)
                    fill(w, job)
                    dst = wbank(w, job)[0:n, 0:D]
                    pe.matmul(dst, hi0, whi[weight][:, 0, :], start=True, stop=False)
                    pe.matmul(dst, hi0, wlo[weight][:, 0, :], start=False, stop=False)
                    pe.matmul(dst, lo0, whi[weight][:, 0, :], start=False, stop=False)
                    pe.matmul(dst, last, whi[weight][:, 1, :], start=False, stop=False)
                    done(w, pe.matmul(dst, last, wlo[weight][:, 1, :], start=False, stop=True), job)

            def transpose_stack(w, kind, u, stack):
                for i in range(2):
                    job = (kind, u, i)
                    fill(w, job)
                    for k in range(HB):
                        src = stack[:, i * HB + k].rearrange("p s d -> p (s d)")
                        mm = pe.transpose(wbank16(w, job)[0:KS, k * N:(k + 1) * N], src, identb[0:N, 0:N])
                    done(w, mm, job)

            def transpose_context_stack(w, u, i):
                job = ("kct", u, i)
                fill(w, job)
                for k in range(2):
                    for jt, (j0, n) in enumerate(JT):
                        src = stack_c[jt][:, 2 * i + k].rearrange("p s d -> p (s d)")
                        mm = pe.transpose(wbank16(w, job)[0:KS, k * JP + j0:k * JP + j0 + n], src, identb[0:n, 0:n])
                done(w, mm, job)

            def score_bank(w, job):
                n, back, plan = w.plan.score.index(job) - 2, 0, w.plan
                if n < 0:
                    if plan is FIRST:
                        return
                    n, back, plan = n + len(BODY.score), 1, BODY
                a, u, i = plan.score[n]
                before = When(w.plan, w.t, plan.ahead(a == 1, u) - back)
                pe.wait_ge(max_made[u], at(before, max_made[u], (a - 1) * G + i + 1))

            def self_scores(w, u, g):
                k = w.plan.score_at[1, u, g][0]
                score_bank(w, (1, u, g))
                for i in range(HG):
                    hd = g * HG + i
                    mm = pe.matmul(score[k][0:N, i * N:(i + 1) * N], qT[u][0:KS, hd, :], kT[u][0:KS, hd, :],
                                   start=True, stop=True)
                mm.then_inc(score_ready[k], 1)

            def cross_scores(w, u, hd):
                k = w.plan.score_at[2, u, hd][0]
                score_bank(w, (2, u, hd))
                pe.wait_ge(kcT_made[u], at(w, kcT_made[u], hd // 2 + 1))
                pe.matmul(score[k][0:N, 0:J], qT[u][0:KS, hd, :], kcT[u][0:KS, hd, 0:J],
                          start=True, stop=True).then_inc(score_ready[k], 1)

            def transpose_max(w, a, u):
                for i in range(2):
                    job = (f"m{a}t", u, i)
                    fill(w, job)
                    pe.wait_ge(parts_made[u], at(w, parts_made[u], (a - 1) * 2 + i + 1))
                    for k in range(HB):
                        mm = pe.transpose(wbank16(w, job)[KS:KM, k * N:(k + 1) * N], max_parts[u][:, i * HB + k, 0:3],
                                          identb[0:N, 0:N])
                    done(w, mm, job)

            def scores_for_exp(w, a, u, g, jt):
                e = w.plan.exp_at[a, u, g, jt]
                pe.wait_ge(probs_made, at(w, probs_made, max(e - 1, 0)))
                pe.wait_ge(mT_made[u], at(w, mT_made[u], (a - 1) * 2 + (g * HG + HG - 1) // HB + 1))
                j0, n = JT[jt] if a == 2 else (0, N)
                keys = kcT if a == 2 else kT
                for i in range(HG):
                    hd = g * HG + i
                    mm = pe.matmul(expin[e % 2][0:n, i * N:(i + 1) * N], keys[u][:, hd, j0:j0 + n],
                                   qT[u][:, hd, :], start=True, stop=True)
                mm.then_inc(exp_ready[e % 2], 1)

            def times_v(w, a, u, g):
                if g == 0:
                    if a == 1:
                        pe.wait_ge(v_made[u], at(w, v_made[u], 1))
                    else:
                        pe.wait_ge(vc_made[u], at(w, vc_made[u], 3))
                tiles = range(3) if a == 2 else range(1)
                pe.wait_ge(probs_made, at(w, probs_made, w.plan.exp_at[a, u, g, tiles[-1]] + 1))
                for some in (range(QH), range(QH, HG)):
                    for jt in tiles:
                        for i in some:
                            hd = g * HG + i
                            n = JT[jt][1] if a == 2 else N
                            v = vc[u][0:n, jt, hd, :] if a == 2 else vs[u][:, hd, :]
                            p0, c0 = 32 * (hd % QH), N * (hd // QH)
                            mm = pe.matmul(attn[p0:p0 + D1, c0:c0 + N], v,
                                           probs[w.plan.exp_at[a, u, g, jt] % NPT][0:n, i * N:(i + 1) * N],
                                           start=(jt == 0), stop=(jt == tiles[-1]))
                mm.then_inc(pv_made, 1)

            def transpose_outputs(w, a, u):
                pe.wait_ge(pv_copied[u], at(w, pv_copied[u], a))
                for i, (c0, c1) in enumerate(XB):
                    job = (f"o{a}x", u, i)
                    fill(w, job)
                    for c in range(c0, c1):
                        mm = pe.transpose(wbank(w, job)[0:N, (c - c0) * P:(c - c0 + 1) * P], pv[u][:, c * N:(c + 1) * N],
                                          identf[:])
                    done(w, mm, job)

            def step(now, x, then, s):
                def cross(first, end):
                    for hd in range(first, end if x is not None else first):
                        cross_scores(now, x, hd)

                def context_stacks(first, end):
                    for i in range(first, end if s is not None else first):
                        pe.wait_ge(stack_c_made[s], at(then, stack_c_made[s], 3))
                        transpose_context_stack(then, s, i)

                if x is not None:
                    pe.wait_ge(qT_made[x], at(now, qT_made[x], 4))
                cross(0, 2)
                if s is not None:
                    project_context(then, s, 0)
                cross(2, 4)
                if s is not None:
                    pe.wait_ge(h_made[s], at(then, h_made[s], 1))
                    transpose_features(then, ("h1", s, 0), s)
                cross(4, 5)
                if s is not None:
                    project_context(then, s, 1)
                cross(5, 6)
                if s is not None:
                    project(then, ("q1", s, 0), s, "q1", 1)
                cross(6, 8)
                if s is not None:
                    project(then, ("k1", s, 0), s, "k1", 1)
                cross(8, 9)
                if s is not None:
                    project(then, ("v1", s, 0), s, "v1", 1)
                cross(9, 11)
                if s is not None:
                    project_context(then, s, 2)
                cross(11, 13)
                if s is not None:
                    pe.wait_ge(stack_q_made[s], at(then, stack_q_made[s], 1))
                    transpose_stack(then, "q1t", s, stack_q[s])
                cross(13, 15)
                if s is not None:
                    pe.wait_ge(stack_k_made[s], at(then, stack_k_made[s], 1))
                    transpose_stack(then, "k1t", s, stack_k[s])
                cross(15, 16)
                if s is not None:
                    pe.wait_ge(qT_made[s], at(then, qT_made[s], 2))
                    pe.wait_ge(kT_made[s], at(then, kT_made[s], 2))
                    self_scores(then, s, 0)
                    self_scores(then, s, 1)
                cross(16, 17)
                if s is not None:
                    self_scores(then, s, 2)
                    self_scores(then, s, 3)
                cross(17, 20)
                context_stacks(0, 2)
                if s is not None:
                    pe.wait_ge(pv_copied[s], at(then, pv_copied[s], 0))
                    transpose_max(then, 1, s)
                    scores_for_exp(then, 1, s, 0, 0)
                    scores_for_exp(then, 1, s, 1, 0)
                    times_v(then, 1, s, 0)
                    scores_for_exp(then, 1, s, 2, 0)
                    times_v(then, 1, s, 1)
                    scores_for_exp(then, 1, s, 3, 0)
                    times_v(then, 1, s, 2)
                if x is not None:
                    transpose_max(now, 2, x)
                    scores_for_exp(now, 2, x, 0, 0)
                if s is not None:
                    times_v(then, 1, s, 3)
                if x is not None:
                    scores_for_exp(now, 2, x, 0, 1)
                    scores_for_exp(now, 2, x, 0, 2)
                context_stacks(2, 4)
                if s is not None:
                    transpose_outputs(then, 1, s)
                if x is not None:
                    scores_for_exp(now, 2, x, 1, 0)
                    scores_for_exp(now, 2, x, 1, 1)
                context_stacks(4, 5)
                if s is not None:
                    pe.wait_ge(o_normed[s], at(then, o_normed[s], 2))
                    transpose_features(then, ("o1t", s, 0), s)
                if x is not None:
                    scores_for_exp(now, 2, x, 1, 2)
                    if s is not None:
                        pe.wait_ge(pv_copied[s], at(then, pv_copied[s], 1))
                    else:
                        pe.wait_ge(pv_copied[1 - x], at(now, pv_copied[1 - x], 2))
                    times_v(now, 2, x, 0)
                context_stacks(5, 6)
                if s is not None:
                    project(then, ("o1", s, 0), s, "o1", 2)
                if x is not None:
                    scores_for_exp(now, 2, x, 2, 0)
                    scores_for_exp(now, 2, x, 2, 1)
                context_stacks(6, 7)
                if x is not None:
                    scores_for_exp(now, 2, x, 2, 2)
                    times_v(now, 2, x, 1)
                if s is not None:
                    pe.wait_ge(h_made[s], at(then, h_made[s], 2))
                    transpose_features(then, ("h2", s, 0), s)
                if x is not None:
                    scores_for_exp(now, 2, x, 3, 0)
                    scores_for_exp(now, 2, x, 3, 1)
                context_stacks(7, 8)
                if s is not None:
                    project(then, ("q2", s, 0), s, "q2", 3)
                if x is not None:
                    scores_for_exp(now, 2, x, 3, 2)
                    times_v(now, 2, x, 2)
                    times_v(now, 2, x, 3)
                context_stacks(8, 9)
                if x is not None:
                    transpose_outputs(now, 2, x)
                context_stacks(9, 10)
                if x is not None:
                    pe.wait_ge(o_normed[x], at(now, o_normed[x], 4))
                    transpose_features(now, ("o2t", x, 0), x)
                if s is not None:
                    pe.wait_ge(stack_q_made[s], at(then, stack_q_made[s], 2))
                    transpose_stack(then, "q2t", s, stack_q[s])
                if x is not None:
                    project(now, ("o2", x, 0), x, "o2", 4)

            start(pe, *work_ready, *score_ready, *exp_ready, pv_made)
            pe.wait_ge(ones_set, 3 * U + 1)
            for m in moments(FIRST, 0):
                step(*m)
            for job in FIRST.work[-NW:]:
                pe.wait_ge(*emptied(When(FIRST, 0), job))
            with pe.Fori(0, NT - 1) as t:
                for m in moments(BODY, t):
                    step(*m)
            for m in moments(LAST, NT - 1):
                step(*m)

        @block.vector
        def _(dve):
            links = [0]

            def link(w, ins):
                links[0] += 1
                ins.then_inc(dve_step, 1)
                dve.wait_ge(dve_step, at(w, dve_step, links[0]))

            def centre(w, u, a, src):
                link(w, nc.vector.bn_stats(stats[u][:], src[:]))
                nc.vector.memset(spacer[0:1, :], 0.0)
                nc.vector.bn_aggr(mv[u][:], stats[u][:]).then_inc(stats_made[u], 1)
                dve.wait_ge(stats_made[u], at(w, stats_made[u], a))
                link(w, nc.vector.scalar_tensor_tensor(out=centred[u][:], in0=src[:], scalar=mv[u][:, 0:1],
                                                       in1=vec[f"n{a}_g"][:], op0=ALU.subtract, op1=ALU.mult))

            def normalise(w, u, a):
                b = vec[f"n{a}_b"]
                dve.wait_ge(rstd_made[u], at(w, rstd_made[u], a))
                nc.vector.scalar_tensor_tensor(out=h[u][:, D:D + 64], in0=centred[u][:, 2 * P:D], scalar=rstd[u][:],
                                               in1=b[:, 2 * P:D], op0=ALU.mult, op1=ALU.add)
                nc.vector.scalar_tensor_tensor(out=h[u][:, 0:D], in0=centred[u][:], scalar=rstd[u][:],
                                               in1=b[:], op0=ALU.mult, op1=ALU.add).then_inc(h_made[u], 1)

            def lows(w, job, u, n):
                dve.wait_ge(hi_made[u], at(w, hi_made[u], n))
                v = wbank(w, job)[:, 0:3 * N].rearrange("p (k n) -> p k n", k=3)
                nc.vector.tensor_tensor(t_hi[u][64:P, 2, :], v[64:P, 2, :], t_hi[u][64:P, 2, :].bitcast(F32),
                                        ALU.subtract)
                nc.vector.tensor_tensor(t_lo[u][:], v[:, 0:2, :], t_hi[u][:, 0:2, :].bitcast(F32),
                                        ALU.subtract).then_inc(lo_made[u], 1)

            def rest(w, job, n, first, dst, made):
                nc.vector.tensor_tensor(heads(dst[:]), heads(wbank(w, job)[0:n, 0:D]), first,
                                        ALU.subtract).then_inc(made, 1)

            def rest_q_of(w, kind, u, n):
                dve.wait_ge(p0_q_made[u], at(w, p0_q_made[u], n))
                rest(w, (kind, u, 0), N, stack_q[u][:, :, 0, :], rest_q[u], rest_q_made[u])

            def rest_c_of(w, u, i):
                dve.wait_ge(p0_c_made[u], at(w, p0_c_made[u], i + 1))
                rest(w, ("kc", u, i), JT[i][1], stack_c[i][:, :, 0, :], rest_c[i], rest_c_made[u])

            def copy_q(w, kind, u):
                for i in range(2):
                    job = (kind, u, i)
                    dve.wait_ge(*filled(w, job))
                    nc.vector.tensor_copy(qT[u][0:KS, i * HB:(i + 1) * HB, :],
                                          wbank16(w, job)[0:KS, 0:HB * N].rearrange("p (h n) -> p h n", h=HB))\
                        .then_inc(qT_made[u], 1)

            def copy_max(w, a, u):
                for i in range(2):
                    job = (f"m{a}t", u, i)
                    dve.wait_ge(*filled(w, job))
                    nc.vector.tensor_copy(qT[u][KS:KM, i * HB:(i + 1) * HB, :],
                                          wbank16(w, job)[KS:KM, 0:HB * N].rearrange("p (h n) -> p h n", h=HB))\
                        .then_inc(mT_made[u], 1)

            def maxima(w, a, u, i):
                k, n = w.plan.score_at[a, u, i]
                dve.wait_ge(score_ready[k], at(w, score_ready[k], n + 1))
                if a == 1:
                    dst, src = neg_max[u][:, i * HG:(i + 1) * HG], \
                        score[k][0:N, 0:HG * N].rearrange("p (h j) -> p h j", h=HG)
                else:
                    dst, src = neg_max[u][:, i:i + 1], score[k][0:N, 0:J]
                nc.vector.tensor_reduce(dst, src, AX_X, ALU.max, negate=True).then_inc(max_made[u], 1)

            def divide(w, a, u):
                for i, (c0, c1) in enumerate(XB):
                    job = (f"o{a}x", u, i)
                    dve.wait_ge(*filled(w, job))
                    h0, h1 = c0 * QH, c1 * QH
                    o = wbank(w, job)[0:N, 0:(c1 - c0) * P].rearrange("p (h d) -> p h d", d=32)
                    link(w, nc.vector.reciprocal(rden[u][:, h0:h1].unsqueeze(2), o[:, :, DH:D1]))
                    r = rden[u][:, h0:h1].unsqueeze(2).broadcast_to([N, h1 - h0, DH])
                    if h1 == H:
                        nc.vector.tensor_tensor(heads(h[u][:, D:D + 64]), o[:, 16 - h0:, 0:DH], r[:, 16 - h0:, :],
                                                ALU.mult)
                    nc.vector.tensor_tensor(heads(h[u][:, h0 * DH:h1 * DH]), o[:, :, 0:DH], r,
                                            ALU.mult).then_inc(o_normed[u], 1)

            def add_residual(w, a, u, dst, made):
                job = (f"o{a}", u, 0)
                dve.wait_ge(*filled(w, job))
                dve.wait_ge(xres_made[u], at(w, xres_made[u], a))
                nc.vector.tensor_tensor(dst[:], wbank(w, job)[0:N, 0:D], xres[u][:], ALU.add).then_inc(made, 1)

            def step(now, x, then, s):
                def cross_maxima(first, end):
                    for hd in range(first, end if x is not None else first):
                        maxima(now, 2, x, hd)

                if s is not None:
                    dve.wait_ge(x_landed[s], at(then, x_landed[s], 16))
                    centre(then, s, 1, xin[s])
                cross_maxima(0, 2)
                if s is not None:
                    normalise(then, s, 1)
                cross_maxima(2, 3)
                if s is not None:
                    rest_c_of(then, s, 0)
                cross_maxima(3, 5)
                if s is not None:
                    lows(then, ("h1", s, 0), s, 1)
                cross_maxima(5, 6)
                if s is not None:
                    rest_c_of(then, s, 1)
                cross_maxima(6, 7)
                if s is not None:
                    rest_q_of(then, "q1", s, 1)
                cross_maxima(7, 9)
                if s is not None:
                    dve.wait_ge(p0_k_made[s], at(then, p0_k_made[s], 1))
                    rest(then, ("k1", s, 0), N, stack_k[s][:, :, 0, :], rest_k[s], rest_k_made[s])
                cross_maxima(9, 11)
                if s is not None:
                    rest_c_of(then, s, 2)
                cross_maxima(11, 13)
                if s is not None:
                    copy_q(then, "q1t", s)
                cross_maxima(13, 16)
                if s is not None:
                    maxima(then, 1, s, 0)
                    maxima(then, 1, s, 1)
                cross_maxima(16, 17)
                if s is not None:
                    maxima(then, 1, s, 2)
                    maxima(then, 1, s, 3)
                cross_maxima(17, 20)
                if s is not None:
                    copy_max(then, 1, s)
                if x is not None:
                    copy_max(now, 2, x)
                if s is not None:
                    divide(then, 1, s)
                    lows(then, ("o1t", s, 0), s, 2)
                    add_residual(then, 1, s, x1[s], x1_made[s])
                    dve.wait_ge(x1_made[s], at(then, x1_made[s], 1))
                    centre(then, s, 2, x1[s])
                    normalise(then, s, 2)
                    lows(then, ("h2", s, 0), s, 3)
                    rest_q_of(then, "q2", s, 2)
                if x is not None:
                    divide(now, 2, x)
                    lows(now, ("o2t", x, 0), x, 4)
                if s is not None:
                    copy_q(then, "q2t", s)
                if x is not None:
                    dve.wait_ge(x2_stored[x], at(now, x2_stored[x], 0))
                    add_residual(now, 2, x, x2[x], x2_made[x])

            start(dve, dve_step, *lo_made, *rest_q_made, *rest_k_made, *rest_c_made, *qT_made, *max_made, *mT_made,
                  *o_normed, *x1_made, *x2_made)
            nc.vector.memset(attn[:, :], 0.0).then_inc(ones_set, 1)
            for u in range(U):
                nc.vector.memset(kT[u][KS:KM, :, :], 1.0).then_inc(ones_set, 1)
                nc.vector.memset(kcT[u][KS:KM, :, :], 1.0).then_inc(ones_set, 1)
                nc.vector.memset(vs[u][:, :, DH:D1], 1.0)
                nc.vector.memset(vc[u][:, :, :, DH:D1], 1.0).then_inc(ones_set, 1)
            for m in moments(FIRST, 0):
                step(*m)
            assert links[0] == DVE_STEPS["first"], links
            links[0] = 0
            with dve.Fori(0, NT - 1) as t:
                for m in moments(BODY, t):
                    step(*m)
            assert links[0] == DVE_STEPS["body"], links
            links[0] = 0
            for m in moments(LAST, NT - 1):
                step(*m)

        @block.scalar
        def _(act):
            def high(w, job, u):
                act.wait_ge(*filled(w, job))
                nc.scalar.copy(t_hi[u][:], wbank(w, job)[:, 0:3 * N].rearrange("p (k n) -> p k n", k=3))\
                    .then_inc(hi_made[u], 1)

            def first_q(w, kind, u):
                job = (kind, u, 0)
                act.wait_ge(*filled(w, job))
                src = wbank(w, job)[0:N, 0:D]
                nc.scalar.copy(q_slots(stack_q[u], "last"), heads(src))
                nc.scalar.copy(q_slots(stack_q[u], 0), repeated(src, N, 2)).then_inc(p0_q_made[u], 1)

            def first_k(w, job, n, stack, made):
                act.wait_ge(*filled(w, job))
                nc.scalar.copy(k_slots(stack, 0), repeated(wbank(w, job)[0:n, 0:D], n, 3)).then_inc(made, 1)

            def copy_v(w, job, n, dst, made):
                act.wait_ge(*filled(w, job))
                nc.scalar.copy(dst[:, :, 0:DH], heads(wbank(w, job)[0:n, 0:D])).then_inc(made, 1)

            def context_parts(w, u, i):
                n = JT[i][1]
                first_k(w, ("kc", u, i), n, stack_c[i], p0_c_made[u])
                copy_v(w, ("vc", u, i), n, vc[u][0:n, i], vc_made[u])

            def exponentials(w, a, u, g, jt):
                e = w.plan.exp_at[a, u, g, jt]
                n = JT[jt][1] if a == 2 else N
                act.wait_ge(exp_ready[e % 2], at(w, exp_ready[e % 2], e // 2 + 1))
                act.wait_ge(pv_made, at(w, pv_made, w.plan.pv_before((a, u, g, jt))))
                nc.scalar.activation(probs[e % NPT][0:n, :], expin[e % 2][0:n, 0:HG * N], ACT.Exp,
                                     scale=SCALE).then_inc(probs_made, 1)

            def copy_product(w, a, u):
                act.wait_ge(pv_made, at(w, pv_made, w.plan.pv.index((a, u, G - 1)) + 1))
                nc.scalar.copy(pv[u][:], attn[:, 0:HC * N]).then_inc(pv_copied[u], 1)

            def copy_k(w, u):
                for i in range(2):
                    job = ("k1t", u, i)
                    act.wait_ge(*filled(w, job))
                    nc.scalar.copy(kT[u][0:KS, i * HB:(i + 1) * HB, :],
                                   wbank16(w, job)[0:KS, 0:HB * N].rearrange("p (h n) -> p h n", h=HB))\
                        .then_inc(kT_made[u], 1)

            def copy_context(w, u, i):
                job = ("kct", u, i)
                act.wait_ge(*filled(w, job))
                nc.scalar.copy(kcT[u][0:KS, 2 * i:2 * i + 2, 0:J],
                               wbank16(w, job)[0:KS, 0:2 * JP].rearrange("p (h j) -> p h j", h=2)[:, :, 0:J])\
                    .then_inc(kcT_made[u], 1)

            def step(now, x, then, s):
                def cross_exponentials(*tiles):
                    for g, jt in tiles if x is not None else ():
                        exponentials(now, 2, x, g, jt)

                def context_copies(first, end):
                    for i in range(first, end if s is not None else first):
                        copy_context(then, s, i)

                if s is not None:
                    context_parts(then, s, 0)
                    high(then, ("h1", s, 0), s)
                    context_parts(then, s, 1)
                    first_q(then, "q1", s)
                    first_k(then, ("k1", s, 0), N, stack_k[s], p0_k_made[s])
                    copy_v(then, ("v1", s, 0), N, vs[s], v_made[s])
                    context_parts(then, s, 2)
                    copy_k(then, s)
                context_copies(0, 2)
                if s is not None:
                    for g in range(G):
                        exponentials(then, 1, s, g, 0)
                cross_exponentials((0, 0))
                if s is not None:
                    copy_product(then, 1, s)
                cross_exponentials((0, 1), (0, 2))
                context_copies(2, 4)
                cross_exponentials((1, 0), (1, 1))
                context_copies(4, 5)
                if s is not None:
                    high(then, ("o1t", s, 0), s)
                cross_exponentials((1, 2))
                context_copies(5, 6)
                cross_exponentials((2, 0), (2, 1))
                context_copies(6, 7)
                cross_exponentials((2, 2))
                if s is not None:
                    high(then, ("h2", s, 0), s)
                cross_exponentials((3, 0), (3, 1))
                context_copies(7, 8)
                if s is not None:
                    first_q(then, "q2", s)
                cross_exponentials((3, 2))
                context_copies(8, 9)
                if x is not None:
                    copy_product(now, 2, x)
                context_copies(9, 10)
                if x is not None:
                    high(now, ("o2t", x, 0), x)

            start(act, probs_made, *pv_copied, *v_made, *vc_made, *kT_made, *kcT_made)
            for m in moments(FIRST, 0):
                step(*m)
            with act.Fori(0, NT - 1) as t:
                for m in moments(BODY, t):
                    step(*m)
            for m in moments(LAST, NT - 1):
                step(*m)

        @block.gpsimd
        def _(pool):
            links = [0]

            def link(w, ins):
                links[0] += 1
                ins.then_inc(pool_step, 1)
                pool.wait_ge(pool_step, at(w, pool_step, links[0]))

            def inverse_deviation(w, u, a):
                pool.wait_ge(stats_made[u], at(w, stats_made[u], a))
                link(w, nc.gpsimd.tensor_tensor(var_eps[u][:], mv[u][:, 1:2], eps[0:N, :], ALU.add))
                nc.gpsimd.tensor_tensor(rstd[u][:], var_eps[u][:], neg_half[0:N, :], ALU.pow)\
                    .then_inc(rstd_made[u], 1)

            def residual(w, u, a, src):
                nc.gpsimd.tensor_tensor(xres[u][:], src[:], vec[f"o{a}_b"][:], ALU.add).then_inc(xres_made[u], 1)

            def split_context(w, after, u):
                pool.wait_ge(ctx_landed[u], at(after, ctx_landed[u], 48))
                link(w, nc.gpsimd.tensor_tensor(ctx_hi[:], ctx_raw[u][:], one[:].unsqueeze(2).broadcast_to([P, 2, J]),
                                                ALU.mult))
                link(w, nc.gpsimd.tensor_tensor(ctx_hi[64:P, 1, :], ctx_raw[u][64:P, 1, :],
                                                ctx_hi[64:P, 1, :].bitcast(F32), ALU.subtract))
                nc.gpsimd.tensor_tensor(ctx_lo[:], ctx_raw[u][:, 0, :], ctx_hi[:, 0, :].bitcast(F32),
                                        ALU.subtract).then_inc(ctx_split[u], 1)

            def more_parts(w, slots, stack, rest, n, made):
                link(w, nc.gpsimd.tensor_tensor(slots(stack, 1), repeated(rest[:], n, 2),
                                                one[0:n, :].unsqueeze(2).unsqueeze(3).broadcast_to([n, H, 2, DH]), ALU.mult))
                second = 1 if slots is q_slots else 3
                nc.gpsimd.tensor_tensor(slots(stack, 2), heads(rest[:]), stack[:, :, second, :], ALU.subtract)\
                    .then_inc(made, 1)

            def more_parts_q(w, u, n):
                pool.wait_ge(rest_q_made[u], at(w, rest_q_made[u], n))
                more_parts(w, q_slots, stack_q[u], rest_q[u], N, stack_q_made[u])

            def more_parts_c(w, u, i):
                pool.wait_ge(rest_c_made[u], at(w, rest_c_made[u], i + 1))
                more_parts(w, k_slots, stack_c[i], rest_c[i], JT[i][1], stack_c_made[u])

            def split_maxima(w, a, u, i):
                pool.wait_ge(max_made[u], at(w, max_made[u], (i + 1) * 2 if a == 1 else G + (i + 1) * HB))
                c = slice(i * HB, (i + 1) * HB)
                ones = one[0:N, :].broadcast_to([N, HB])
                m, r, parts = neg_max[u][:, c], max_rest[u][:, c], max_parts[u][:, c, :]
                link(w, nc.gpsimd.tensor_tensor(parts[:, :, 0], m, ones, ALU.mult))
                link(w, nc.gpsimd.tensor_tensor(r, m, parts[:, :, 0], ALU.subtract))
                link(w, nc.gpsimd.tensor_tensor(parts[:, :, 1], r, ones, ALU.mult))
                nc.gpsimd.tensor_tensor(parts[:, :, 2], r, parts[:, :, 1], ALU.subtract).then_inc(parts_made[u], 1)

            def step(now, x, then, s):
                if s is not None:
                    inverse_deviation(then, s, 1)
                    pool.wait_ge(x_landed[s], at(then, x_landed[s], 16))
                    residual(then, s, 1, xin[s])
                    more_parts_c(then, s, 0)
                    more_parts_q(then, s, 1)
                    pool.wait_ge(rest_k_made[s], at(then, rest_k_made[s], 1))
                    more_parts(then, k_slots, stack_k[s], rest_k[s], N, stack_k_made[s])
                    more_parts_c(then, s, 1)
                if x is not None:
                    split_maxima(now, 2, x, 0)
                if s is not None:
                    more_parts_c(then, s, 2)
                    for i in range(2):
                        split_maxima(then, 1, s, i)
                if x is not None:
                    split_maxima(now, 2, x, 1)
                if now.plan is not LAST:
                    pool.wait_ge(*filled(then, ("vc", s, 2)))
                    after = When(BODY, now.t, 1) if x is not None else now
                    split_context(now, after, 1 - s)
                if s is not None:
                    inverse_deviation(then, s, 2)
                    residual(then, s, 2, x1[s])
                    more_parts_q(then, s, 2)

            start(pool, pool_step)
            now = When(FIRST, 0)
            split_context(now, now, 0)
            for m in moments(FIRST, 0):
                step(*m)
            assert links[0] == POOL_STEPS["first"], links
            links[0] = 0
            with pool.Fori(0, NT - 1) as t:
                for m in moments(BODY, t):
                    step(*m)
            assert links[0] == POOL_STEPS["body"], links
            links[0] = 0
            for m in moments(LAST, NT - 1):
                step(*m)


def make_identity(nc, pool, ident, step):
    nc.gpsimd.memset(ident[:], 0.0).then_inc(step, 1)
    pool.wait_ge(step, 1)
    nc.gpsimd.affine_select(out=ident[:], in_=ident[:], compare_op=ALU.not_equal, fill=1.0, base=0,
                            pattern=[[-1, P]], channel_multiplier=1).then_inc(step, 1)


TT = 5
NF = B * N // (P * TT)
FT = FF // P
W = TT * P // 2
FV_STEPS, FP_STEPS = 2 * TT, TT


def feed_forward_phase(nc, x2, n3_g, n3_b, ff_w1, ff_b1, ff_w2, ff_b2, out):
    with ExitStack() as ctx:
        def sb(name, shape, dt=F32):
            return ctx.enter_context(nc.sbuf_tensor(name, shape, dt))

        w1_hi, w1_lo = sb("w1_hi", [P, 3, 2 * FF], F32R), sb("w1_lo", [P, 3, 2 * FF], F32R)
        w2_hi, w2_lo = sb("w2_hi", [P, FT, D], F32R), sb("w2_lo", [P, FT, D], F32R)
        vectors = {"g": n3_g, "b": n3_b, "ff_b2": ff_b2}
        vec = {k: sb(f"{k}3_rows", [P, D]) for k in vectors}
        b1 = sb("b1_cols", [P, 2 * FT])
        identf = sb("identf3", [P, P])
        neg_half, eps = sb("neg_half3", [P, 1]), sb("eps3", [P, 1])

        CB = 640
        with ExitStack() as prep:
            NB1 = 2 * FF // CB
            raw = [prep.enter_context(nc.sbuf_tensor(f"w1_raw{i}", [P, 3, CB], F32)) for i in range(2)]
            w2_raw = [prep.enter_context(nc.sbuf_tensor(f"w2_raw{i}", [P, FT // 2, D], F32)) for i in range(2)]
            w1_landed = [prep.enter_context(nc.semaphore(f"w1_landed{i}")) for i in range(2)]
            w2_landed = [prep.enter_context(nc.semaphore(f"w2_landed{i}")) for i in range(2)]
            vectors_landed = prep.enter_context(nc.semaphore("vectors3_landed"))
            w_hi_made = prep.enter_context(nc.semaphore("w_hi_made"))
            w_lo_made = prep.enter_context(nc.semaphore("w_lo_made"))
            ident_step = prep.enter_context(nc.semaphore("ident3_step"))
            block = prep.enter_context(nc.Block())

            @block.sync
            def _(sp):
                for i in range(NB1):
                    if i >= 2:
                        sp.wait_ge(w_lo_made, i - 1)
                    w = ff_w1[:, i * CB:(i + 1) * CB]
                    for p0, p1, tile, src in rows3(w):
                        sp.dma_start(raw[i % 2][p0:p1, tile, :], src).then_inc(w1_landed[i % 2], 16)
                    if i < 2:
                        sp.dma_start(w2_raw[i][:], ff_w2.rearrange("(h k p) n -> h p k n", h=2, p=P)[i])\
                            .then_inc(w2_landed[i], 16)
                for k, v in vectors.items():
                    sp.dma_start(vec[k][:], v.rearrange("(a d) -> a d", a=1).broadcast_to([P, D]))\
                        .then_inc(vectors_landed, 16)
                with nc.allow_non_contiguous_dma("a bias, once"):
                    sp.dma_start(b1[:], ff_b1.rearrange("(k p) -> p k", p=P)).then_inc(vectors_landed, 16)
                sp.wait_ge(vectors_landed, 16 * (len(vectors) + 1))

            @block.scalar
            def _(act):
                for i in range(NB1):
                    act.wait_ge(w1_landed[i % 2], 64 * (i // 2 + 1))
                    nc.scalar.copy(w1_hi[:, :, i * CB:(i + 1) * CB], raw[i % 2][:]).then_inc(w_hi_made, 1)
                for i in range(2):
                    act.wait_ge(w2_landed[i], 16)
                    c = slice(i * (FT // 2), (i + 1) * (FT // 2))
                    nc.scalar.copy(w2_hi[:, c, :], w2_raw[i][:]).then_inc(w_hi_made, 1)

            @block.vector
            def _(dve):
                nc.vector.memset(neg_half[:], -0.5)
                nc.vector.memset(eps[:], EPS)
                for i in range(NB1):
                    dve.wait_ge(w_hi_made, i + 1)
                    c = slice(i * CB, (i + 1) * CB)
                    nc.vector.tensor_tensor(w1_lo[:, :, c], raw[i % 2][:], w1_hi[:, :, c].bitcast(F32),
                                            ALU.subtract).then_inc(w_lo_made, 1)
                for i in range(2):
                    dve.wait_ge(w_hi_made, NB1 + i + 1)
                    c = slice(i * (FT // 2), (i + 1) * (FT // 2))
                    nc.vector.tensor_tensor(w2_lo[:, c, :], w2_raw[i][:], w2_hi[:, c, :].bitcast(F32), ALU.subtract)

            @block.gpsimd
            def _(pool):
                make_identity(nc, pool, identf, ident_step)

        spacer = sb("spacer3", [P, 1])
        xt = [sb(f"xt{i}", [P, D]) for i in range(TT)]
        xb = [sb(f"xb{i}", [P, D]) for i in range(TT)]
        yt = [sb(f"yt{i}", [P, D]) for i in range(2)]
        h = [sb(f"h3_{i}", [P, D + 64]) for i in range(2)]
        centred = [sb(f"centred3_{i}", [P, D]) for i in range(2)]
        stats = [sb(f"stats3_{i}", [P, 6]) for i in range(TT)]
        mv = [sb(f"mv3_{i}", [P, 2]) for i in range(TT)]
        var_eps = [sb(f"var_eps3_{i}", [P, 1]) for i in range(TT)]
        rstd = [sb(f"rstd3_{i}", [P, 1]) for i in range(TT)]
        t_hi = sb("t3_hi", [P, 3, TT * P], F32R)
        t_lo = sb("t3_lo", [P, 2, TT * P], F32R)
        gelu = [sb(f"gelu{i}", [P, W]) for i in range(2)]
        hidden = [sb(f"hidden{i}", [P, W]) for i in range(2)]
        hid_hi, hid_lo = sb("hid_hi", [P, FT, TT * P], F32R), sb("hid_lo", [P, FT, TT * P], F32R)

        turn = [ctx.enter_context(nc.psum_tensor(f"turn{i}", [P, 512], F32)) for i in range(2)]
        ps_a = [ctx.enter_context(nc.psum_tensor(f"ps_a{i}", [P, 512], F32)) for i in range(2)]
        ps_g = [ctx.enter_context(nc.psum_tensor(f"ps_g{i}", [P, 512], F32)) for i in range(2)]
        ps_y = [ctx.enter_context(nc.psum_tensor(f"ps_y{i}", [P, 512], F32)) for i in range(2)]

        PER, START = {}, {}

        def sem(name, per, first=0):
            s = ctx.enter_context(nc.semaphore(name))
            PER[s], START[s] = per, first
            return s

        def start(eng, *sems):
            for s in sems:
                eng.sem_inc(s, START[s])

        def at(t, s, n):
            assert n > 0 or START[s] > 0, s
            return t * PER[s] + (START[s] + n)

        NU = 2 * FT
        xt_landed = [sem(f"xt_landed{i}", 16) for i in range(TT)]
        y_stored = [sem(f"y_stored{i}", 16 * [3, 2][i], 16) for i in range(2)]
        stats_made, h_made, lo_made, hidden_made, y_made = (
            sem("stats3_made", TT), sem("h3_made", TT), sem("lo3_made", TT, 1), sem("hidden_made", NU, 1), sem("y_made", TT, 1))
        rstd_made, xb_made, hid_lo_made = sem("rstd3_made", TT), sem("xb_made", TT), sem("hid_lo_made", NU, 1)
        hi_made, gelu_made, hid_hi_made = sem("hi3_made", TT), sem("gelu_made", NU), sem("hid_hi_made", NU)
        turned, g_ready, a_ready, y_ready = sem("turned", TT, 1), sem("g_ready", NU), sem("a_ready", NU), sem("y_ready", TT)
        dve_step, pool_step = sem("dve3_step", FV_STEPS), sem("pool3_step", FP_STEPS)

        x2_tiles = x2.rearrange("(t i p) d -> t i p d", i=TT, p=P)
        out_tiles = out.rearrange("(t i p) d -> t i p d", i=TT, p=P)
        block = ctx.enter_context(nc.Block())

        @block.sync
        def _(sp):
            def load(t, i):
                sp.dma_start(xt[i][:], x2_tiles[t, i]).then_inc(xt_landed[i], 16)

            def store(t, i):
                sp.wait_ge(y_made, at(t, y_made, i + 1))
                sp.dma_start(out_tiles[t, i], yt[i % 2][:]).then_inc(y_stored[i % 2], 16)

            start(sp, *y_stored)
            for i in range(TT):
                load(0, i)
            with sp.Fori(0, NF - 1) as t:
                for i in range(TT):
                    sp.wait_ge(h_made, at(t, h_made, i + 1))
                    sp.wait_ge(xb_made, at(t, xb_made, i + 1))
                    load(t + 1, i)
                for i in range(TT):
                    store(t, i)
            for i in range(TT):
                store(NF - 1, i)
            for i in range(2):
                sp.wait_ge(y_stored[i], at(NF - 1, y_stored[i], PER[y_stored[i]]))

        @block.tensor
        def _(pe):
            start(pe, turned)
            with pe.Fori(0, NF) as t:
                for i in range(TT):
                    pe.wait_ge(lo_made, at(t, lo_made, max(i - 1, 0)))
                    pe.wait_ge(h_made, at(t, h_made, i + 1))
                    for k in range(3):
                        mm = pe.transpose(turn[i % 2][:, k * P:(k + 1) * P], h[i % 2][:, k * P:(k + 1) * P], identf[:])
                    mm.then_inc(turned, 1)
                for half in range(2):
                    for f in range(FT):
                        n = half * FT + f
                        c = slice(half * W, (half + 1) * W)
                        pe.wait_ge(lo_made, at(t, lo_made, [3, TT][half]))
                        for bank, f0, ready in ((ps_g[n % 2], FT + f, g_ready), (ps_a[n % 2], f, a_ready)):
                            pe.wait_ge(hidden_made, at(t, hidden_made, max(n - 1, 0)))
                            w = slice(f0 * P, (f0 + 1) * P)
                            passes = [(w1_hi[:, 0, w], t_hi[:, 0, c]), (w1_lo[:, 0, w], t_hi[:, 0, c]),
                                      (w1_hi[:, 1, w], t_hi[:, 1, c]), (w1_lo[:, 1, w], t_hi[:, 1, c]),
                                      (w1_hi[:, 0, w], t_lo[:, 0, c]), (w1_hi[:, 1, w], t_lo[:, 1, c]),
                                      (w1_hi[:, 2, w], t_hi[:, 2, c]), (w1_lo[:, 2, w], t_hi[:, 2, c])]
                            for k, (a, b) in enumerate(passes):
                                mm = pe.matmul(bank[:, 0:W], a, b, start=(k == 0), stop=(k == len(passes) - 1))
                            mm.then_inc(ready, 1)
                for i in range(TT):
                    pe.wait_ge(y_made, at(t, y_made, max(i - 1, 0)))
                    pe.wait_ge(hid_hi_made, at(t, hid_hi_made, FT if i < 2 else NU))
                    pe.wait_ge(hid_lo_made, at(t, hid_lo_made, FT if i < 2 else NU))
                    y, c = ps_y[i % 2][:, 0:D], slice(i * P, (i + 1) * P)
                    for f in range(FT):
                        pe.matmul(y, hid_hi[:, f, c], w2_hi[:, f, :], start=(f == 0), stop=False)
                        pe.matmul(y, hid_hi[:, f, c], w2_lo[:, f, :], start=False, stop=False)
                        mm = pe.matmul(y, hid_lo[:, f, c], w2_hi[:, f, :], start=False, stop=(f == FT - 1))
                    mm.then_inc(y_ready, 1)

        @block.vector
        def _(dve):
            step = [0]

            def link(t, ins):
                step[0] += 1
                ins.then_inc(dve_step, 1)
                dve.wait_ge(dve_step, at(t, dve_step, step[0]))

            def split_low(t, i):
                dve.wait_ge(hi_made, at(t, hi_made, i + 1))
                c = slice(i * P, (i + 1) * P)
                v = turn[i % 2][:, 0:3 * P].rearrange("p (k n) -> p k n", k=3)
                nc.vector.tensor_tensor(t_hi[64:P, 2, c], v[64:P, 2, :], t_hi[64:P, 2, c].bitcast(F32), ALU.subtract)
                nc.vector.tensor_tensor(t_lo[:, :, c], v[:, 0:2, :], t_hi[:, 0:2, c].bitcast(F32),
                                        ALU.subtract).then_inc(lo_made, 1)

            start(dve, lo_made, hidden_made, y_made)
            with dve.Fori(0, NF) as t:
                for i in range(TT):
                    dve.wait_ge(xt_landed[i], at(t, xt_landed[i], 16))
                    link(t, nc.vector.bn_stats(stats[i][:], xt[i][:]))
                    nc.vector.memset(spacer[0:1, :], 0.0)
                    nc.vector.bn_aggr(mv[i][:], stats[i][:]).then_inc(stats_made, 1)
                for i in range(TT):
                    hb = h[i % 2]
                    dve.wait_ge(turned, at(t, turned, max(i - 1, 0)))
                    dve.wait_ge(stats_made, at(t, stats_made, i + 1))
                    link(t, nc.vector.scalar_tensor_tensor(out=centred[i % 2][:], in0=xt[i][:], scalar=mv[i][:, 0:1],
                                                           in1=vec["g"][:], op0=ALU.subtract, op1=ALU.mult))
                    dve.wait_ge(rstd_made, at(t, rstd_made, i + 1))
                    nc.vector.scalar_tensor_tensor(out=hb[:, D:D + 64], in0=centred[i % 2][:, 2 * P:D], scalar=rstd[i][:],
                                                   in1=vec["b"][:, 2 * P:D], op0=ALU.mult, op1=ALU.add)
                    nc.vector.scalar_tensor_tensor(out=hb[:, 0:D], in0=centred[i % 2][:], scalar=rstd[i][:],
                                                   in1=vec["b"][:], op0=ALU.mult, op1=ALU.add).then_inc(h_made, 1)
                    if i:
                        split_low(t, i - 1)
                split_low(t, TT - 1)
                for n in range(NU):
                    dve.wait_ge(a_ready, at(t, a_ready, n + 1))
                    dve.wait_ge(gelu_made, at(t, gelu_made, n + 1))
                    dve.wait_ge(hid_lo_made, at(t, hid_lo_made, max(n - 1, 0)))
                    nc.vector.scalar_tensor_tensor(out=hidden[n % 2][:], in0=ps_a[n % 2][:, 0:W],
                                                   scalar=b1[:, n % FT:n % FT + 1], in1=gelu[n % 2][:],
                                                   op0=ALU.add, op1=ALU.mult).then_inc(hidden_made, 1)
                for i in range(TT):
                    dve.wait_ge(y_ready, at(t, y_ready, i + 1))
                    dve.wait_ge(xb_made, at(t, xb_made, i + 1))
                    dve.wait_ge(y_stored[i % 2], at(t, y_stored[i % 2], 16 * (i // 2)))
                    nc.vector.tensor_tensor(yt[i % 2][:], ps_y[i % 2][:, 0:D], xb[i][:], ALU.add)\
                        .then_inc(y_made, 1)
            assert step[0] == FV_STEPS, step[0]

        @block.scalar
        def _(act):
            def features(n):
                half, f = n // FT, n % FT
                return f, slice(half * W, (half + 1) * W)

            def split_high(t, n):
                f, c = features(n)
                act.wait_ge(hidden_made, at(t, hidden_made, n + 1))
                nc.scalar.copy(hid_hi[:, f, c], hidden[n % 2][:]).then_inc(hid_hi_made, 1)

            with act.Fori(0, NF) as t:
                for i in range(TT):
                    act.wait_ge(turned, at(t, turned, i + 1))
                    nc.scalar.copy(t_hi[:, :, i * P:(i + 1) * P],
                                   turn[i % 2][:, 0:3 * P].rearrange("p (k n) -> p k n", k=3)).then_inc(hi_made, 1)
                for n in range(NU):
                    act.wait_ge(g_ready, at(t, g_ready, n + 1))
                    act.wait_ge(hidden_made, at(t, hidden_made, max(n - 1, 0)))
                    f = n % FT
                    nc.scalar.activation(gelu[n % 2][:], ps_g[n % 2][:, 0:W], ACT.Gelu,
                                         bias=b1[:, FT + f:FT + f + 1]).then_inc(gelu_made, 1)
                    if n:
                        split_high(t, n - 1)
                split_high(t, NU - 1)

        @block.gpsimd
        def _(pool):
            step = [0]

            def link(t, ins):
                step[0] += 1
                ins.then_inc(pool_step, 1)
                pool.wait_ge(pool_step, at(t, pool_step, step[0]))

            start(pool, hid_lo_made)
            with pool.Fori(0, NF) as t:
                for i in range(TT):
                    pool.wait_ge(stats_made, at(t, stats_made, i + 1))
                    link(t, nc.gpsimd.tensor_tensor(var_eps[i][:], mv[i][:, 1:2], eps[:], ALU.add))
                    nc.gpsimd.tensor_tensor(rstd[i][:], var_eps[i][:], neg_half[:], ALU.pow).then_inc(rstd_made, 1)
                pool.wait_ge(y_made, at(t, y_made, 0))
                for i in range(TT):
                    pool.wait_ge(xt_landed[i], at(t, xt_landed[i], 16))
                    nc.gpsimd.tensor_tensor(xb[i][:], xt[i][:], vec["ff_b2"][:], ALU.add).then_inc(xb_made, 1)
                for n in range(NU):
                    half, f = n // FT, n % FT
                    c = slice(half * W, (half + 1) * W)
                    pool.wait_ge(hid_hi_made, at(t, hid_hi_made, n + 1))
                    nc.gpsimd.tensor_tensor(hid_lo[:, f, c], hidden[n % 2][:], hid_hi[:, f, c].bitcast(F32),
                                            ALU.subtract).then_inc(hid_lo_made, 1)
            assert step[0] == FP_STEPS, step[0]


_P = "L0_xattn_"
_WEIGHTS = ["n1_g", "n1_b", "q1", "k1", "v1", "o1_w", "o1_b", "n2_g", "n2_b", "q2", "k2", "v2", "o2_w", "o2_b",
            "n3_g", "n3_b", "ff_w1", "ff_b1", "ff_w2", "ff_b2"]


def kernel(**inputs):
    import numpy as np
    import concourse.bacc as bacc
    from concourse.bass_utils import run_bass_kernel_spmd

    arrays = {"x": np.ascontiguousarray(inputs["x"]),
              "ctxT": np.ascontiguousarray(np.transpose(inputs["ctx_768"], (0, 2, 1)))}
    for name in _WEIGHTS:
        arrays[name] = np.ascontiguousarray(inputs[_P + name])
    nc = bacc.Bacc("TRN2", target_bir_lowering=False, num_devices=1)
    args = [nc.dram_tensor(f"in_{name}", a.shape, mybir.dt.from_np(a.dtype), kind="ExternalInput").ap()
            for name, a in arrays.items()]
    out = nc.dram_tensor("out_0", (B, N, D), F32, kind="ExternalOutput").ap()
    build(nc, *args, out)
    r = run_bass_kernel_spmd(nc, [{f"in_{name}": a for name, a in arrays.items()}], core_ids=[0])
    return r.results[0]["out_0"]
```

```python
from contextlib import ExitStack

import concourse.bass as bass
from concourse import mybir

F32 = mybir.dt.float32
F32R = mybir.dt.float32r
BF16 = mybir.dt.bfloat16
ALU = mybir.AluOpType
ACT = mybir.ActivationFunctionType
AX_X = mybir.AxisListType.X

B, N, D = 32, 100, 320
H, DH = 20, 16
J, C = 361, 192
FF = 1280
EPS = 1e-5
SCALE = DH ** -0.5
P = 128
U = 2
NT = B // U
SL = 6
KS = SL * DH
KM = KS + 3
JT = [(0, 120), (120, 120), (240, 121)]
JP = 362
G, HG = 4, 5
DVE_STEPS = {"first": 8, "body": 16, "last": 8}
POOL_STEPS = {"first": 21, "body": 44, "last": 23}
HB = 10
D1 = DH + 1
QH = 4
HC = H // QH
XB = [(0, 3), (3, HC)]



STEPS = {"first": [(None, None, 0), (None, 0, 1)], "body": [(0, 1, 0), (1, 0, 1)],
         "last": [(0, 1, None), (1, None, None)]}
NW = 3
EARLY = 8
NPT = 6
OF_CROSS, OF_NEXT = ("m2t", "o2x", "o2t", "o2"), ("h1", "q1", "k1", "v1", "q1t", "k1t")


def work_jobs(x, s, c):
    order = [("m1t", 0), ("m1t", 1), ("kc", 0), ("vc", 0), ("h1", 0), ("q1", 0), ("kc", 1), ("vc", 1),
             ("o1x", 0), ("o1x", 1), ("k1", 0), ("o1t", 0), ("v1", 0), ("m2t", 0), ("m2t", 1), ("o1", 0),
             ("kc", 2), ("vc", 2), ("h2", 0), ("q2", 0), ("kct", 0), ("kct", 1), ("kct", 2), ("kct", 3),
             ("q2t", 0), ("q2t", 1), ("kct", 4), ("kct", 5), ("q1t", 0), ("q1t", 1), ("o2x", 0), ("o2x", 1),
             ("k1t", 0), ("k1t", 1), ("kct", 6), ("kct", 7), ("o2t", 0), ("kct", 8), ("kct", 9), ("o2", 0)]
    whose = {kind: x if kind in OF_CROSS else c if kind in OF_NEXT else s for kind, _ in order}
    return [(kind, whose[kind], i) for kind, i in order if whose[kind] is not None]


def score_jobs(x, s, c):
    cross = [] if x is None else [(2, x, hd) for hd in range(H)]
    own = [] if s is None else [(1, s, g) for g in range(G)]
    coming = [] if s is None else [(2, s, hd) for hd in range(EARLY)]
    return own[:2] + cross[EARLY:9] + own[2:] + cross[9:] + coming


def exp_jobs(x, s, c):
    return ([] if s is None else [(1, s, g, 0) for g in range(G)]) + \
        ([] if x is None else [(2, x, g, j) for g in range(G) for j in range(3)])


def pv_jobs(x, s, c):
    return ([] if s is None else [(1, s, g) for g in range(G)]) + ([] if x is None else [(2, x, g) for g in range(G)])


class Plan:

    def __init__(self, name):
        def over(jobs):
            return [job for step in STEPS[name] for job in jobs(*step)]

        self.name = name
        self.work, self.score, self.exp, self.pv = over(work_jobs), over(score_jobs), over(exp_jobs), over(pv_jobs)
        self.work_at = {job: (i % NW, i // NW) for i, job in enumerate(self.work)}
        self.score_at = {job: (i % 2, i // 2) for i, job in enumerate(self.score)}
        self.exp_at = {job: i for i, job in enumerate(self.exp)}

    def on_work(self, k):
        return sum(1 for b, _ in self.work_at.values() if b == k)

    def ahead(self, kind, u):
        return int(self.name == "body" and (kind in OF_NEXT or kind not in OF_CROSS and u == 0))

    def pv_before(self, job):
        i = self.exp_at[job] - NPT
        return self.pv.index(self.exp[i][:3]) + 1 if i >= 0 else 0


FIRST, BODY, LAST = Plan("first"), Plan("body"), Plan("last")


class When:

    def __init__(self, plan, t, ahead=0):
        self.plan, self.t, self.ahead = plan, t, ahead


def moments(plan, t):
    return [(When(plan, t), x, When(plan, t, plan.ahead("kc", s)), s, When(plan, t, plan.ahead("h1", c)), c)
            for x, s, c in STEPS[plan.name]]


def rows3(w):
    return [(0, P, 0, w[0:P]), (0, P, 1, w[P:2 * P]), (0, 64, 2, w[2 * P:D]), (64, P, 2, w[2 * P:D])]


def rows2(w):
    return [(0, P, 0, w[0:P]), (0, 64, 1, w[P:C]), (64, P, 1, w[P:C])]


def build(nc, x, ctxT, n1_g, n1_b, q1, k1, v1, o1_w, o1_b, n2_g, n2_b, q2, k2, v2, o2_w, o2_b,
          n3_g, n3_b, ff_w1, ff_b1, ff_w2, ff_b2, out):
    x2_dram = nc.dram_tensor("x2_dram", [B * N, D], F32).ap()
    attention_phase(nc, x, ctxT, n1_g, n1_b, (q1, k1, v1), o1_w, o1_b, n2_g, n2_b, q2, k2, v2, o2_w, o2_b,
                    x2_dram.rearrange("(b n) d -> b n d", n=N))
    feed_forward_phase(nc, x2_dram, n3_g, n3_b, ff_w1, ff_b1, ff_w2, ff_b2, out.rearrange("b n d -> (b n) d"))


def attention_phase(nc, x, ctxT, n1_g, n1_b, qkv1, o1_w, o1_b, n2_g, n2_b, q2, k2, v2, o2_w, o2_b, x2_dram):
    with ExitStack() as ctx:
        def sb(name, shape, dt=F32):
            return ctx.enter_context(nc.sbuf_tensor(name, shape, dt))

        names = {"q1": (qkv1[0], 3), "k1": (qkv1[1], 3), "v1": (qkv1[2], 3), "kc": (k2, 2), "vc": (v2, 2),
                 "o1": (o1_w, 3), "q2": (q2, 3), "o2": (o2_w, 3)}
        whi = {k: sb(f"w_{k}_hi", [P, kt, D], F32R) for k, (_, kt) in names.items()}
        wlo = {k: sb(f"w_{k}_lo", [P, kt, D], F32R) for k, (_, kt) in names.items()}
        vectors = {"n1_g": n1_g, "n1_b": n1_b, "n2_g": n2_g, "n2_b": n2_b, "o1_b": o1_b, "o2_b": o2_b}
        vec = {k: sb(f"{k}_rows", [N, D]) for k in vectors}
        identf = sb("identf", [P, P])
        identb = sb("identb", [P, P], BF16)
        neg_half, eps, one = sb("neg_half", [P, 1]), sb("eps", [P, 1]), sb("one", [P, 1])

        def two(name, shape, dt=F32):
            return [sb(f"{name}{u}", shape, dt) for u in range(U)]

        kT = two("kT", [KM, H, N], BF16)
        kcT = two("kcT", [KM, H, JP], BF16)
        vs = two("vs", [N, H, D1])
        vc = two("vc", [JT[2][1], 3, H, D1])

        with ExitStack() as prep:
            raw = {k: prep.enter_context(nc.sbuf_tensor(f"w_{k}_raw", [P, kt, D], F32))
                   for k, (_, kt) in names.items()}
            weight_landed = {k: prep.enter_context(nc.semaphore(f"w_{k}_landed")) for k in names}
            vectors_landed = prep.enter_context(nc.semaphore("vectors_landed"))
            whi_made = prep.enter_context(nc.semaphore("whi_made"))
            ident_step = prep.enter_context(nc.semaphore("ident_step"))
            block = prep.enter_context(nc.Block())

            @block.sync
            def _(sp):
                for k, (w, kt) in names.items():
                    for p0, p1, tile, src in (rows3(w) if kt == 3 else rows2(w)):
                        sp.dma_start(raw[k][p0:p1, tile, :], src).then_inc(weight_landed[k], 16)
                for k, v in vectors.items():
                    src = v.rearrange("(a d) -> a d", a=1).broadcast_to([N, D])
                    sp.dma_start(vec[k][:], src).then_inc(vectors_landed, 16)
                sp.wait_ge(vectors_landed, 16 * len(vectors))

            @block.scalar
            def _(act):
                for k, (_, kt) in names.items():
                    act.wait_ge(weight_landed[k], 16 * (kt + 1))
                    nc.scalar.copy(whi[k][:], raw[k][:]).then_inc(whi_made, 1)

            @block.vector
            def _(dve):
                nc.vector.memset(neg_half[:], -0.5)
                nc.vector.memset(eps[:], EPS)
                nc.vector.memset(one[:], 1.0)
                for u in range(U):
                    nc.vector.memset(vs[u][:, :, DH:D1], 1.0)
                    nc.vector.memset(vc[u][:, :, :, DH:D1], 1.0)
                    nc.vector.memset(kT[u][KS:KM, :, :], 1.0)
                for i, k in enumerate(names):
                    dve.wait_ge(whi_made, i + 1)
                    nc.vector.tensor_tensor(wlo[k][:], raw[k][:], whi[k][:].bitcast(F32), ALU.subtract)

            @block.gpsimd
            def _(pool):
                make_identity(nc, pool, identf, ident_step)
                pool.wait_ge(ident_step, 2)
                nc.gpsimd.tensor_copy(identb[:], identf[:]).then_inc(ident_step, 1)
                pool.wait_ge(ident_step, 3)
                for u in range(U):
                    nc.gpsimd.memset(kcT[u][KS:KM, :, :], 1.0)

        spacer = sb("spacer", [P, 1])
        xin = two("xin", [N, D])
        x1 = two("x1", [N, D])
        x2 = two("x2", [N, D])
        xres = two("xres", [N, D])
        h = two("h", [N, D + 64])
        centred = two("centred", [N, D])
        stats = two("stats", [N, 6])
        mv = two("mv", [N, 2])
        var_eps = two("var_eps", [N, 1])
        rstd = two("rstd", [N, 1])
        t_hi = two("t_hi", [P, 3, N], F32R)
        t_lo = two("t_lo", [P, 2, N], F32R)
        stack_q = two("stack_q", [N, H, SL, DH], BF16)
        stack_k = two("stack_k", [N, H, SL, DH], BF16)
        rest_q = two("rest_q", [N, D])
        rest_k = two("rest_k", [N, D])
        stack_c = [sb(f"stack_c{i}", [n, H, SL, DH], BF16) for i, (_, n) in enumerate(JT)]
        rest_c = [sb(f"rest_c{i}", [n, D]) for i, (_, n) in enumerate(JT)]
        qT = two("qT", [KM, H, N], BF16)
        ctx_raw = two("ctx_raw", [P, 2, J])
        ctx_hi = sb("ctx_hi", [P, 2, J], F32R)
        ctx_lo = sb("ctx_lo", [P, J], F32R)
        neg_max = two("neg_max", [N, H])
        max_rest = two("max_rest", [N, H])
        max_parts = two("max_parts", [N, H, 4], BF16)
        probs = [sb(f"probs{i}", [JT[2][1], HG * N]) for i in range(NPT)]
        rden = two("rden", [N, H])
        pv = two("pv", [P, HC * N])

        work = [ctx.enter_context(nc.psum_tensor(f"work{i}", [P, 512], F32)) for i in range(NW)]
        score = [ctx.enter_context(nc.psum_tensor(f"score{i}", [P, 512], F32)) for i in range(2)]
        expin = [ctx.enter_context(nc.psum_tensor(f"expin{i}", [P, 512], F32)) for i in range(2)]
        attn = ctx.enter_context(nc.psum_tensor("attn", [P, 512], F32))

        PER, START, BEFORE = {}, {}, {}

        def sem(name, per, first=0):
            s = ctx.enter_context(nc.semaphore(name))
            PER[s], START[s] = per, first
            return s

        def shared(name, count):
            s = sem(name, count(BODY), 1)
            BEFORE[s] = count(FIRST)
            return s

        def start(eng, *sems):
            for s in sems:
                eng.sem_inc(s, START[s])

        def sem2(name, per, first=0):
            return [sem(f"{name}{u}", per, first) for u in range(U)]

        x_landed, ctx_landed, x2_stored = sem2("x_landed", 16), sem2("ctx_landed", 48), sem2("x2_stored", 16, 16)
        attn_cleared = sem("attn_cleared", 0)
        stats_made = sem2("stats_made", 2)
        h_made = sem2("h_made", 2)
        lo_made, o2_lo_made = sem2("lo_made", 3, 3), sem2("o2_lo_made", 1, 1)
        rest_q_made, rest_k_made, rest_c_made = sem2("rest_q_made", 2, 2), sem2("rest_k_made", 1, 1), sem2("rest_c_made", 3, 3)
        q1T_made, q2T_made = sem2("q1T_made", 2, 2), sem2("q2T_made", 2, 2)
        max_made = sem2("max_made", G + H, G + H)
        kcT_odd_made = sem2("kcT_odd_made", H // 4, H // 4)
        o_normed = sem2("o_normed", 4, 4)
        x1_made, x2_made = sem2("x1_made", 1, 1), sem2("x2_made", 1, 1)
        rstd_made = sem2("rstd_made", 2)
        xres_made = sem2("xres_made", 2)
        ctx_split = sem2("ctx_split", 1)
        stack_q_made, stack_k_made, stack_c_made = sem2("stack_q_made", 2), sem2("stack_k_made", 1), sem2("stack_c_made", 3)
        parts_made = sem2("parts_made", 4)
        hi_made, o2_hi_made = sem2("hi_made", 3), sem2("o2_hi_made", 1)
        p0_q_made, p0_k_made, p0_c_made = sem2("p0_q_made", 2), sem2("p0_k_made", 1), sem2("p0_c_made", 3)
        mT_made = sem2("mT_made", 4, 4)
        pv_copied = sem2("pv_copied", 2, 2)
        v_made, vc_made = sem2("v_made", 1, 1), sem2("vc_made", 3, 3)
        kT_made = sem2("kT_made", 2, 2)
        kcT_made = sem2("kcT_made", H // 4, H // 4)
        probs_made = shared("probs_made", lambda plan: len(plan.exp))
        work_ready = [shared(f"work_ready{k}", lambda plan: plan.on_work(k)) for k in range(NW)]
        score_ready = [shared(f"score_ready{k}", lambda plan: len(plan.score) // 2) for k in range(2)]
        exp_ready = [shared(f"exp_ready{k}", lambda plan: len(plan.exp) // 2) for k in range(2)]
        pv_made = shared("pv_made", lambda plan: len(plan.pv))
        dve_step = shared("dve_step", lambda plan: DVE_STEPS[plan.name])
        pool_step = shared("pool_step", lambda plan: POOL_STEPS[plan.name])

        def at(w, s, n):
            if s not in BEFORE:
                return w.t * PER[s] + (w.ahead * PER[s] + START[s] + n)
            if w.plan is FIRST:
                return START[s] + n
            return w.t * PER[s] + (START[s] + BEFORE[s] + n)

        def emptied(w, job, back=0):
            kind, u, i = job
            s, n = {
                "h1": (lo_made[u], 1), "o1t": (lo_made[u], 2), "h2": (lo_made[u], 3), "o2t": (o2_lo_made[u], 1),
                "q1": (rest_q_made[u], 1), "q2": (rest_q_made[u], 2), "k1": (rest_k_made[u], 1),
                "v1": (v_made[u], 1), "kc": (rest_c_made[u], i + 1), "vc": (vc_made[u], i + 1),
                "q1t": (q1T_made[u], i + 1), "q2t": (q2T_made[u], i + 1), "k1t": (kT_made[u], i + 1),
                "kct": ((kcT_odd_made if i % 2 else kcT_made)[u], i // 2 + 1), "m1t": (mT_made[u], i + 1), "m2t": (mT_made[u], i + 3),
                "o1x": (o_normed[u], i + 1), "o2x": (o_normed[u], i + 3),
                "o1": (x1_made[u], 1), "o2": (x2_made[u], 1),
            }[kind]
            plan = BODY if back else w.plan
            return s, at(When(w.plan, w.t, plan.ahead(kind, u) - back), s, n)

        def wbank(w, job):
            return work[w.plan.work_at[job][0]]

        def wbank16(w, job):
            return wbank(w, job)[:, :].bitcast(BF16)

        def filled(w, job):
            k, n = w.plan.work_at[job]
            return work_ready[k], at(w, work_ready[k], n + 1)

        def q_slots(stack, part):
            return {0: stack[:, :, 0:4:3, :], 1: stack[:, :, 1:5:3, :], 2: stack[:, :, 2, :],
                    "last": stack[:, :, 5, :]}[part]

        def k_slots(stack, part):
            return {0: stack[:, :, 0:3, :], 1: stack[:, :, 3:5, :], 2: stack[:, :, 5, :]}[part]

        def heads(ap):
            return ap.rearrange("p (h d) -> p h d", d=DH)

        def repeated(ap, n, k):
            return heads(ap).unsqueeze(2).broadcast_to([n, H, k, DH])

        block = ctx.enter_context(nc.Block())

        @block.sync
        def _(sp):
            def load(b, u):
                sp.dma_start(xin[u][:], x[b]).then_inc(x_landed[u], 16)

            def load_context(b, u):
                c = ctxT[b]
                sp.dma_start(ctx_raw[u][0:P, 0, :], c[0:P]).then_inc(ctx_landed[u], 16)
                sp.dma_start(ctx_raw[u][0:64, 1, :], c[P:C]).then_inc(ctx_landed[u], 16)
                sp.dma_start(ctx_raw[u][64:P, 1, :], c[P:C]).then_inc(ctx_landed[u], 16)

            start(sp, *x2_stored)
            for u in range(U):
                load_context(u, u)
                load(u, u)
            with sp.Fori(0, NT - 1) as t:
                now = When(BODY, t)
                for u in range(U):
                    sp.wait_ge(ctx_split[u], at(now, ctx_split[u], 1))
                    load_context(t * U + (U + u), u)
                    sp.wait_ge(xres_made[u], at(now, xres_made[u], 1))
                    sp.wait_ge(h_made[u], at(now, h_made[u], 1))
                    load(t * U + (U + u), u)
                for u in range(U):
                    sp.wait_ge(x2_made[u], at(now, x2_made[u], 1))
                    sp.dma_start(x2_dram[t * U + u], x2[u][:]).then_inc(x2_stored[u], 16)
            now = When(LAST, NT - 1)
            for u in range(U):
                sp.wait_ge(x2_made[u], at(now, x2_made[u], 1))
                sp.dma_start(x2_dram[B - U + u], x2[u][:]).then_inc(x2_stored[u], 16)
            for u in range(U):
                sp.wait_ge(x2_stored[u], at(now, x2_stored[u], 16))

        @block.tensor
        def _(pe):
            filling = [0]

            def fill(w, job):
                assert w.plan.work[filling[0]] == job, (w.plan.work[filling[0]], job)
                filling[0] = (filling[0] + 1) % len(w.plan.work)
                k, n = w.plan.work_at[job]
                if n:
                    pe.wait_ge(*emptied(w, w.plan.work[(n - 1) * NW + k]))
                elif w.plan is not FIRST:
                    pe.wait_ge(*emptied(w, BODY.work[(BODY.on_work(k) - 1) * NW + k], back=1))

            def done(w, ins, job):
                ins.then_inc(work_ready[w.plan.work_at[job][0]], 1)

            def transpose_features(w, job, u):
                fill(w, job)
                for k in range(3):
                    mm = pe.transpose(wbank(w, job)[:, k * N:(k + 1) * N], h[u][:, k * P:(k + 1) * P], identf[0:N, 0:N])
                done(w, mm, job)

            def project(w, job, u, weight, n, halves=(0, 1)):
                dst, a, b = wbank(w, job)[0:N, 0:D], t_hi[u], t_lo[u]
                highs, lows = (hi_made[u], lo_made[u]) if n else (o2_hi_made[u], o2_lo_made[u])
                if 0 in halves:
                    fill(w, job)
                    pe.wait_ge(highs, at(w, highs, n or 1))
                    pe.matmul(dst, a[:, 0, :], whi[weight][:, 0, :], start=True, stop=False)
                    pe.matmul(dst, a[:, 0, :], wlo[weight][:, 0, :], start=False, stop=False)
                    pe.matmul(dst, a[:, 1, :], whi[weight][:, 1, :], start=False, stop=False)
                    pe.matmul(dst, a[:, 1, :], wlo[weight][:, 1, :], start=False, stop=False)
                if 1 in halves:
                    pe.wait_ge(lows, at(w, lows, n or 1))
                    pe.matmul(dst, b[:, 0, :], whi[weight][:, 0, :], start=False, stop=False)
                    pe.matmul(dst, b[:, 1, :], whi[weight][:, 1, :], start=False, stop=False)
                    pe.matmul(dst, a[:, 2, :], whi[weight][:, 2, :], start=False, stop=False)
                    done(w, pe.matmul(dst, a[:, 2, :], wlo[weight][:, 2, :], start=False, stop=True), job)

            def project_context(w, u, i, weight):
                pe.wait_ge(ctx_split[u], at(w, ctx_split[u], 1))
                j0, n = JT[i]
                hi0, lo0, last = ctx_hi[:, 0, j0:j0 + n], ctx_lo[:, j0:j0 + n], ctx_hi[:, 1, j0:j0 + n]
                job = (weight, u, i)
                fill(w, job)
                dst = wbank(w, job)[0:n, 0:D]
                pe.matmul(dst, hi0, whi[weight][:, 0, :], start=True, stop=False)
                pe.matmul(dst, hi0, wlo[weight][:, 0, :], start=False, stop=False)
                pe.matmul(dst, lo0, whi[weight][:, 0, :], start=False, stop=False)
                pe.matmul(dst, last, whi[weight][:, 1, :], start=False, stop=False)
                done(w, pe.matmul(dst, last, wlo[weight][:, 1, :], start=False, stop=True), job)

            def transpose_stack(w, kind, u, stack):
                for i in range(2):
                    job = (kind, u, i)
                    fill(w, job)
                    for k in range(HB):
                        src = stack[:, i * HB + k].rearrange("p s d -> p (s d)")
                        mm = pe.transpose(wbank16(w, job)[0:KS, k * N:(k + 1) * N], src, identb[0:N, 0:N])
                    done(w, mm, job)

            def transpose_context_stack(w, u, i):
                job = ("kct", u, i)
                fill(w, job)
                for k in range(2):
                    for jt, (j0, n) in enumerate(JT):
                        src = stack_c[jt][:, 2 * i + k].rearrange("p s d -> p (s d)")
                        mm = pe.transpose(wbank16(w, job)[0:KS, k * JP + j0:k * JP + j0 + n], src, identb[0:n, 0:n])
                done(w, mm, job)

            def score_bank(w, job):
                n, back, plan = w.plan.score.index(job) - 2, 0, w.plan
                if n < 0:
                    if plan is FIRST:
                        return
                    n, back, plan = n + len(BODY.score), 1, BODY
                a, u, i = plan.score[n]
                before = When(w.plan, w.t, plan.ahead("kc" if a == 1 or i < EARLY else "o2", u) - back)
                pe.wait_ge(max_made[u], at(before, max_made[u], (a - 1) * G + i + 1))

            def self_scores(w, u, g):
                k = w.plan.score_at[1, u, g][0]
                score_bank(w, (1, u, g))
                for i in range(HG):
                    hd = g * HG + i
                    mm = pe.matmul(score[k][0:N, i * N:(i + 1) * N], qT[u][0:KS, hd, :], kT[u][0:KS, hd, :],
                                   start=True, stop=True)
                mm.then_inc(score_ready[k], 1)

            def cross_scores(w, u, hd):
                k = w.plan.score_at[2, u, hd][0]
                score_bank(w, (2, u, hd))
                copied = (kcT_odd_made if hd // 2 % 2 else kcT_made)[u]
                pe.wait_ge(copied, at(w, copied, hd // 4 + 1))
                pe.matmul(score[k][0:N, 0:J], qT[u][0:KS, hd, :], kcT[u][0:KS, hd, 0:J],
                          start=True, stop=True).then_inc(score_ready[k], 1)

            def transpose_max(w, a, u):
                for i in range(2):
                    job = (f"m{a}t", u, i)
                    fill(w, job)
                    pe.wait_ge(parts_made[u], at(w, parts_made[u], (a - 1) * 2 + i + 1))
                    for k in range(HB):
                        mm = pe.transpose(wbank16(w, job)[KS:KM, k * N:(k + 1) * N], max_parts[u][:, i * HB + k, 0:3],
                                          identb[0:N, 0:N])
                    done(w, mm, job)

            def scores_for_exp(w, a, u, g, jt):
                e = w.plan.exp_at[a, u, g, jt]
                pe.wait_ge(probs_made, at(w, probs_made, max(e - 1, 0)))
                pe.wait_ge(mT_made[u], at(w, mT_made[u], (a - 1) * 2 + (g * HG + HG - 1) // HB + 1))
                j0, n = JT[jt] if a == 2 else (0, N)
                keys = kcT if a == 2 else kT
                for i in range(HG):
                    hd = g * HG + i
                    mm = pe.matmul(expin[e % 2][0:n, i * N:(i + 1) * N], keys[u][:, hd, j0:j0 + n],
                                   qT[u][:, hd, :], start=True, stop=True)
                mm.then_inc(exp_ready[e % 2], 1)

            def times_v(w, a, u, g):
                if g == 0:
                    if a == 1:
                        pe.wait_ge(v_made[u], at(w, v_made[u], 1))
                    else:
                        pe.wait_ge(vc_made[u], at(w, vc_made[u], 3))
                tiles = range(3) if a == 2 else range(1)
                pe.wait_ge(probs_made, at(w, probs_made, w.plan.exp_at[a, u, g, tiles[-1]] + 1))
                for some in (range(QH), range(QH, HG)):
                    for jt in tiles:
                        for i in some:
                            hd = g * HG + i
                            n = JT[jt][1] if a == 2 else N
                            v = vc[u][0:n, jt, hd, :] if a == 2 else vs[u][:, hd, :]
                            p0, c0 = 32 * (hd % QH), N * (hd // QH)
                            mm = pe.matmul(attn[p0:p0 + D1, c0:c0 + N], v,
                                           probs[w.plan.exp_at[a, u, g, jt] % NPT][0:n, i * N:(i + 1) * N],
                                           start=(jt == 0), stop=(jt == tiles[-1]))
                mm.then_inc(pv_made, 1)

            def transpose_outputs(w, a, u):
                pe.wait_ge(pv_copied[u], at(w, pv_copied[u], a))
                for i, (c0, c1) in enumerate(XB):
                    job = (f"o{a}x", u, i)
                    fill(w, job)
                    for c in range(c0, c1):
                        mm = pe.transpose(wbank(w, job)[0:N, (c - c0) * P:(c - c0 + 1) * P], pv[u][:, c * N:(c + 1) * N],
                                          identf[:])
                    done(w, mm, job)

            def step(now, x, then, s, after, c):
                def cross(first, end):
                    for hd in range(first, end if x is not None else first):
                        cross_scores(now, x, hd)

                def early(first, end):
                    for hd in range(first, end if s is not None else first):
                        pe.wait_ge(q2T_made[s], at(then, q2T_made[s], 1))
                        cross_scores(then, s, hd)

                if x is not None:
                    pe.wait_ge(q2T_made[x], at(now, q2T_made[x], 2))

                def own_scores(first, end):
                    for g in range(first, end if s is not None else first):
                        pe.wait_ge(q1T_made[s], at(then, q1T_made[s], g // 2 + 1))
                        pe.wait_ge(kT_made[s], at(then, kT_made[s], g // 2 + 1))
                        self_scores(then, s, g)

                def context_stacks(first, end):
                    for i in range(first, end if s is not None else first):
                        pe.wait_ge(stack_c_made[s], at(then, stack_c_made[s], 3))
                        transpose_context_stack(then, s, i)

                own_scores(0, 2)
                cross(EARLY, 9)
                own_scores(2, 4)
                cross(9, 11)
                if s is not None:
                    transpose_max(then, 1, s)
                cross(11, 12)
                if s is not None:
                    project_context(then, s, 0, "kc")
                cross(12, 13)
                if s is not None:
                    project_context(then, s, 0, "vc")
                    scores_for_exp(then, 1, s, 0, 0)
                cross(13, 14)
                if s is not None:
                    scores_for_exp(then, 1, s, 1, 0)
                if c is not None:
                    pe.wait_ge(h_made[c], at(after, h_made[c], 1))
                    transpose_features(after, ("h1", c, 0), c)
                cross(14, 15)
                if s is not None:
                    pe.wait_ge(pv_copied[s], at(then, pv_copied[s], 0))
                    times_v(then, 1, s, 0)
                    scores_for_exp(then, 1, s, 2, 0)
                cross(15, 16)
                if s is not None:
                    times_v(then, 1, s, 1)
                    scores_for_exp(then, 1, s, 3, 0)
                if c is not None:
                    project(after, ("q1", c, 0), c, "q1", 1, halves=(0,))
                cross(16, 17)
                if c is not None:
                    project(after, ("q1", c, 0), c, "q1", 1, halves=(1,))
                if s is not None:
                    times_v(then, 1, s, 2)
                cross(17, 18)
                if s is not None:
                    times_v(then, 1, s, 3)
                    project_context(then, s, 1, "kc")
                cross(18, 19)
                if s is not None:
                    project_context(then, s, 1, "vc")
                cross(19, 20)
                if s is not None:
                    transpose_outputs(then, 1, s)
                if c is not None:
                    project(after, ("k1", c, 0), c, "k1", 1)
                if s is not None:
                    pe.wait_ge(o_normed[s], at(then, o_normed[s], 2))
                    transpose_features(then, ("o1t", s, 0), s)
                if c is not None:
                    project(after, ("v1", c, 0), c, "v1", 1)
                if x is not None:
                    transpose_max(now, 2, x)
                    scores_for_exp(now, 2, x, 0, 0)
                    scores_for_exp(now, 2, x, 0, 1)
                if s is not None:
                    project(then, ("o1", s, 0), s, "o1", 2)
                    project_context(then, s, 2, "kc")
                    project_context(then, s, 2, "vc")
                if x is not None:
                    scores_for_exp(now, 2, x, 0, 2)
                    scores_for_exp(now, 2, x, 1, 0)
                    if s is not None:
                        pe.wait_ge(pv_copied[s], at(then, pv_copied[s], 1))
                    else:
                        pe.wait_ge(pv_copied[1 - x], at(now, pv_copied[1 - x], 2))
                    times_v(now, 2, x, 0)
                    scores_for_exp(now, 2, x, 1, 1)
                    scores_for_exp(now, 2, x, 1, 2)
                if s is not None:
                    pe.wait_ge(h_made[s], at(then, h_made[s], 2))
                    transpose_features(then, ("h2", s, 0), s)
                if x is not None:
                    scores_for_exp(now, 2, x, 2, 0)
                    times_v(now, 2, x, 1)
                    scores_for_exp(now, 2, x, 2, 1)
                if s is not None:
                    project(then, ("q2", s, 0), s, "q2", 3)
                if x is not None:
                    scores_for_exp(now, 2, x, 2, 2)
                context_stacks(0, 2)
                if x is not None:
                    scores_for_exp(now, 2, x, 3, 0)
                    times_v(now, 2, x, 2)
                context_stacks(2, 3)
                if x is not None:
                    scores_for_exp(now, 2, x, 3, 1)
                context_stacks(3, 4)
                if x is not None:
                    scores_for_exp(now, 2, x, 3, 2)
                if s is not None:
                    pe.wait_ge(stack_q_made[s], at(then, stack_q_made[s], 2))
                    transpose_stack(then, "q2t", s, stack_q[s])
                context_stacks(4, 5)
                if x is not None:
                    times_v(now, 2, x, 3)
                context_stacks(5, 6)
                if c is not None:
                    pe.wait_ge(stack_q_made[c], at(after, stack_q_made[c], 1))
                    transpose_stack(after, "q1t", c, stack_q[c])
                if x is not None:
                    transpose_outputs(now, 2, x)
                if c is not None:
                    pe.wait_ge(stack_k_made[c], at(after, stack_k_made[c], 1))
                    transpose_stack(after, "k1t", c, stack_k[c])
                early(0, 2)
                context_stacks(6, 7)
                early(2, 4)
                context_stacks(7, 8)
                if x is not None:
                    pe.wait_ge(o_normed[x], at(now, o_normed[x], 4))
                    transpose_features(now, ("o2t", x, 0), x)
                context_stacks(8, 9)
                early(4, 6)
                context_stacks(9, 10)
                early(6, 7)
                if x is not None:
                    project(now, ("o2", x, 0), x, "o2", None)
                early(7, 8)

            start(pe, *work_ready, *score_ready, *exp_ready, pv_made)
            pe.wait_ge(attn_cleared, 1)
            for m in moments(FIRST, 0):
                step(*m)
            for job in FIRST.work[-NW:]:
                pe.wait_ge(*emptied(When(FIRST, 0), job))
            with pe.Fori(0, NT - 1) as t:
                for m in moments(BODY, t):
                    step(*m)
            for m in moments(LAST, NT - 1):
                step(*m)

        @block.vector
        def _(dve):
            links = [0]

            def link(w, ins):
                links[0] += 1
                ins.then_inc(dve_step, 1)
                dve.wait_ge(dve_step, at(w, dve_step, links[0]))

            def centre(w, u, a, src):
                link(w, nc.vector.bn_stats(stats[u][:], src[:]))
                nc.vector.memset(spacer[0:1, :], 0.0)
                nc.vector.bn_aggr(mv[u][:], stats[u][:]).then_inc(stats_made[u], 1)
                dve.wait_ge(stats_made[u], at(w, stats_made[u], a))
                link(w, nc.vector.scalar_tensor_tensor(out=centred[u][:], in0=src[:], scalar=mv[u][:, 0:1],
                                                       in1=vec[f"n{a}_g"][:], op0=ALU.subtract, op1=ALU.mult))

            def normalise(w, u, a):
                b = vec[f"n{a}_b"]
                dve.wait_ge(rstd_made[u], at(w, rstd_made[u], a))
                nc.vector.scalar_tensor_tensor(out=h[u][:, D:D + 64], in0=centred[u][:, 2 * P:D], scalar=rstd[u][:],
                                               in1=b[:, 2 * P:D], op0=ALU.mult, op1=ALU.add)
                nc.vector.scalar_tensor_tensor(out=h[u][:, 0:D], in0=centred[u][:], scalar=rstd[u][:],
                                               in1=b[:], op0=ALU.mult, op1=ALU.add).then_inc(h_made[u], 1)

            def lows(w, job, u, n):
                highs, made = (hi_made[u], lo_made[u]) if n else (o2_hi_made[u], o2_lo_made[u])
                dve.wait_ge(highs, at(w, highs, n or 1))
                v = wbank(w, job)[:, 0:3 * N].rearrange("p (k n) -> p k n", k=3)
                nc.vector.tensor_tensor(t_hi[u][64:P, 2, :], v[64:P, 2, :], t_hi[u][64:P, 2, :].bitcast(F32),
                                        ALU.subtract)
                nc.vector.tensor_tensor(t_lo[u][:], v[:, 0:2, :], t_hi[u][:, 0:2, :].bitcast(F32),
                                        ALU.subtract).then_inc(made, 1)

            def rest(w, job, n, first, dst, made):
                nc.vector.tensor_tensor(heads(dst[:]), heads(wbank(w, job)[0:n, 0:D]), first,
                                        ALU.subtract).then_inc(made, 1)

            def rest_q_of(w, kind, u, n):
                dve.wait_ge(p0_q_made[u], at(w, p0_q_made[u], n))
                rest(w, (kind, u, 0), N, stack_q[u][:, :, 0, :], rest_q[u], rest_q_made[u])

            def rest_c_of(w, u, i):
                dve.wait_ge(p0_c_made[u], at(w, p0_c_made[u], i + 1))
                rest(w, ("kc", u, i), JT[i][1], stack_c[i][:, :, 0, :], rest_c[i], rest_c_made[u])

            def copy_q(w, kind, u, made):
                for i in range(2):
                    job = (kind, u, i)
                    dve.wait_ge(*filled(w, job))
                    nc.vector.tensor_copy(qT[u][0:KS, i * HB:(i + 1) * HB, :],
                                          wbank16(w, job)[0:KS, 0:HB * N].rearrange("p (h n) -> p h n", h=HB))\
                        .then_inc(made, 1)

            def maxima(w, a, u, i):
                k, n = w.plan.score_at[a, u, i]
                dve.wait_ge(score_ready[k], at(w, score_ready[k], n + 1))
                if a == 1:
                    dst, src = neg_max[u][:, i * HG:(i + 1) * HG], \
                        score[k][0:N, 0:HG * N].rearrange("p (h j) -> p h j", h=HG)
                else:
                    dst, src = neg_max[u][:, i:i + 1], score[k][0:N, 0:J]
                nc.vector.tensor_reduce(dst, src, AX_X, ALU.max, negate=True).then_inc(max_made[u], 1)

            def divide(w, a, u):
                for i, (c0, c1) in enumerate(XB):
                    job = (f"o{a}x", u, i)
                    dve.wait_ge(*filled(w, job))
                    h0, h1 = c0 * QH, c1 * QH
                    o = wbank(w, job)[0:N, 0:(c1 - c0) * P].rearrange("p (h d) -> p h d", d=32)
                    link(w, nc.vector.reciprocal(rden[u][:, h0:h1].unsqueeze(2), o[:, :, DH:D1]))
                    r = rden[u][:, h0:h1].unsqueeze(2).broadcast_to([N, h1 - h0, DH])
                    if h1 == H:
                        nc.vector.tensor_tensor(heads(h[u][:, D:D + 64]), o[:, 16 - h0:, 0:DH], r[:, 16 - h0:, :],
                                                ALU.mult)
                    nc.vector.tensor_tensor(heads(h[u][:, h0 * DH:h1 * DH]), o[:, :, 0:DH], r,
                                            ALU.mult).then_inc(o_normed[u], 1)

            def add_residual(w, a, u, dst, made):
                job = (f"o{a}", u, 0)
                dve.wait_ge(*filled(w, job))
                dve.wait_ge(xres_made[u], at(w, xres_made[u], a))
                nc.vector.tensor_tensor(dst[:], wbank(w, job)[0:N, 0:D], xres[u][:], ALU.add).then_inc(made, 1)

            def copy_context(w, u, i):
                job = ("kct", u, i)
                dve.wait_ge(*filled(w, job))
                nc.vector.tensor_copy(kcT[u][0:KS, 2 * i:2 * i + 2, 0:J],
                                      wbank16(w, job)[0:KS, 0:2 * JP].rearrange("p (h j) -> p h j", h=2)[:, :, 0:J])\
                    .then_inc(kcT_odd_made[u], 1)

            def step(now, x, then, s, after, c):
                def early_maxima(first, end):
                    for hd in range(first, end if s is not None else first):
                        maxima(then, 2, s, hd)

                def own_maxima(first, end):
                    for g in range(first, end if s is not None else first):
                        maxima(then, 1, s, g)

                def cross_maxima(first, end):
                    for hd in range(first, end if x is not None else first):
                        maxima(now, 2, x, hd)

                own_maxima(0, 2)
                cross_maxima(EARLY, 9)
                own_maxima(2, 4)
                cross_maxima(9, 11)
                cross_maxima(11, 12)
                if c is not None:
                    dve.wait_ge(x_landed[c], at(after, x_landed[c], 16))
                    centre(after, c, 1, xin[c])
                cross_maxima(12, 13)
                if s is not None:
                    rest_c_of(then, s, 0)
                if c is not None:
                    normalise(after, c, 1)
                cross_maxima(13, 15)
                if c is not None:
                    lows(after, ("h1", c, 0), c, 1)
                cross_maxima(15, 17)
                if c is not None:
                    rest_q_of(after, "q1", c, 1)
                cross_maxima(17, 19)
                if s is not None:
                    rest_c_of(then, s, 1)
                cross_maxima(19, 20)
                if s is not None:
                    divide(then, 1, s)
                if c is not None:
                    dve.wait_ge(p0_k_made[c], at(after, p0_k_made[c], 1))
                    rest(after, ("k1", c, 0), N, stack_k[c][:, :, 0, :], rest_k[c], rest_k_made[c])
                if s is not None:
                    lows(then, ("o1t", s, 0), s, 2)
                if s is not None:
                    add_residual(then, 1, s, x1[s], x1_made[s])
                    dve.wait_ge(x1_made[s], at(then, x1_made[s], 1))
                    centre(then, s, 2, x1[s])
                    rest_c_of(then, s, 2)
                    normalise(then, s, 2)
                    lows(then, ("h2", s, 0), s, 3)
                    rest_q_of(then, "q2", s, 2)
                    copy_context(then, s, 1)
                    copy_context(then, s, 3)
                    copy_q(then, "q2t", s, q2T_made[s])
                    copy_context(then, s, 5)
                if c is not None:
                    copy_q(after, "q1t", c, q1T_made[c])
                if x is not None:
                    divide(now, 2, x)
                early_maxima(0, 4)
                if s is not None:
                    copy_context(then, s, 7)
                if x is not None:
                    lows(now, ("o2t", x, 0), x, None)
                early_maxima(4, 6)
                if s is not None:
                    copy_context(then, s, 9)
                early_maxima(6, 7)
                if x is not None:
                    dve.wait_ge(x2_stored[x], at(now, x2_stored[x], 0))
                    add_residual(now, 2, x, x2[x], x2_made[x])
                early_maxima(7, 8)

            start(dve, dve_step, *kcT_odd_made, *lo_made, *o2_lo_made, *rest_q_made, *rest_k_made, *rest_c_made,
                  *q1T_made, *q2T_made, *max_made, *o_normed, *x1_made, *x2_made)
            nc.vector.memset(attn[:, :], 0.0).then_inc(attn_cleared, 1)
            for m in moments(FIRST, 0):
                step(*m)
            assert links[0] == DVE_STEPS["first"], links
            links[0] = 0
            with dve.Fori(0, NT - 1) as t:
                for m in moments(BODY, t):
                    step(*m)
            assert links[0] == DVE_STEPS["body"], links
            links[0] = 0
            for m in moments(LAST, NT - 1):
                step(*m)

        @block.scalar
        def _(act):
            def high(w, job, u, made):
                act.wait_ge(*filled(w, job))
                nc.scalar.copy(t_hi[u][:], wbank(w, job)[:, 0:3 * N].rearrange("p (k n) -> p k n", k=3))\
                    .then_inc(made, 1)

            def first_q(w, kind, u):
                job = (kind, u, 0)
                act.wait_ge(*filled(w, job))
                src = wbank(w, job)[0:N, 0:D]
                nc.scalar.copy(q_slots(stack_q[u], "last"), heads(src))
                nc.scalar.copy(q_slots(stack_q[u], 0), repeated(src, N, 2)).then_inc(p0_q_made[u], 1)

            def first_k(w, job, n, stack, made):
                act.wait_ge(*filled(w, job))
                nc.scalar.copy(k_slots(stack, 0), repeated(wbank(w, job)[0:n, 0:D], n, 3)).then_inc(made, 1)

            def copy_v(w, job, n, dst, made):
                act.wait_ge(*filled(w, job))
                nc.scalar.copy(dst[:, :, 0:DH], heads(wbank(w, job)[0:n, 0:D])).then_inc(made, 1)

            def context_parts(w, u, i):
                n = JT[i][1]
                first_k(w, ("kc", u, i), n, stack_c[i], p0_c_made[u])
                copy_v(w, ("vc", u, i), n, vc[u][0:n, i], vc_made[u])

            def exponentials(w, a, u, g, jt):
                e = w.plan.exp_at[a, u, g, jt]
                n = JT[jt][1] if a == 2 else N
                act.wait_ge(exp_ready[e % 2], at(w, exp_ready[e % 2], e // 2 + 1))
                act.wait_ge(pv_made, at(w, pv_made, w.plan.pv_before((a, u, g, jt))))
                nc.scalar.activation(probs[e % NPT][0:n, :], expin[e % 2][0:n, 0:HG * N], ACT.Exp,
                                     scale=SCALE).then_inc(probs_made, 1)

            def copy_product(w, a, u):
                act.wait_ge(pv_made, at(w, pv_made, w.plan.pv.index((a, u, G - 1)) + 1))
                nc.scalar.copy(pv[u][:], attn[:, 0:HC * N]).then_inc(pv_copied[u], 1)

            def copy_max(w, a, u):
                for i in range(2):
                    job = (f"m{a}t", u, i)
                    act.wait_ge(*filled(w, job))
                    nc.scalar.copy(qT[u][KS:KM, i * HB:(i + 1) * HB, :],
                                          wbank16(w, job)[KS:KM, 0:HB * N].rearrange("p (h n) -> p h n", h=HB))\
                        .then_inc(mT_made[u], 1)

            def copy_stack(w, kind, u, dst, made):
                for i in range(2):
                    job = (kind, u, i)
                    act.wait_ge(*filled(w, job))
                    nc.scalar.copy(dst[0:KS, i * HB:(i + 1) * HB, :],
                                   wbank16(w, job)[0:KS, 0:HB * N].rearrange("p (h n) -> p h n", h=HB))\
                        .then_inc(made, 1)

            def copy_context(w, u, i):
                job = ("kct", u, i)
                act.wait_ge(*filled(w, job))
                nc.scalar.copy(kcT[u][0:KS, 2 * i:2 * i + 2, 0:J],
                               wbank16(w, job)[0:KS, 0:2 * JP].rearrange("p (h j) -> p h j", h=2)[:, :, 0:J])\
                    .then_inc(kcT_made[u], 1)

            def step(now, x, then, s, after, c):
                def cross_exponentials(*tiles):
                    for g, jt in tiles if x is not None else ():
                        exponentials(now, 2, x, g, jt)

                if s is not None:
                    copy_max(then, 1, s)
                    context_parts(then, s, 0)
                    exponentials(then, 1, s, 0, 0)
                    exponentials(then, 1, s, 1, 0)
                if c is not None:
                    high(after, ("h1", c, 0), c, hi_made[c])
                if s is not None:
                    exponentials(then, 1, s, 2, 0)
                    exponentials(then, 1, s, 3, 0)
                if c is not None:
                    first_q(after, "q1", c)
                if s is not None:
                    copy_product(then, 1, s)
                    context_parts(then, s, 1)
                if c is not None:
                    first_k(after, ("k1", c, 0), N, stack_k[c], p0_k_made[c])
                if s is not None:
                    high(then, ("o1t", s, 0), s, hi_made[s])
                if c is not None:
                    copy_v(after, ("v1", c, 0), N, vs[c], v_made[c])
                if x is not None:
                    copy_max(now, 2, x)
                cross_exponentials((0, 0), (0, 1))
                if s is not None:
                    context_parts(then, s, 2)
                cross_exponentials((0, 2), (1, 0), (1, 1), (1, 2))
                if s is not None:
                    high(then, ("h2", s, 0), s, hi_made[s])
                cross_exponentials((2, 0), (2, 1))
                if s is not None:
                    first_q(then, "q2", s)
                cross_exponentials((2, 2))
                if s is not None:
                    copy_context(then, s, 0)
                cross_exponentials((3, 0))
                if s is not None:
                    copy_context(then, s, 2)
                cross_exponentials((3, 1), (3, 2))
                if s is not None:
                    copy_context(then, s, 4)
                if x is not None:
                    copy_product(now, 2, x)
                if c is not None:
                    copy_stack(after, "k1t", c, kT[c], kT_made[c])
                if s is not None:
                    copy_context(then, s, 6)
                if x is not None:
                    high(now, ("o2t", x, 0), x, o2_hi_made[x])
                if s is not None:
                    copy_context(then, s, 8)

            start(act, probs_made, *pv_copied, *v_made, *vc_made, *mT_made, *kT_made, *kcT_made)
            for m in moments(FIRST, 0):
                step(*m)
            with act.Fori(0, NT - 1) as t:
                for m in moments(BODY, t):
                    step(*m)
            for m in moments(LAST, NT - 1):
                step(*m)

        @block.gpsimd
        def _(pool):
            links = [0]

            def link(w, ins):
                links[0] += 1
                ins.then_inc(pool_step, 1)
                pool.wait_ge(pool_step, at(w, pool_step, links[0]))

            def inverse_deviation(w, u, a):
                pool.wait_ge(stats_made[u], at(w, stats_made[u], a))
                link(w, nc.gpsimd.tensor_tensor(var_eps[u][:], mv[u][:, 1:2], eps[0:N, :], ALU.add))
                nc.gpsimd.tensor_tensor(rstd[u][:], var_eps[u][:], neg_half[0:N, :], ALU.pow)\
                    .then_inc(rstd_made[u], 1)

            def residual(w, u, a, src):
                nc.gpsimd.tensor_tensor(xres[u][:], src[:], vec[f"o{a}_b"][:], ALU.add).then_inc(xres_made[u], 1)

            def split_context(w, after, u):
                pool.wait_ge(ctx_landed[u], at(after, ctx_landed[u], 48))
                link(w, nc.gpsimd.tensor_tensor(ctx_hi[:], ctx_raw[u][:], one[:].unsqueeze(2).broadcast_to([P, 2, J]),
                                                ALU.mult))
                link(w, nc.gpsimd.tensor_tensor(ctx_hi[64:P, 1, :], ctx_raw[u][64:P, 1, :],
                                                ctx_hi[64:P, 1, :].bitcast(F32), ALU.subtract))
                nc.gpsimd.tensor_tensor(ctx_lo[:], ctx_raw[u][:, 0, :], ctx_hi[:, 0, :].bitcast(F32),
                                        ALU.subtract).then_inc(ctx_split[u], 1)

            def more_parts(w, slots, stack, rest, n, made):
                link(w, nc.gpsimd.tensor_tensor(slots(stack, 1), repeated(rest[:], n, 2),
                                                one[0:n, :].unsqueeze(2).unsqueeze(3).broadcast_to([n, H, 2, DH]), ALU.mult))
                second = 1 if slots is q_slots else 3
                nc.gpsimd.tensor_tensor(slots(stack, 2), heads(rest[:]), stack[:, :, second, :], ALU.subtract)\
                    .then_inc(made, 1)

            def more_parts_q(w, u, n):
                pool.wait_ge(rest_q_made[u], at(w, rest_q_made[u], n))
                more_parts(w, q_slots, stack_q[u], rest_q[u], N, stack_q_made[u])

            def more_parts_c(w, u, i):
                pool.wait_ge(rest_c_made[u], at(w, rest_c_made[u], i + 1))
                more_parts(w, k_slots, stack_c[i], rest_c[i], JT[i][1], stack_c_made[u])

            def split_maxima(w, a, u, i):
                pool.wait_ge(max_made[u], at(w, max_made[u], (i + 1) * 2 if a == 1 else G + (i + 1) * HB))
                c = slice(i * HB, (i + 1) * HB)
                ones = one[0:N, :].broadcast_to([N, HB])
                m, r, parts = neg_max[u][:, c], max_rest[u][:, c], max_parts[u][:, c, :]
                link(w, nc.gpsimd.tensor_tensor(parts[:, :, 0], m, ones, ALU.mult))
                link(w, nc.gpsimd.tensor_tensor(r, m, parts[:, :, 0], ALU.subtract))
                link(w, nc.gpsimd.tensor_tensor(parts[:, :, 1], r, ones, ALU.mult))
                nc.gpsimd.tensor_tensor(parts[:, :, 2], r, parts[:, :, 1], ALU.subtract).then_inc(parts_made[u], 1)

            def step(now, x, then, s, after, c):
                if s is not None:
                    for i in range(2):
                        split_maxima(then, 1, s, i)
                if c is not None:
                    inverse_deviation(after, c, 1)
                if s is not None:
                    more_parts_c(then, s, 0)
                if x is not None:
                    split_maxima(now, 2, x, 0)
                if c is not None:
                    more_parts_q(after, c, 1)
                if x is not None:
                    split_maxima(now, 2, x, 1)
                if s is not None:
                    pool.wait_ge(x2_made[s], at(then, x2_made[s], 0))
                    residual(then, s, 1, xin[s])
                    more_parts_c(then, s, 1)
                    inverse_deviation(then, s, 2)
                    residual(then, s, 2, x1[s])
                    more_parts_c(then, s, 2)
                    more_parts_q(then, s, 2)
                if c is not None:
                    pool.wait_ge(rest_k_made[c], at(after, rest_k_made[c], 1))
                    more_parts(after, k_slots, stack_k[c], rest_k[c], N, stack_k_made[c])
                    if s is not None:
                        pool.wait_ge(*filled(then, ("vc", s, 2)))
                    split_context(now, after, c)

            start(pool, pool_step)
            for m in moments(FIRST, 0):
                step(*m)
            assert links[0] == POOL_STEPS["first"], links
            links[0] = 0
            with pool.Fori(0, NT - 1) as t:
                for m in moments(BODY, t):
                    step(*m)
            assert links[0] == POOL_STEPS["body"], links
            links[0] = 0
            for m in moments(LAST, NT - 1):
                step(*m)


def make_identity(nc, pool, ident, step):
    nc.gpsimd.memset(ident[:], 0.0).then_inc(step, 1)
    pool.wait_ge(step, 1)
    nc.gpsimd.affine_select(out=ident[:], in_=ident[:], compare_op=ALU.not_equal, fill=1.0, base=0,
                            pattern=[[-1, P]], channel_multiplier=1).then_inc(step, 1)


TT = 5
NF = B * N // (P * TT)
FT = FF // P
W = TT * P // 2
FV_STEPS, FP_STEPS = 2 * TT, TT


def feed_forward_phase(nc, x2, n3_g, n3_b, ff_w1, ff_b1, ff_w2, ff_b2, out):
    with ExitStack() as ctx:
        def sb(name, shape, dt=F32):
            return ctx.enter_context(nc.sbuf_tensor(name, shape, dt))

        w1_hi, w1_lo = sb("w1_hi", [P, 3, 2 * FF], F32R), sb("w1_lo", [P, 3, 2 * FF], F32R)
        w2_hi, w2_lo = sb("w2_hi", [P, FT, D], F32R), sb("w2_lo", [P, FT, D], F32R)
        vectors = {"g": n3_g, "b": n3_b, "ff_b2": ff_b2}
        vec = {k: sb(f"{k}3_rows", [P, D]) for k in vectors}
        b1 = sb("b1_cols", [P, 2 * FT])
        identf = sb("identf3", [P, P])
        neg_half, eps = sb("neg_half3", [P, 1]), sb("eps3", [P, 1])

        CB = 640
        with ExitStack() as prep:
            NB1 = 2 * FF // CB
            raw = [prep.enter_context(nc.sbuf_tensor(f"w1_raw{i}", [P, 3, CB], F32)) for i in range(NB1)]
            w2_raw = [prep.enter_context(nc.sbuf_tensor(f"w2_raw{i}", [P, FT // 2, D], F32)) for i in range(2)]
            w1_landed = [prep.enter_context(nc.semaphore(f"w1_landed{i}")) for i in range(NB1)]
            w2_landed = [prep.enter_context(nc.semaphore(f"w2_landed{i}")) for i in range(2)]
            vectors_landed = prep.enter_context(nc.semaphore("vectors3_landed"))
            w_hi_made = prep.enter_context(nc.semaphore("w_hi_made"))
            ident_step = prep.enter_context(nc.semaphore("ident3_step"))
            block = prep.enter_context(nc.Block())

            @block.sync
            def _(sp):
                for i in range(NB1):
                    w = ff_w1[:, i * CB:(i + 1) * CB]
                    for p0, p1, tile, src in rows3(w):
                        sp.dma_start(raw[i][p0:p1, tile, :], src).then_inc(w1_landed[i], 16)
                    if i < 2:
                        sp.dma_start(w2_raw[i][:], ff_w2.rearrange("(h k p) n -> h p k n", h=2, p=P)[i])\
                            .then_inc(w2_landed[i], 16)
                for k, v in vectors.items():
                    sp.dma_start(vec[k][:], v.rearrange("(a d) -> a d", a=1).broadcast_to([P, D]))\
                        .then_inc(vectors_landed, 16)
                with nc.allow_non_contiguous_dma("a bias, once"):
                    sp.dma_start(b1[:], ff_b1.rearrange("(k p) -> p k", p=P)).then_inc(vectors_landed, 16)
                sp.wait_ge(vectors_landed, 16 * (len(vectors) + 1))

            @block.scalar
            def _(act):
                for i in range(NB1):
                    act.wait_ge(w1_landed[i], 64)
                    nc.scalar.copy(w1_hi[:, :, i * CB:(i + 1) * CB], raw[i][:]).then_inc(w_hi_made, 1)
                for i in range(2):
                    act.wait_ge(w2_landed[i], 16)
                    c = slice(i * (FT // 2), (i + 1) * (FT // 2))
                    nc.scalar.copy(w2_hi[:, c, :], w2_raw[i][:]).then_inc(w_hi_made, 1)

            @block.vector
            def _(dve):
                nc.vector.memset(neg_half[:], -0.5)
                nc.vector.memset(eps[:], EPS)
                for i in range(NB1):
                    dve.wait_ge(w_hi_made, i + 1)
                    c = slice(i * CB, (i + 1) * CB)
                    nc.vector.tensor_tensor(w1_lo[:, :, c], raw[i][:], w1_hi[:, :, c].bitcast(F32),
                                            ALU.subtract)
                for i in range(2):
                    dve.wait_ge(w_hi_made, NB1 + i + 1)
                    c = slice(i * (FT // 2), (i + 1) * (FT // 2))
                    nc.vector.tensor_tensor(w2_lo[:, c, :], w2_raw[i][:], w2_hi[:, c, :].bitcast(F32), ALU.subtract)

            @block.gpsimd
            def _(pool):
                make_identity(nc, pool, identf, ident_step)

        spacer = sb("spacer3", [P, 1])
        xt = [sb(f"xt{i}", [P, D]) for i in range(TT)]
        xb = [sb(f"xb{i}", [P, D]) for i in range(TT)]
        yt = [sb(f"yt{i}", [P, D]) for i in range(2)]
        h = [sb(f"h3_{i}", [P, D + 64]) for i in range(2)]
        centred = [sb(f"centred3_{i}", [P, D]) for i in range(2)]
        stats = [sb(f"stats3_{i}", [P, 6]) for i in range(TT)]
        mv = [sb(f"mv3_{i}", [P, 2]) for i in range(TT)]
        var_eps = [sb(f"var_eps3_{i}", [P, 1]) for i in range(TT)]
        rstd = [sb(f"rstd3_{i}", [P, 1]) for i in range(TT)]
        t_hi = sb("t3_hi", [P, 3, TT * P], F32R)
        t_lo = sb("t3_lo", [P, 2, TT * P], F32R)
        gelu = [sb(f"gelu{i}", [P, W]) for i in range(2)]
        hidden = [sb(f"hidden{i}", [P, W]) for i in range(2)]
        hid_hi, hid_lo = sb("hid_hi", [P, FT, TT * P], F32R), sb("hid_lo", [P, FT, TT * P], F32R)

        turn = [ctx.enter_context(nc.psum_tensor(f"turn{i}", [P, 512], F32)) for i in range(2)]
        ps_a = [ctx.enter_context(nc.psum_tensor(f"ps_a{i}", [P, 512], F32)) for i in range(2)]
        ps_g = [ctx.enter_context(nc.psum_tensor(f"ps_g{i}", [P, 512], F32)) for i in range(2)]
        ps_y = [ctx.enter_context(nc.psum_tensor(f"ps_y{i}", [P, 512], F32)) for i in range(2)]

        PER, START = {}, {}

        def sem(name, per, first=0):
            s = ctx.enter_context(nc.semaphore(name))
            PER[s], START[s] = per, first
            return s

        def start(eng, *sems):
            for s in sems:
                eng.sem_inc(s, START[s])

        def at(t, s, n):
            assert n > 0 or START[s] > 0, s
            return t * PER[s] + (START[s] + n)

        NU = 2 * FT
        xt_landed = [sem(f"xt_landed{i}", 16) for i in range(TT)]
        y_stored = [sem(f"y_stored{i}", 16 * [3, 2][i], 16) for i in range(2)]
        stats_made, h_made, lo_made, hidden_made, y_made = (
            sem("stats3_made", TT), sem("h3_made", TT), sem("lo3_made", TT, 1), sem("hidden_made", NU, 1), sem("y_made", TT, 1))
        rstd_made, xb_made, hid_lo_made = sem("rstd3_made", TT), sem("xb_made", TT), sem("hid_lo_made", NU, 1)
        hi_made, gelu_made, hid_hi_made = sem("hi3_made", TT), sem("gelu_made", NU), sem("hid_hi_made", NU)
        turned, g_ready, a_ready, y_ready = sem("turned", TT, 1), sem("g_ready", NU), sem("a_ready", NU), sem("y_ready", TT)
        dve_step, pool_step = sem("dve3_step", FV_STEPS), sem("pool3_step", FP_STEPS)

        x2_tiles = x2.rearrange("(t i p) d -> t i p d", i=TT, p=P)
        out_tiles = out.rearrange("(t i p) d -> t i p d", i=TT, p=P)
        block = ctx.enter_context(nc.Block())

        @block.sync
        def _(sp):
            def load(t, i):
                sp.dma_start(xt[i][:], x2_tiles[t, i]).then_inc(xt_landed[i], 16)

            def store(t, i):
                sp.wait_ge(y_made, at(t, y_made, i + 1))
                sp.dma_start(out_tiles[t, i], yt[i % 2][:]).then_inc(y_stored[i % 2], 16)

            start(sp, *y_stored)
            for i in range(TT):
                load(0, i)
            with sp.Fori(0, NF - 1) as t:
                for i in range(TT):
                    sp.wait_ge(h_made, at(t, h_made, i + 1))
                    sp.wait_ge(xb_made, at(t, xb_made, i + 1))
                    load(t + 1, i)
                for i in range(TT):
                    store(t, i)
            for i in range(TT):
                store(NF - 1, i)
            for i in range(2):
                sp.wait_ge(y_stored[i], at(NF - 1, y_stored[i], PER[y_stored[i]]))

        @block.tensor
        def _(pe):
            def turn_tile(t, i):
                pe.wait_ge(lo_made, at(t, lo_made, max(i - 1, 0)))
                pe.wait_ge(h_made, at(t, h_made, i + 1))
                for k in range(3):
                    mm = pe.transpose(turn[i % 2][:, k * P:(k + 1) * P], h[i % 2][:, k * P:(k + 1) * P], identf[:])
                mm.then_inc(turned, 1)

            def first_layer(t):
                for half in range(2):
                    for f in range(FT):
                        n = half * FT + f
                        c = slice(half * W, (half + 1) * W)
                        pe.wait_ge(lo_made, at(t, lo_made, [3, TT][half]))
                        for bank, f0, ready in ((ps_g[n % 2], FT + f, g_ready), (ps_a[n % 2], f, a_ready)):
                            pe.wait_ge(hidden_made, at(t, hidden_made, max(n - 1, 0)))
                            w = slice(f0 * P, (f0 + 1) * P)
                            passes = [(w1_hi[:, 0, w], t_hi[:, 0, c]), (w1_lo[:, 0, w], t_hi[:, 0, c]),
                                      (w1_hi[:, 1, w], t_hi[:, 1, c]), (w1_lo[:, 1, w], t_hi[:, 1, c]),
                                      (w1_hi[:, 0, w], t_lo[:, 0, c]), (w1_hi[:, 1, w], t_lo[:, 1, c]),
                                      (w1_hi[:, 2, w], t_hi[:, 2, c]), (w1_lo[:, 2, w], t_hi[:, 2, c])]
                            for k, (a, b) in enumerate(passes):
                                mm = pe.matmul(bank[:, 0:W], a, b, start=(k == 0), stop=(k == len(passes) - 1))
                            mm.then_inc(ready, 1)

            def second_layer(t, i):
                pe.wait_ge(y_made, at(t, y_made, max(i - 1, 0)))
                pe.wait_ge(hid_hi_made, at(t, hid_hi_made, FT if i < 2 else NU))
                pe.wait_ge(hid_lo_made, at(t, hid_lo_made, FT if i < 2 else NU))
                y, c = ps_y[i % 2][:, 0:D], slice(i * P, (i + 1) * P)
                for f in range(FT):
                    pe.matmul(y, hid_hi[:, f, c], w2_hi[:, f, :], start=(f == 0), stop=False)
                    pe.matmul(y, hid_hi[:, f, c], w2_lo[:, f, :], start=False, stop=False)
                    mm = pe.matmul(y, hid_lo[:, f, c], w2_hi[:, f, :], start=False, stop=(f == FT - 1))
                mm.then_inc(y_ready, 1)

            start(pe, turned)
            for i in range(TT):
                turn_tile(0, i)
            with pe.Fori(0, NF - 1) as t:
                first_layer(t)
                for i in range(TT):
                    second_layer(t, i)
                    turn_tile(t + 1, i)
            first_layer(NF - 1)
            for i in range(TT):
                second_layer(NF - 1, i)

        @block.vector
        def _(dve):
            def link(t, ins, n):
                ins.then_inc(dve_step, 1)
                dve.wait_ge(dve_step, at(t, dve_step, n))

            def split_low(t, i):
                dve.wait_ge(hi_made, at(t, hi_made, i + 1))
                c = slice(i * P, (i + 1) * P)
                v = turn[i % 2][:, 0:3 * P].rearrange("p (k n) -> p k n", k=3)
                nc.vector.tensor_tensor(t_hi[64:P, 2, c], v[64:P, 2, :], t_hi[64:P, 2, c].bitcast(F32), ALU.subtract)
                nc.vector.tensor_tensor(t_lo[:, :, c], v[:, 0:2, :], t_hi[:, 0:2, c].bitcast(F32),
                                        ALU.subtract).then_inc(lo_made, 1)

            def statistics(t, i):
                dve.wait_ge(xt_landed[i], at(t, xt_landed[i], 16))
                link(t, nc.vector.bn_stats(stats[i][:], xt[i][:]), i + 1)
                nc.vector.memset(spacer[0:1, :], 0.0)
                nc.vector.bn_aggr(mv[i][:], stats[i][:]).then_inc(stats_made, 1)

            def normalise(t, i):
                hb = h[i % 2]
                dve.wait_ge(turned, at(t, turned, max(i - 1, 0)))
                dve.wait_ge(stats_made, at(t, stats_made, i + 1))
                link(t, nc.vector.scalar_tensor_tensor(out=centred[i % 2][:], in0=xt[i][:], scalar=mv[i][:, 0:1],
                                                       in1=vec["g"][:], op0=ALU.subtract, op1=ALU.mult), TT + i + 1)
                dve.wait_ge(rstd_made, at(t, rstd_made, i + 1))
                nc.vector.scalar_tensor_tensor(out=hb[:, D:D + 64], in0=centred[i % 2][:, 2 * P:D], scalar=rstd[i][:],
                                               in1=vec["b"][:, 2 * P:D], op0=ALU.mult, op1=ALU.add)
                nc.vector.scalar_tensor_tensor(out=hb[:, 0:D], in0=centred[i % 2][:], scalar=rstd[i][:],
                                               in1=vec["b"][:], op0=ALU.mult, op1=ALU.add).then_inc(h_made, 1)

            def hidden_features(t):
                for n in range(NU):
                    dve.wait_ge(a_ready, at(t, a_ready, n + 1))
                    dve.wait_ge(gelu_made, at(t, gelu_made, n + 1))
                    dve.wait_ge(hid_lo_made, at(t, hid_lo_made, max(n - 1, 0)))
                    nc.vector.scalar_tensor_tensor(out=hidden[n % 2][:], in0=ps_a[n % 2][:, 0:W],
                                                   scalar=b1[:, n % FT:n % FT + 1], in1=gelu[n % 2][:],
                                                   op0=ALU.add, op1=ALU.mult).then_inc(hidden_made, 1)

            def result(t, i):
                dve.wait_ge(y_ready, at(t, y_ready, i + 1))
                dve.wait_ge(xb_made, at(t, xb_made, i + 1))
                dve.wait_ge(y_stored[i % 2], at(t, y_stored[i % 2], 16 * (i // 2)))
                nc.vector.tensor_tensor(yt[i % 2][:], ps_y[i % 2][:, 0:D], xb[i][:], ALU.add).then_inc(y_made, 1)

            start(dve, lo_made, hidden_made, y_made)
            for i in range(TT):
                statistics(0, i)
            for i in range(TT):
                normalise(0, i)
                if i:
                    split_low(0, i - 1)
            split_low(0, TT - 1)
            with dve.Fori(0, NF - 1) as t:
                hidden_features(t)
                for i in range(TT):
                    statistics(t + 1, i)
                for i in range(2):
                    normalise(t + 1, i)
                for i in range(TT):
                    result(t, i)
                    split_low(t + 1, i)
                    if i + 2 < TT:
                        normalise(t + 1, i + 2)
            hidden_features(NF - 1)
            for i in range(TT):
                result(NF - 1, i)

        @block.scalar
        def _(act):
            def features(n):
                half, f = n // FT, n % FT
                return f, slice(half * W, (half + 1) * W)

            def split_high(t, n):
                f, c = features(n)
                act.wait_ge(hidden_made, at(t, hidden_made, n + 1))
                nc.scalar.copy(hid_hi[:, f, c], hidden[n % 2][:]).then_inc(hid_hi_made, 1)

            def high(t, i):
                act.wait_ge(turned, at(t, turned, i + 1))
                nc.scalar.copy(t_hi[:, :, i * P:(i + 1) * P],
                               turn[i % 2][:, 0:3 * P].rearrange("p (k n) -> p k n", k=3)).then_inc(hi_made, 1)

            def gelus(t):
                for n in range(NU):
                    act.wait_ge(g_ready, at(t, g_ready, n + 1))
                    act.wait_ge(hidden_made, at(t, hidden_made, max(n - 1, 0)))
                    f = n % FT
                    nc.scalar.activation(gelu[n % 2][:], ps_g[n % 2][:, 0:W], ACT.Gelu,
                                         bias=b1[:, FT + f:FT + f + 1]).then_inc(gelu_made, 1)
                    if n:
                        split_high(t, n - 1)
                split_high(t, NU - 1)

            for i in range(TT):
                high(0, i)
            with act.Fori(0, NF - 1) as t:
                gelus(t)
                for i in range(TT):
                    high(t + 1, i)
            gelus(NF - 1)

        @block.gpsimd
        def _(pool):
            def link(t, ins, n):
                ins.then_inc(pool_step, 1)
                pool.wait_ge(pool_step, at(t, pool_step, n))

            start(pool, hid_lo_made)
            def front(t):
                for i in range(TT):
                    pool.wait_ge(stats_made, at(t, stats_made, i + 1))
                    link(t, nc.gpsimd.tensor_tensor(var_eps[i][:], mv[i][:, 1:2], eps[:], ALU.add), i + 1)
                    nc.gpsimd.tensor_tensor(rstd[i][:], var_eps[i][:], neg_half[:], ALU.pow).then_inc(rstd_made, 1)
                pool.wait_ge(y_made, at(t, y_made, 0))
                for i in range(TT):
                    pool.wait_ge(xt_landed[i], at(t, xt_landed[i], 16))
                    nc.gpsimd.tensor_tensor(xb[i][:], xt[i][:], vec["ff_b2"][:], ALU.add).then_inc(xb_made, 1)

            def low_hidden(t):
                for n in range(NU):
                    half, f = n // FT, n % FT
                    c = slice(half * W, (half + 1) * W)
                    pool.wait_ge(hid_hi_made, at(t, hid_hi_made, n + 1))
                    nc.gpsimd.tensor_tensor(hid_lo[:, f, c], hidden[n % 2][:], hid_hi[:, f, c].bitcast(F32),
                                            ALU.subtract).then_inc(hid_lo_made, 1)

            front(0)
            with pool.Fori(0, NF - 1) as t:
                low_hidden(t)
                front(t + 1)
            low_hidden(NF - 1)


_P = "L0_xattn_"
_WEIGHTS = ["n1_g", "n1_b", "q1", "k1", "v1", "o1_w", "o1_b", "n2_g", "n2_b", "q2", "k2", "v2", "o2_w", "o2_b",
            "n3_g", "n3_b", "ff_w1", "ff_b1", "ff_w2", "ff_b2"]


def kernel(**inputs):
    import numpy as np
    import concourse.bacc as bacc
    from concourse.bass_utils import run_bass_kernel_spmd

    arrays = {"x": np.ascontiguousarray(inputs["x"]),
              "ctxT": np.ascontiguousarray(np.transpose(inputs["ctx_768"], (0, 2, 1)))}
    for name in _WEIGHTS:
        arrays[name] = np.ascontiguousarray(inputs[_P + name])
    nc = bacc.Bacc("TRN2", target_bir_lowering=False, num_devices=1)
    args = [nc.dram_tensor(f"in_{name}", a.shape, mybir.dt.from_np(a.dtype), kind="ExternalInput").ap()
            for name, a in arrays.items()]
    out = nc.dram_tensor("out_0", (B, N, D), F32, kind="ExternalOutput").ap()
    build(nc, *args, out)
    r = run_bass_kernel_spmd(nc, [{f"in_{name}": a for name, a in arrays.items()}], core_ids=[0])
    return r.results[0]["out_0"]
```
